# Optimizing a Trainium2 kernel written in Bass

```python
import numpy as np
import jax
import jax.numpy as jnp

def _softmax(x, axis=-1):
    return jax.nn.softmax(x, axis=axis)

def _gelu(x):
    return jax.nn.gelu(x, approximate=True)

def _silu(x):
    return jax.nn.silu(x)

def _sigmoid(x):
    return jax.nn.sigmoid(x)

def _layernorm(x, axis=-1, eps=1e-05):
    m = jnp.mean(x, axis=axis, keepdims=True)
    v = jnp.var(x, axis=axis, keepdims=True)
    return (x - m) / jnp.sqrt(v + eps)

def _scatter_add(tgt, idx, src, axis=0):
    return tgt.at[idx].add(src)

def _segment_sum(src, seg, n):
    return jax.ops.segment_sum(src, seg, n)
kernel_name = 'mk_sandwich_d2_jaxref_r8_56bda2'

def setup_inputs(seed: int=0):
    np.random.seed(seed)
    _w = jnp.asarray

    def _L0_attn_setup():
        import jax, jax.numpy as jnp
        import numpy as np
        HEADS = 16
        DIM_HEAD = 64
        SCALE = DIM_HEAD ** (-0.5)
        key = jax.random.key(seed)
        k1, k2, k3 = jax.random.split(key, 3)
        dim, inner = (128, HEADS * DIM_HEAD)
        b, n = (2, 256)
        x = jax.random.normal(k1, (b, n, dim), dtype=jnp.float32)
        w_qkv = jax.random.normal(k2, (dim, 3 * inner), dtype=jnp.float32) * dim ** (-0.5)
        w_out = jax.random.normal(k3, (inner, dim), dtype=jnp.float32) * inner ** (-0.5)
        b_out = jnp.zeros((dim,), dtype=jnp.float32)
        return {'x': x, 'w_qkv': w_qkv, 'w_out': w_out, 'b_out': b_out}
    _L0_attn_in = _L0_attn_setup()

    def _L0_ffn_setup():
        import jax, jax.numpy as jnp
        import numpy as np
        D_MODEL = 128
        HIDDEN = 256
        N_EXPERTS = 8
        TOP_K = 2
        key = jax.random.key(seed)
        ks = jax.random.split(key, 9)
        s = 0.02
        x = jax.random.normal(ks[0], (4, 256, D_MODEL), dtype=jnp.float32)
        sw1 = jax.random.normal(ks[1], (D_MODEL, HIDDEN), dtype=jnp.float32) * s
        sw2 = jax.random.normal(ks[2], (D_MODEL, HIDDEN), dtype=jnp.float32) * s
        sw3 = jax.random.normal(ks[3], (HIDDEN, D_MODEL), dtype=jnp.float32) * s
        ew1 = jax.random.normal(ks[4], (N_EXPERTS, D_MODEL, HIDDEN), dtype=jnp.float32) * s
        ew2 = jax.random.normal(ks[5], (N_EXPERTS, D_MODEL, HIDDEN), dtype=jnp.float32) * s
        ew3 = jax.random.normal(ks[6], (N_EXPERTS, HIDDEN, D_MODEL), dtype=jnp.float32) * s
        rw = jax.random.normal(ks[7], (D_MODEL, N_EXPERTS), dtype=jnp.float32) * s
        rb = jax.random.normal(ks[8], (N_EXPERTS,), dtype=jnp.float32) * s
        return {'x': x, 'sw1': sw1, 'sw2': sw2, 'sw3': sw3, 'ew1': ew1, 'ew2': ew2, 'ew3': ew3, 'rw': rw, 'rb': rb}
    _L0_ffn_in = _L0_ffn_setup()

    def _L1_attn_setup():
        import jax, jax.numpy as jnp
        import numpy as np
        H = 16
        key = jax.random.key(seed)
        ks = jax.random.split(key, 7)
        B, L, D, d = (1, 128, 128, 128 // H)
        s = 0.02
        return {'x': jax.random.normal(ks[0], (B, L, D), jnp.float32), 'Wq': jax.random.normal(ks[1], (D, D), jnp.float32) * s, 'Wk': jax.random.normal(ks[2], (D, D), jnp.float32) * s, 'Wv': jax.random.normal(ks[3], (D, D), jnp.float32) * s, 'Wo': jax.random.normal(ks[4], (D, D), jnp.float32) * s, 'gw': jax.random.normal(ks[5], (1, d), jnp.float32) * s, 'sw': jax.random.normal(ks[6], (1, d), jnp.float32) * s}
    _L1_attn_in = _L1_attn_setup()

    def _L1_ffn_setup():
        import jax, jax.numpy as jnp
        import numpy as np
        DIM = 128
        E = 16
        TOPK = 2
        G = 4
        TOPK_G = 2
        INTER = 64
        N_SHARED = 2
        ROUTE_SCALE = 1.0

        def _gate(xf, gate_w, gate_b):
            scores = xf @ gate_w.T
            scores = jax.nn.softmax(scores.astype(jnp.float32), axis=-1)
            orig = scores
            scores = scores + gate_b
            T = xf.shape[0]
            sg = scores.reshape(T, G, E // G)
            group_scores = jax.lax.top_k(sg, 2)[0].sum(-1)
            _, gidx = jax.lax.top_k(group_scores, TOPK_G)
            keep = jax.nn.one_hot(gidx, G).sum(axis=1) > 0
            sg = jnp.where(keep[:, :, None], sg, -jnp.inf)
            scores = sg.reshape(T, E)
            _, idx = jax.lax.top_k(scores, TOPK)
            weights = jnp.take_along_axis(orig, idx, axis=1)
            weights = (weights * ROUTE_SCALE).astype(xf.dtype)
            return (weights, idx)
        key = jax.random.key(seed)
        ks = jax.random.split(key, 16)
        s = lambda fan_in: 1.0 / np.sqrt(fan_in)
        inp = {'x': jax.random.normal(ks[0], (4, 128, DIM), dtype=jnp.float32), 'gate_w': jax.random.normal(ks[1], (E, DIM), dtype=jnp.float32) * s(DIM), 'gate_b': jnp.zeros((E,), dtype=jnp.float32), 'We1': jax.random.normal(ks[2], (E, DIM, INTER), dtype=jnp.float32) * s(DIM), 'be1': jnp.zeros((E, INTER), dtype=jnp.float32), 'We2': jax.random.normal(ks[3], (E, INTER, DIM), dtype=jnp.float32) * s(INTER), 'be2': jnp.zeros((E, DIM), dtype=jnp.float32), 'We3': jax.random.normal(ks[4], (E, DIM, INTER), dtype=jnp.float32) * s(DIM), 'be3': jnp.zeros((E, INTER), dtype=jnp.float32), 'ws1': jax.random.normal(ks[5], (DIM, N_SHARED * INTER), dtype=jnp.float32) * s(DIM), 'bs1': jnp.zeros((N_SHARED * INTER,), dtype=jnp.float32), 'ws2': jax.random.normal(ks[6], (N_SHARED * INTER, DIM), dtype=jnp.float32) * s(N_SHARED * INTER), 'bs2': jnp.zeros((DIM,), dtype=jnp.float32), 'ws3': jax.random.normal(ks[7], (DIM, N_SHARED * INTER), dtype=jnp.float32) * s(DIM), 'bs3': jnp.zeros((N_SHARED * INTER,), dtype=jnp.float32)}
        return inp
    _L1_ffn_in = _L1_ffn_setup()
    _d = {'L0_attn_x': _L0_attn_in['x'], 'L0_attn_w_qkv': _L0_attn_in['w_qkv'], 'L0_attn_w_out': _L0_attn_in['w_out'], 'L0_attn_b_out': _L0_attn_in['b_out'], 'L0_ffn_sw1': _L0_ffn_in['sw1'], 'L0_ffn_sw2': _L0_ffn_in['sw2'], 'L0_ffn_sw3': _L0_ffn_in['sw3'], 'L0_ffn_ew1': _L0_ffn_in['ew1'], 'L0_ffn_ew2': _L0_ffn_in['ew2'], 'L0_ffn_ew3': _L0_ffn_in['ew3'], 'L0_ffn_rw': _L0_ffn_in['rw'], 'L0_ffn_rb': _L0_ffn_in['rb'], 'L1_attn_Wq': _L1_attn_in['Wq'], 'L1_attn_Wk': _L1_attn_in['Wk'], 'L1_attn_Wv': _L1_attn_in['Wv'], 'L1_attn_Wo': _L1_attn_in['Wo'], 'L1_attn_gw': _L1_attn_in['gw'], 'L1_attn_sw': _L1_attn_in['sw'], 'L1_ffn_gate_w': _L1_ffn_in['gate_w'], 'L1_ffn_gate_b': _L1_ffn_in['gate_b'], 'L1_ffn_We1': _L1_ffn_in['We1'], 'L1_ffn_be1': _L1_ffn_in['be1'], 'L1_ffn_We2': _L1_ffn_in['We2'], 'L1_ffn_be2': _L1_ffn_in['be2'], 'L1_ffn_We3': _L1_ffn_in['We3'], 'L1_ffn_be3': _L1_ffn_in['be3'], 'L1_ffn_ws1': _L1_ffn_in['ws1'], 'L1_ffn_bs1': _L1_ffn_in['bs1'], 'L1_ffn_ws2': _L1_ffn_in['ws2'], 'L1_ffn_bs2': _L1_ffn_in['bs2'], 'L1_ffn_ws3': _L1_ffn_in['ws3'], 'L1_ffn_bs3': _L1_ffn_in['bs3']}
    _x0 = _d['L0_attn_x']
    _d['L0_attn_x'] = jax.random.normal(jax.random.fold_in(jax.random.key(seed), 1), (16, 256, 128), dtype=_x0.dtype)
    del _x0
    return _d

def reference(L0_attn_x, L0_attn_w_qkv, L0_attn_w_out, L0_attn_b_out, L0_ffn_sw1, L0_ffn_sw2, L0_ffn_sw3, L0_ffn_ew1, L0_ffn_ew2, L0_ffn_ew3, L0_ffn_rw, L0_ffn_rb, L1_attn_Wq, L1_attn_Wk, L1_attn_Wv, L1_attn_Wo, L1_attn_gw, L1_attn_sw, L1_ffn_gate_w, L1_ffn_gate_b, L1_ffn_We1, L1_ffn_be1, L1_ffn_We2, L1_ffn_be2, L1_ffn_We3, L1_ffn_be3, L1_ffn_ws1, L1_ffn_bs1, L1_ffn_ws2, L1_ffn_bs2, L1_ffn_ws3, L1_ffn_bs3):

    def _L0_attn_ref(x, w_qkv, w_out, b_out):
        import jax, jax.numpy as jnp
        import numpy as np
        HEADS = 16
        DIM_HEAD = 64
        SCALE = DIM_HEAD ** (-0.5)
        b, n, _ = x.shape
        qkv = x @ w_qkv
        q, k, v = jnp.split(qkv, 3, axis=-1)

        def to_heads(t):
            return t.reshape(b, n, HEADS, DIM_HEAD).transpose(0, 2, 1, 3)
        q, k, v = (to_heads(q), to_heads(k), to_heads(v))
        dots = jnp.einsum('bhid,bhjd->bhij', q, k) * SCALE
        attn = jax.nn.softmax(dots, axis=-1)
        out = jnp.einsum('bhij,bhjd->bhid', attn, v)
        out = out.transpose(0, 2, 1, 3).reshape(b, n, HEADS * DIM_HEAD)
        return out @ w_out + b_out

    def _L0_ffn_ref(x, sw1, sw2, sw3, ew1, ew2, ew3, rw, rb):
        import jax, jax.numpy as jnp
        import numpy as np
        D_MODEL = 128
        HIDDEN = 256
        N_EXPERTS = 8
        TOP_K = 2
        shared = jnp.einsum('bth,hd->btd', jax.nn.silu(jnp.einsum('btd,dh->bth', x, sw1)) * jnp.einsum('btd,dh->bth', x, sw2), sw3)
        probs = jax.nn.softmax(jnp.einsum('btd,de->bte', x, rw) + rb, axis=-1)
        w, idx = jax.lax.top_k(probs, TOP_K)
        w = w / jnp.sum(w, axis=-1, keepdims=True)
        gates = jnp.sum(w[..., None] * jax.nn.one_hot(idx, N_EXPERTS, dtype=x.dtype), axis=-2)
        h = jax.nn.silu(jnp.einsum('btd,edh->beth', x, ew1)) * jnp.einsum('btd,edh->beth', x, ew2)
        eout = jnp.einsum('beth,ehd->betd', h, ew3)
        routed = jnp.einsum('betd,bte->btd', eout, gates)
        return shared + routed

    def _L1_attn_ref(x, Wq, Wk, Wv, Wo, gw, sw):
        import jax, jax.numpy as jnp
        import numpy as np
        H = 16
        B, L, D = x.shape
        d = D // H
        Q = (x @ Wq.T).reshape(B, L, H, d)
        K = (x @ Wk.T).reshape(B, L, H, d)
        V = (x @ Wv.T).reshape(B, L, H, d)
        KV = jnp.einsum('blhd,blhe->blhde', K, V)
        g = jax.nn.sigmoid(x.reshape(B, L, H, d) @ gw.T)
        g = jnp.clip(g, 1e-06, None)
        log_c = jnp.clip(jnp.cumsum(jnp.log(g), axis=1), -30.0, 30.0)
        Gc = (jnp.exp(log_c) + 1e-06)[..., None]
        R = jax.nn.silu(K @ sw.T)[..., None]
        S = jnp.cumsum(KV * R / Gc, axis=1) * Gc
        out = jnp.einsum('blhd,blhde->blhe', Q, S).reshape(B, L, D)
        return out @ Wo.T

    def _L1_ffn_ref(x, gate_w, gate_b, We1, be1, We2, be2, We3, be3, ws1, bs1, ws2, bs2, ws3, bs3):
        import jax, jax.numpy as jnp
        import numpy as np
        DIM = 128
        E = 16
        TOPK = 2
        G = 4
        TOPK_G = 2
        INTER = 64
        N_SHARED = 2
        ROUTE_SCALE = 1.0

        def _gate(xf, gate_w, gate_b):
            scores = xf @ gate_w.T
            scores = jax.nn.softmax(scores.astype(jnp.float32), axis=-1)
            orig = scores
            scores = scores + gate_b
            T = xf.shape[0]
            sg = scores.reshape(T, G, E // G)
            group_scores = jax.lax.top_k(sg, 2)[0].sum(-1)
            _, gidx = jax.lax.top_k(group_scores, TOPK_G)
            keep = jax.nn.one_hot(gidx, G).sum(axis=1) > 0
            sg = jnp.where(keep[:, :, None], sg, -jnp.inf)
            scores = sg.reshape(T, E)
            _, idx = jax.lax.top_k(scores, TOPK)
            weights = jnp.take_along_axis(orig, idx, axis=1)
            weights = (weights * ROUTE_SCALE).astype(xf.dtype)
            return (weights, idx)
        shape = x.shape
        xf = x.reshape(-1, DIM)
        weights, idx = _gate(xf, gate_w, gate_b)
        combine = (jax.nn.one_hot(idx, E, dtype=xf.dtype) * weights[..., None]).sum(1)
        h1 = jnp.einsum('td,edi->tei', xf, We1) + be1
        h3 = jnp.einsum('td,edi->tei', xf, We3) + be3
        h = jax.nn.silu(h1) * h3
        yo = jnp.einsum('tei,eid->ted', h, We2) + be2
        y = jnp.einsum('te,ted->td', combine, yo)
        z = jax.nn.silu(xf @ ws1 + bs1) * (xf @ ws3 + bs3) @ ws2 + bs2
        return (y + z).reshape(shape)
    x = L0_attn_x
    x = x + _layernorm(_L0_attn_ref(_layernorm(x, axis=-1), L0_attn_w_qkv, L0_attn_w_out, L0_attn_b_out), axis=-1)
    x = x + _layernorm(_L0_ffn_ref(_layernorm(x, axis=-1), L0_ffn_sw1, L0_ffn_sw2, L0_ffn_sw3, L0_ffn_ew1, L0_ffn_ew2, L0_ffn_ew3, L0_ffn_rw, L0_ffn_rb), axis=-1)
    x = x + _layernorm(_L1_attn_ref(_layernorm(x, axis=-1), L1_attn_Wq, L1_attn_Wk, L1_attn_Wv, L1_attn_Wo, L1_attn_gw, L1_attn_sw), axis=-1)
    x = x + _layernorm(_L1_ffn_ref(_layernorm(x, axis=-1), L1_ffn_gate_w, L1_ffn_gate_b, L1_ffn_We1, L1_ffn_be1, L1_ffn_We2, L1_ffn_be2, L1_ffn_We3, L1_ffn_be3, L1_ffn_ws1, L1_ffn_bs1, L1_ffn_ws2, L1_ffn_bs2, L1_ffn_ws3, L1_ffn_bs3), axis=-1)
    return x

_drawn_inputs = setup_inputs


def setup_inputs(seed=0):
    import zlib

    import numpy as np

    out = dict(_drawn_inputs(seed))
    spreads = {'L0_attn_b_out': (0.0, 0.1),
     'L1_ffn_gate_b': (0.0, 0.1),
     'L1_ffn_be1': (0.0, 0.57),
     'L1_ffn_be2': (0.0, 0.324),
     'L1_ffn_be3': (0.0, 0.567),
     'L1_ffn_bs1': (0.0, 0.1),
     'L1_ffn_bs2': (0.0, 0.1),
     'L1_ffn_bs3': (0.0, 0.1)}
    factors = {'L1_attn_gw': 30.356}
    for name, (base, spread) in spreads.items():
        noise = np.random.default_rng([zlib.crc32(name.encode()), seed]).standard_normal(out[name].shape)
        drawn = base * np.exp(spread * noise) if base else spread * noise
        out[name] = jnp.asarray(drawn.astype(out[name].dtype))
    for name, factor in factors.items():
        out[name] = (out[name] * factor).astype(out[name].dtype)
    return out
```

```python
import numpy as np
import concourse.bass as bass
from concourse import mybir
from contextlib import ExitStack

F32 = mybir.dt.float32
F32R = mybir.dt.float32r
I32 = mybir.dt.int32
U32 = mybir.dt.uint32
ALU = mybir.AluOpType
ACT = mybir.ActivationFunctionType
AX = mybir.AxisListType.X

P = 128
TILES = 4
W = TILES * P
EPS = 1e-5


def at(it, per, n):
    return it * per + n


def as32(ap):
    return ap.bitcast(F32)


def product(pe, out, w, x, start=True, stop=True):
    (wh, wl), (xh, xl) = w, x
    pe.matmul(out, wh, xh, start=start, stop=False)
    pe.matmul(out, wh, xl, start=False, stop=False)
    return pe.matmul(out, wl, xh, start=False, stop=stop)


def wait_apart(eng, sem, n, passed):
    eng.wait_ge(sem, n).then_inc(passed, 1)


class Chain:

    def __init__(self, eng, sem, passed, per):
        self.passed = passed
        self.eng, self.sem, self.per, self.it, self.n, self.base = eng, sem, per, 0, 0, 0

    def begin(self, it):
        self.base, self.it, self.n = self.n, it, 0

    def link(self, ins, apart=False):
        ins.then_inc(self.sem, 1)
        self.n += 1
        n = at(self.it, self.per, self.base + self.n)
        if apart:
            wait_apart(self.eng, self.sem, n, self.passed)
        else:
            self.eng.wait_ge(self.sem, n)

    def end(self):
        assert self.n == self.per, (self.n, self.per)


def row_stats(ch, tiles, stats, mean_var, var_eps, ready):
    dve = ch.eng
    for t in range(TILES):
        ins = dve.bn_stats(stats[:, t, :], tiles(t))
        if t < TILES - 1:
            ins.then_inc(ch.sem, 1)
            ch.n += 1
    ch.link(ins, apart=True)
    for t in range(TILES):
        ins = dve.bn_aggr(mean_var[:, t, :], stats[:, t, :])
        if t < TILES - 1:
            ins.then_inc(ch.sem, 1)
            ch.n += 1
    ch.link(ins)
    dve.tensor_scalar(var_eps[:, :], mean_var[:, :, 1], EPS, None, ALU.add).then_inc(ready, 1)


def inverse_std(pool, var_eps, minus_half, rstd, ready, n_ready, done):
    pool.wait_ge(ready, n_ready)
    pool.tensor_tensor(rstd[:, :], var_eps[:, :], minus_half[:, 0:TILES], ALU.pow).then_inc(done, 1)


def normalised(dve, tiles_out, tiles_in, mean_var, rstd):
    for t in range(TILES):
        ins = dve.tensor_scalar(tiles_out(t), tiles_in(t), mean_var[:, t, 0:1], rstd[:, t:t + 1],
                                ALU.subtract, ALU.mult)
    return ins


class Norms:

    def __init__(self, sb, sem, tag):
        self.stats = sb(f"{tag}_stats", [P, TILES, 6], F32)
        self.mean_var = sb(f"{tag}_mean_var", [P, TILES, 2], F32)
        self.var_eps = sb(f"{tag}_var_eps", [P, TILES], F32)
        self.rstd = sb(f"{tag}_rstd", [P, TILES], F32)
        self.branch = sb(f"{tag}_branch", [P, W], F32)
        self.y = sb(f"{tag}_y", [P, W], F32)
        self.var_ready = sem(f"{tag}_var_ready")
        self.rstd_ready = sem(f"{tag}_rstd_ready")
        self.y_ready = sem(f"{tag}_y_ready")
        self.y_transposed = sem(f"{tag}_y_transposed")
        self.yT_hi_ready = sem(f"{tag}_yT_hi_ready")
        self.yT_lo_ready = sem(f"{tag}_yT_lo_ready")

    def y_tile(self, t):
        return self.y[:, t * P:(t + 1) * P]


def add_branch(ch, nb, x_blk, delta_blk, it, n):
    dve = ch.eng
    row_stats(ch, lambda t: delta_blk[:, t * P:(t + 1) * P], nb.stats, nb.mean_var, nb.var_eps, nb.var_ready)

    def finish():
        dve.wait_ge(nb.rstd_ready, at(it, 4, 2 * n + 1))
        ch.link(normalised(dve, lambda t: nb.branch[:, t * P:(t + 1) * P],
                           lambda t: delta_blk[:, t * P:(t + 1) * P], nb.mean_var, nb.rstd))
        ch.link(dve.tensor_tensor(x_blk, x_blk, nb.branch[:, :], ALU.add), apart=True)
    return finish


def build(nc, a, out):
    x_in, w_qkv, w_out = a["L0_attn_x"], a["L0_attn_w_qkv"], a["L0_attn_w_out"]
    B, N, D = x_in.shape
    NT = B * N // P
    NBLK = NT // TILES
    INNER = w_out.shape[0]
    HEADS = 16
    DH = INNER // HEADS
    assert D == P and N == 2 * P and NBLK % 2 == 0
    E0, HID = a["L0_ffn_rw"].shape[1], a["L0_ffn_sw1"].shape[1]
    E1, INTER = a["L1_ffn_We1"].shape[0], a["L1_ffn_We1"].shape[2]
    ITS = NBLK // 2

    with ExitStack() as ctx:
        def sb(name, shape, dt):
            return ctx.enter_context(nc.sbuf_tensor(name, shape, dt))

        def sem(name):
            return ctx.enter_context(nc.semaphore(name))

        x = sb("x", [P, NBLK + 1, W], F32)
        delta = sb("delta", [P, NBLK + 1, W], F32)
        ident = sb("ident", [P, P], F32)
        minus_half = sb("minus_half", [P, TILES], F32)
        bank = [ctx.enter_context(nc.psum_tensor(f"bank{i}", [P, W], F32)) for i in range(8)]
        b_out = sb("b_out", [P, 1], F32)
        raw0 = [sb(f"raw0_{i}", [P, (E0 + 1) * HID], F32) for i in range(2)]
        raw0_down = sb("raw0_down", [P, (E0 + 1) * HID], F32)
        raw0_router = sb("raw0_router", [P, E0], F32)
        rb = sb("rb", [E0, 1], F32)
        raw1 = [sb(f"raw1_{i}", [P, (E1 + 2) * INTER], F32) for i in range(2)]
        raw1_down = sb("raw1_down", [P, (E1 + 2) * INTER], F32)
        raw1_gate = sb("raw1_gate", [E1, P], F32)
        be1 = sb("be1", [P, E1 // 2 + 1], F32)
        be3 = sb("be3", [P, E1 // 2 + 1], F32)
        be2 = sb("be2", [E1, P], F32)
        bs2 = sb("bs2", [P, 1], F32)
        gate_b = sb("gate_b", [P, TILES, E1], F32)
        raw_lin = sb("raw_lin", [P, 4, P], F32)
        gw = sb("gw", [P, 1], F32)
        sw = sb("sw", [P, 1], F32)
        x_loaded = sem("x_loaded")
        attn_w_loaded = sem("attn_w_loaded")
        later_w_loaded = sem("later_w_loaded")
        lw = dict(locals())
        attention(nc, a, lw)
        experts(nc, a, lw, 0)
        linear_attention(nc, a, lw)
        experts(nc, a, lw, 1)
        finish(nc, lw, out)


def attention(nc, a, g):
    x, delta, ident, bank = g["x"], g["delta"], g["ident"], g["bank"]
    minus_half, b_out = g["minus_half"], g["b_out"]
    B, N, NBLK, INNER, HEADS, DH, ITS = (g[k] for k in ("B", "N", "NBLK", "INNER", "HEADS", "DH", "ITS"))
    x_loaded, attn_w_loaded, later_w_loaded = g["x_loaded"], g["attn_w_loaded"], g["later_w_loaded"]
    E0, HID, E1, INTER = g["E0"], g["HID"], g["E1"], g["INTER"]
    PAIRS = HEADS // 2
    SCALE = float(DH) ** -0.5
    ctx = ExitStack()
    with ctx:
        def sb(name, shape, dt):
            return ctx.enter_context(nc.sbuf_tensor(name, shape, dt))

        def sem(name):
            return ctx.enter_context(nc.semaphore(name))

        A_w = [sb(f"A_{k}", [P, HEADS, P], F32R) for k in ("hi", "lo")]
        U_w = [sb(f"U_{k}", [P, HEADS, P], F32R) for k in ("hi", "lo")]

        with ExitStack() as pctx:
            def psb(name, shape, dt):
                return pctx.enter_context(nc.sbuf_tensor(name, shape, dt))

            def psem(name):
                return pctx.enter_context(nc.semaphore(name))

            wqkv_sb = psb("wqkv_sb", [P, 3 * INNER], F32)
            wout_sb = psb("wout_sb", [P, PAIRS, P], F32)
            wT = psb("wT", [P, 3, PAIRS, P], F32)
            ident_ready = psem("ident_ready")
            w_transposed = psem("w_transposed")
            w_copied = psem("w_copied")
            folded = psem("folded")
            fold_hi = psem("fold_hi")
            fold_lo = psem("fold_lo")
            later = []

            def head_of(j):
                return j // 8 * 8 + j // 4 % 2 + j % 4 * 2

            def bank_of(j, k):
                h = head_of(4 * j % HEADS)
                return (A_w if j < HEADS // 4 else U_w)[k][:, h:h + 7:2, :]
            with nc.Block() as block:
                @block.sync
                def _(sp):
                    sp.dma_start(wqkv_sb[:, :], a["L0_attn_w_qkv"]).then_inc(attn_w_loaded, 16)
                    sp.dma_start(wout_sb[:, :, :],
                                 a["L0_attn_w_out"].rearrange("(c p) n -> p c n", p=P)).then_inc(attn_w_loaded, 16)
                    xr = a["L0_attn_x"].rearrange("b n d -> (b n) d").rearrange("(m t p) d -> m p t d", p=P, t=TILES)
                    with nc.allow_non_contiguous_dma(reason="a bias column"):
                        sp.dma_start(b_out[:, :], a["L0_attn_b_out"].rearrange("(p o) -> p o", o=1))\
                            .then_inc(attn_w_loaded, 16)
                    for m in range(NBLK):
                        sp.dma_start(x[:, m, :].rearrange("p (t d) -> p t d", t=TILES), xr[m]).then_inc(x_loaded, 16)

                    def column(v):
                        return v.rearrange("(p o) -> p o", o=1)

                    def load(dst, src):
                        later.append(1)
                        sp.dma_start(dst, src).then_inc(later_w_loaded, 16)
                    with nc.allow_non_contiguous_dma(reason="bias columns"):
                        load(g["rb"][:, :], column(a["L0_ffn_rb"]))
                        load(g["bs2"][:, :], column(a["L1_ffn_bs2"]))
                        load(g["be1"][:, 0:1], column(a["L1_ffn_bs1"]))
                        load(g["be3"][:, 0:1], column(a["L1_ffn_bs3"]))
                        load(g["be1"][:, 1:], a["L1_ffn_be1"].rearrange("(s h) i -> (h i) s", h=2))
                        load(g["be3"][:, 1:], a["L1_ffn_be3"].rearrange("(s h) i -> (h i) s", h=2))
                        for h in range(16):
                            load(g["gw"][8 * h:8 * h + 8, :], a["L1_attn_gw"].rearrange("o d -> d o"))
                            load(g["sw"][8 * h:8 * h + 8, :], a["L1_attn_sw"].rearrange("o d -> d o"))
                    for i, n in enumerate(("1", "2")):
                        load(g["raw0"][i][:, 0:HID], a[f"L0_ffn_sw{n}"])
                        load(g["raw0"][i][:, HID:].rearrange("p (e h) -> p e h", e=E0),
                             a[f"L0_ffn_ew{n}"].rearrange("e d h -> d e h"))
                    load(g["raw0_down"][:, 0:HID].rearrange("p (j n) -> p j n", n=P),
                         a["L0_ffn_sw3"].rearrange("(j p) n -> p j n", p=P))
                    load(g["raw0_down"][:, HID:].rearrange("p (e n) -> p e n", n=P),
                         a["L0_ffn_ew3"].rearrange("e h n -> (e h) n").rearrange("(e p) n -> p e n", p=P))
                    load(g["raw0_router"][:, :], a["L0_ffn_rw"])
                    for i, n in enumerate(("1", "3")):
                        load(g["raw1"][i][:, 0:P], a[f"L1_ffn_ws{n}"])
                        load(g["raw1"][i][:, P:].rearrange("p (e h) -> p e h", e=E1),
                             a[f"L1_ffn_We{n}"].rearrange("e d h -> d e h"))
                    load(g["raw1_down"][:, 0:P], a["L1_ffn_ws2"])
                    load(g["raw1_down"][:, P:].rearrange("p (e n) -> p e n", n=P),
                         a["L1_ffn_We2"].rearrange("e h n -> (e h) n").rearrange("(e p) n -> p e n", p=P))
                    load(g["raw1_gate"][:, :], a["L1_ffn_gate_w"])
                    load(g["be2"][:, :], a["L1_ffn_be2"])
                    for t in range(TILES):
                        load(g["gate_b"][:, t, :],
                             a["L1_ffn_gate_b"].rearrange("(o e) -> o e", o=1).to_broadcast([P, E1]))
                    for i, n in enumerate(("Wq", "Wk", "Wv", "Wo")):
                        load(g["raw_lin"][:, i, :], a[f"L1_attn_{n}"])

                @block.gpsimd
                def _(pool):
                    pool.memset(ident[:, :], 0.0).then_inc(ident_ready, 1)
                    pool.wait_ge(ident_ready, 1)
                    pool.affine_select(out=ident[:, :], in_=ident[:, :], compare_op=ALU.not_equal, fill=1.0,
                                       base=0, pattern=[[-1, P]], channel_multiplier=1).then_inc(ident_ready, 1)
                    pool.memset(minus_half[:, :], -0.5)
                    pool.memset(x[:, NBLK, :], 0.0)
                    pool.memset(delta[:, NBLK, :], 0.0)

                @block.tensor
                def _(pe):
                    pe.wait_ge(ident_ready, 2)
                    pe.wait_ge(attn_w_loaded, 48)
                    for j in range(3 * PAIRS):
                        ins = pe.transpose(bank[j // 4][:, j % 4 * P:(j % 4 + 1) * P], wqkv_sb[:, j * P:(j + 1) * P],
                                           ident[:, :])
                        if j % 4 == 3:
                            ins.then_inc(w_transposed, 1)
                    pe.wait_ge(w_copied, 3 * PAIRS // 4)
                    for j in range(2 * HEADS):
                        h = head_of(j % HEADS)
                        r = slice(DH * (h % 2), DH * (h % 2) + DH)
                        lhs, rhs = (wT[r, 0, h // 2, :], wT[r, 1, h // 2, :]) if j < HEADS else \
                            (wT[r, 2, h // 2, :], wout_sb[r, h // 2, :])
                        ins = pe.matmul(bank[j // 4][:, j % 4 * P:(j % 4 + 1) * P], lhs, rhs, start=True, stop=True)
                        if j % 4 == 3:
                            ins.then_inc(folded, 1)

                @block.scalar
                def _(act):
                    for j in range(3 * PAIRS // 4):
                        act.wait_ge(w_transposed, j + 1)
                        act.activation(wT[:, :, :, :].rearrange("p a c d -> p (a c d)")[:, j * W:(j + 1) * W],
                                       bank[j][:, :], ACT.Copy).then_inc(w_copied, 1)
                    for j in range(HEADS // 2):
                        act.wait_ge(folded, j + 1)
                        act.activation(bank_of(j, 0), bank[j][:, :].rearrange("p (h d) -> p h d", d=P), ACT.Copy,
                                       scale=SCALE if j < HEADS // 4 else 1.0).then_inc(fold_hi, 1)

                @block.vector
                def _(dve):
                    for j in range(HEADS // 2):
                        dve.wait_ge(fold_hi, j + 1)
                        dve.scalar_tensor_tensor(out=bank_of(j, 1), in0=bank[j][:, :].rearrange("p (h d) -> p h d", d=P),
                                                 scalar=SCALE if j < HEADS // 4 else 1.0, in1=as32(bank_of(j, 0)), op0=ALU.mult, op1=ALU.subtract).then_inc(fold_lo, 1)
            g["n_later"] = len(later)

        nb = Norms(sb, sem, "l0a")
        y_tok = [[sb(f"y_tok_{k}{p}", [P, W], F32R) for k in ("hi", "lo")] for p in range(2)]
        yT = [[sb(f"yT_{k}{p}", [P, W], F32R) for k in ("hi", "lo")] for p in range(2)]
        z = [[sb(f"z_{k}{p}", [P, W], F32R) for k in ("hi", "lo")] for p in range(2)]
        probs = [sb(f"probs{p}", [P, W], F32) for p in range(2)]
        pT = [[sb(f"pT_{k}{p}", [P, W], F32R) for k in ("hi", "lo")] for p in range(2)]
        c = [[sb(f"c_{k}{p}", [P, W], F32R) for k in ("hi", "lo")] for p in range(2)]
        outT = sb("outT", [P, W], F32)
        neg_max = sb("neg_max", [P, 2, 2], F32)
        row_sum = sb("row_sum", [P, 2, 2], F32)
        inv_sum = sb("inv_sum", [P, 2, 2], F32)
        z_bank, s_bank, t_bank, c_bank, o_bank, m_bank = bank[0], bank[1:3], bank[3:5], bank[5], bank[6], bank[7]

        z_done, z_hi_done, z_lo_done = sem("z_done"), sem("z_hi_done"), sem("z_lo_done")
        s_done, max_done, exp_done = sem("s_done"), sem("max_done"), sem("exp_done")
        inv_done, probs_ready = sem("inv_done"), sem("probs_ready")
        t_done, t_hi_done, t_lo_done = sem("t_done"), sem("t_hi_done"), sem("t_lo_done")
        c_done, c_hi_done, c_lo_done = sem("c_done"), sem("c_hi_done"), sem("c_lo_done")
        o_done, outT_done, back_done, delta_done = sem("o_done"), sem("outT_done"), sem("back_done"), sem("delta_done")
        y_lo_done, y_hi_done = sem("y_lo_done"), sem("y_hi_done")
        dve_step, passed = sem("dve_step"), sem("passed")
        UN = 2 * HEADS
        U2, H2 = 2 * UN, 2 * HEADS
        LEAD = 3

        def xt(it, n):
            return lambda t: x[:, it * 2 + n, t * P:(t + 1) * P]

        block = ctx.enter_context(nc.Block())

        @block.tensor
        def _(pe):
            def transpose_y(it, n):
                pe.wait_ge(nb.y_ready, at(it, 2, n + 1))
                if n:
                    pe.wait_ge(delta_done, at(it, 2, n))
                for t in range(TILES):
                    ins = pe.transpose(m_bank[:, t * P:(t + 1) * P], nb.y_tile(t), ident[:, :])
                ins.then_inc(nb.y_transposed, 1)

            def project(it, h):
                if h % HEADS == 0:
                    pe.wait_ge(nb.yT_hi_ready, at(it, 2, h // HEADS + 1))
                    pe.wait_ge(nb.yT_lo_ready, at(it, 2, h // HEADS + 1))
                if h:
                    pe.wait_ge(z_hi_done, at(it, H2, h))
                    pe.wait_ge(z_lo_done, at(it, H2, h))
                y = [k[:, :] for k in yT[h // HEADS % 2]]
                product(pe, z_bank[:, :], [k[:, h % HEADS, :] for k in A_w], y).then_inc(z_done, 1)

            def scores(it, u):
                h, b = u // 2, u % 2
                if b == 0:
                    pe.wait_ge(z_hi_done, at(it, H2, h + 1))
                    pe.wait_ge(z_lo_done, at(it, H2, h + 1))
                if u >= 2:
                    pe.wait_ge(exp_done, at(it, U2, u - 1))
                keys = [k[:, b * N:(b + 1) * N] for k in yT[h // HEADS % 2]]
                for q in range(2):
                    ins = product(pe, s_bank[u % 2][:, q * N:(q + 1) * N],
                                  [k[:, b * N + q * P:b * N + (q + 1) * P] for k in z[h % 2]], keys)
                ins.then_inc(s_done, 1)

            def transpose_probs(it, u):
                pe.wait_ge(probs_ready, at(it, U2, u + 1))
                pe.wait_ge(t_hi_done, at(it, U2, u + 1))
                pe.wait_ge(t_lo_done, at(it, U2, u + 1))
                for q in range(2):
                    for k in range(2):
                        ins = pe.transpose(t_bank[u % 2][:, k * N + q * P:k * N + (q + 1) * P],
                                           probs[u % 2][:, q * N + k * P:q * N + (k + 1) * P], ident[:, :])
                ins.then_inc(t_done, 1)

            def mix(it, u):
                h, b = u // 2, u % 2
                pe.wait_ge(t_hi_done, at(it, U2, u + 3))
                pe.wait_ge(t_lo_done, at(it, U2, u + 3))
                if b == 0:
                    pe.wait_ge(c_hi_done, at(it, H2, h + 1))
                    pe.wait_ge(c_lo_done, at(it, H2, h + 1))
                for k in range(2):
                    s = slice((2 * b + k) * P, (2 * b + k + 1) * P)
                    ins = product(pe, c_bank[:, b * N:(b + 1) * N], [v[:, s] for v in y_tok[h // HEADS % 2]],
                                  [v[:, k * N:(k + 1) * N] for v in pT[u % 2]], start=(k == 0), stop=(k == 1))
                ins.then_inc(c_done, 1)

            def project_out(it, h):
                pe.wait_ge(c_hi_done, at(it, H2, h + 2))
                pe.wait_ge(c_lo_done, at(it, H2, h + 2))
                if h % HEADS == 0:
                    pe.wait_ge(outT_done, at(it, 2, h // HEADS + 1))
                product(pe, o_bank[:, :], [k[:, h % HEADS, :] for k in U_w], [k[:, :] for k in c[h % 2]],
                        start=(h % HEADS == 0), stop=(h % HEADS == HEADS - 1)).then_inc(o_done, 1)

            def slot(it, h):
                project(it, h + 3)
                if h >= -1:
                    mix(it, 2 * h + 2)
                if h >= 0:
                    project_out(it, h)
                if h >= -2:
                    transpose_probs(it, 2 * h + 4)
                scores(it, 2 * h + 6)
                if h >= -1:
                    mix(it, 2 * h + 3)
                scores(it, 2 * h + 7)
                if h >= -2:
                    transpose_probs(it, 2 * h + 5)

            transpose_y(0, 0)
            for h in range(-LEAD, 0):
                slot(0, h)
            with pe.Fori(0, ITS) as it:
                for p in range(2):
                    for j in range(HEADS):
                        slot(it, HEADS * p + j)
                        if j == 8:
                            transpose_y(it, p + 1)
                    pe.wait_ge(outT_done, at(it, 2, p + 2))
                    pe.wait_ge(nb.yT_lo_ready, at(it, 2, p + 2))
                    for t in range(TILES):
                        ins = pe.transpose(m_bank[:, t * P:(t + 1) * P], outT[:, t * P:(t + 1) * P], ident[:, :])
                    ins.then_inc(back_done, 1)

        @block.scalar
        def _(act):
            def yT_hi(it, n):
                act.wait_ge(nb.y_transposed, at(it, 2, n + 1))
                if n:
                    act.wait_ge(c_done, at(it, U2, UN * (n - 1) + 2))
                act.activation(yT[n % 2][0][:, :], m_bank[:, :], ACT.Copy).then_inc(nb.yT_hi_ready, 1)

            def z_hi(it, h):
                act.wait_ge(z_done, at(it, H2, h + 1))
                if h >= 2:
                    act.wait_ge(s_done, at(it, U2, 2 * h - 2))
                act.activation(z[h % 2][0][:, :], z_bank[:, :], ACT.Copy).then_inc(z_hi_done, 1)

            def exps(it, u):
                act.wait_ge(max_done, at(it, U2, u + 1))
                if u >= 2:
                    act.wait_ge(t_done, at(it, U2, u - 1))
                for q in range(2):
                    ins = act.activation(probs[u % 2][:, q * N:(q + 1) * N], s_bank[u % 2][:, q * N:(q + 1) * N],
                                         ACT.Exp, bias=neg_max[:, u % 2, q:q + 1],
                                         accum_out=row_sum[:, u % 2, q:q + 1])
                ins.then_inc(exp_done, 1)

            def pT_hi(it, u):
                act.wait_ge(t_done, at(it, U2, u + 1))
                act.wait_ge(c_done, at(it, U2, u + 1))
                act.activation(pT[u % 2][0][:, :], t_bank[u % 2][:, :], ACT.Copy).then_inc(t_hi_done, 1)

            def c_hi(it, h):
                act.wait_ge(c_done, at(it, U2, 2 * h + 4))
                act.wait_ge(o_done, at(it, H2, h + 1))
                act.activation(c[h % 2][0][:, :], c_bank[:, :], ACT.Copy).then_inc(c_hi_done, 1)

            act.sem_inc(t_hi_done, 2)
            act.sem_inc(c_hi_done, 1)
            act.sem_inc(outT_done, 1)
            def slot(it, h):
                z_hi(it, h + 3)
                if h >= -2:
                    exps(it, 2 * h + 5)
                    pT_hi(it, 2 * h + 4)
                if h >= -1:
                    c_hi(it, h + 1)
                exps(it, 2 * h + 6)
                if h >= -2:
                    pT_hi(it, 2 * h + 5)

            yT_hi(0, 0)
            for h in range(-LEAD, 0):
                slot(0, h)
            with act.Fori(0, ITS) as it:
                for p in range(2):
                    for j in range(HEADS):
                        slot(it, HEADS * p + j)
                        if j == 8:
                            yT_hi(it, p + 1)
                    act.wait_ge(o_done, at(it, H2, HEADS * (p + 1) + 2))
                    act.wait_ge(back_done, at(it, 2, p + 1))
                    act.activation(outT[:, :], o_bank[:, :], ACT.Identity, bias=b_out[:, 0:1]).then_inc(outT_done, 1)

        @block.gpsimd
        def _(pool):
            def norm_probs(it, u):
                wait_apart(pool, inv_done, at(it, U2, u + 1), passed)
                for q in range(2):
                    v = probs[u % 2][:, q * N:(q + 1) * N]
                    ins = pool.tensor_scalar(v, v, inv_sum[:, u % 2, q:q + 1], 1.0, ALU.mult, ALU.mult)
                ins.then_inc(probs_ready, 1)

            def y_lo(it, n):
                pool.wait_ge(y_hi_done, at(it, 2, n + 1))
                pool.tensor_tensor(y_tok[n % 2][1][:, :], nb.y[:, :], as32(y_tok[n % 2][0][:, :]), ALU.subtract)\
                    .then_inc(y_lo_done, 1)

            pool.sem_inc(back_done, 1)
            pool.sem_inc(c_done, 2)
            pool.sem_inc(o_done, 2)
            inverse_std(pool, nb.var_eps, minus_half, nb.rstd, nb.var_ready, 1, nb.rstd_ready)
            y_lo(0, 0)
            for u in range(2 * LEAD - 1):
                norm_probs(0, u)
            with pool.Fori(0, ITS) as it:
                for p in range(2):
                    for s in range(UN):
                        norm_probs(it, UN * p + s + 2 * LEAD - 1)
                        if s == 8:
                            inverse_std(pool, nb.var_eps, minus_half, nb.rstd, nb.var_ready, at(it, 2, p + 2),
                                        nb.rstd_ready)
                        if s == 13:
                            y_lo(it, p + 1)

        @block.vector
        def _(dve):
            ch = Chain(dve, dve_step, passed, 2 * 9)

            def stats_of(it, n):
                row_stats(ch, xt(it, n), nb.stats, nb.mean_var, nb.var_eps, nb.var_ready)

            def make_y(it, n):
                dve.wait_ge(nb.rstd_ready, at(it, 2, n + 1))
                if n:
                    dve.wait_ge(nb.y_transposed, at(it, 2, n))
                    dve.wait_ge(y_lo_done, at(it, 2, n))
                    dve.wait_ge(c_done, at(it, U2, UN * (n - 1) + 2))
                normalised(dve, nb.y_tile, xt(it, n), nb.mean_var, nb.rstd).then_inc(nb.y_ready, 1)
                dve.wait_ge(nb.y_ready, at(it, 2, n + 1))
                ch.link(dve.tensor_copy(y_tok[n % 2][0][:, :], nb.y[:, :]))
                dve.sem_inc(y_hi_done, 1)

            def yT_lo(it, n):
                dve.wait_ge(nb.yT_hi_ready, at(it, 2, n + 1))
                dve.tensor_tensor(yT[n % 2][1][:, :], m_bank[:, :], as32(yT[n % 2][0][:, :]), ALU.subtract)\
                    .then_inc(nb.yT_lo_ready, 1)

            def z_lo(it, h):
                dve.wait_ge(z_hi_done, at(it, H2, h + 1))
                dve.tensor_tensor(z[h % 2][1][:, :], z_bank[:, :], as32(z[h % 2][0][:, :]), ALU.subtract)\
                    .then_inc(z_lo_done, 1)

            def maxima(it, u):
                dve.wait_ge(s_done, at(it, U2, u + 1))
                dve.tensor_reduce(neg_max[:, u % 2, :], s_bank[u % 2][:, :].rearrange("p (q k) -> p q k", q=2),
                                  AX, ALU.max, negate=True).then_inc(max_done, 1)

            def inverse_sums(it, u):
                dve.wait_ge(exp_done, at(it, U2, u + 1))
                dve.reciprocal(inv_sum[:, u % 2, :], row_sum[:, u % 2, :]).then_inc(inv_done, 1)

            def pT_lo(it, u):
                dve.wait_ge(t_hi_done, at(it, U2, u + 3))
                dve.tensor_tensor(pT[u % 2][1][:, :], t_bank[u % 2][:, :], as32(pT[u % 2][0][:, :]), ALU.subtract)\
                    .then_inc(t_lo_done, 1)

            def c_lo(it, h):
                dve.wait_ge(c_hi_done, at(it, H2, h + 2))
                dve.tensor_tensor(c[h % 2][1][:, :], c_bank[:, :], as32(c[h % 2][0][:, :]), ALU.subtract)\
                    .then_inc(c_lo_done, 1)

            dve.sem_inc(t_lo_done, 2)
            dve.sem_inc(c_lo_done, 1)
            dve.sem_inc(delta_done, 1)
            dve.wait_ge(x_loaded, 16 * NBLK)
            stats_of(0, 0)
            make_y(0, 0)
            yT_lo(0, 0)
            def slot(it, h):
                z_lo(it, h + 3)
                if h >= -1:
                    pT_lo(it, 2 * h + 3)
                if h >= -2:
                    inverse_sums(it, 2 * h + 5)
                maxima(it, 2 * h + 6)
                if h >= -2:
                    pT_lo(it, 2 * h + 4)
                if h >= -1:
                    c_lo(it, h + 1)
                inverse_sums(it, 2 * h + 6)
                maxima(it, 2 * h + 7)

            for h in range(-LEAD, 0):
                slot(0, h)
            with dve.Fori(0, ITS) as it:
                ch.begin(it)
                for p in range(2):
                    for j in range(HEADS):
                        slot(it, HEADS * p + j)
                        if j == 3:
                            stats_of(it, p + 1)
                        if j == 6:
                            make_y(it, p + 1)
                        if j == 8:
                            yT_lo(it, p + 1)
                    wait_apart(dve, back_done, at(it, 2, p + 2), passed)
                    dve.tensor_copy(delta[:, it * 2 + p, :], m_bank[:, :]).then_inc(delta_done, 1)
                ch.end()


def split_weights(act, dve, pairs, hi_done, staged):
    for n, (raw, hi, lo) in enumerate(pairs):
        if act is not None:
            act.activation(hi, raw, ACT.Copy).then_inc(hi_done, 1)
        else:
            dve.wait_ge(hi_done, n + 1)
            dve.tensor_tensor(lo, raw, as32(hi), ALU.subtract).then_inc(staged, 1)


def experts(nc, a, g, layer):
    x, delta, ident, bank, minus_half = g["x"], g["delta"], g["ident"], g["bank"], g["minus_half"]
    NBLK, ITS = g["NBLK"], g["ITS"]
    E = g["E1"] if layer else g["E0"]
    HALVES = 1 if layer else g["HID"] // P
    STEPS = E // 2 + 1 if layer else (E + 1) * HALVES
    SHARED = HALVES
    MAPS = (STEPS - SHARED) // HALVES
    raw = g["raw1"] if layer else g["raw0"]
    raw_down = g["raw1_down"] if layer else g["raw0_down"]
    be1, be3, be2, bs2, rb, gate_b = (g[k] for k in ("be1", "be3", "be2", "bs2", "rb", "gate_b"))
    tag = f"l{layer}e"
    NLATER = 16 * g["n_later"]
    ctx = ExitStack()
    with ctx:
        def sb(name, shape, dt):
            return ctx.enter_context(nc.sbuf_tensor(f"{tag}_{name}", shape, dt))

        def sem(name):
            return ctx.enter_context(nc.semaphore(f"{tag}_{name}"))

        up_w = [[sb(f"up{i}_{k}", [P, STEPS, P], F32R) for k in ("hi", "lo")] for i in range(2)]
        down_w = [sb(f"down_{k}", [P, STEPS, P], F32R) for k in ("hi", "lo")]
        router_w = [sb(f"router_{k}", [P, E], F32R) for k in ("hi", "lo")]
        be2_w = [sb(f"be2_{k}", [E, P], F32R) for k in ("hi", "lo")]
        pick32 = sb("pick32", [E, MAPS, P], F32)
        pick = sb("pick", [E, MAPS, P], F32R)
        count = sb("count", [P, E], I32)
        place = sb("place", [P, TILES, E], F32)
        exp_base = sb("exp_base", [P, TILES, E], F32)
        gateT32 = sb("gateT32", [P, E], F32)
        if layer:
            before = sb("before", [P, TILES, 16], F32)
            after = sb("after", [P, TILES, 16], F32)

        with ExitStack() as pctx:
            made = pctx.enter_context(nc.semaphore(f"{tag}_made"))
            hi_done = pctx.enter_context(nc.semaphore(f"{tag}_hi_done"))
            lo_done = pctx.enter_context(nc.semaphore(f"{tag}_split"))
            gate_transposed = pctx.enter_context(nc.semaphore(f"{tag}_gate_transposed"))
            gate_copied = pctx.enter_context(nc.semaphore(f"{tag}_gate_copied"))
            small = pctx.enter_context(nc.semaphore(f"{tag}_small"))
            pairs = []
            flat = [(raw[0], up_w[0]), (raw[1], up_w[1]), (raw_down, down_w)]
            for r, w in flat:
                for s0 in range(0, STEPS, 9):
                    pairs.append((r[:, s0 * P:(s0 + 9) * P],) +
                                 tuple(k[:, s0:s0 + 9, :].rearrange("p s n -> p (s n)") for k in w))
            pairs.append((gateT32[:, :] if layer else g["raw0_router"][:, :],) + tuple(k[:, :] for k in router_w))
            if layer:
                pairs.append((be2[:, :],) + tuple(k[:, :] for k in be2_w))
            with nc.Block() as block:
                @block.gpsimd
                def _(pool):
                    pool.memset(pick32[:, :, :], 0.0).then_inc(made, 1)
                    pool.iota(count[:, :], pattern=[[1, E]], base=0, channel_multiplier=0).then_inc(made, 1)
                    pool.memset(exp_base[:, :, :], float(np.e))
                    pool.wait_ge(made, 2)
                    if layer:
                        v = pick32[:, :, :].rearrange("e m (h i) -> e m h i", h=2)
                        pattern = [[2, MAPS], [1, 2], [0, P // 2]]
                    else:
                        v, pattern = pick32[:, :, :], [[1, MAPS], [0, P]]
                    pool.affine_select(out=v, in_=v, compare_op=ALU.not_equal, fill=1.0, base=0,
                                       pattern=pattern, channel_multiplier=-1).then_inc(made, 1)
                    if layer:
                        pool.memset(before[:, :, :], 0.0).then_inc(made, 1)
                        pool.memset(after[:, :, :], 0.0).then_inc(made, 1)
                        pool.wait_ge(made, 5)
                        for t, sign in ((before, 1), (after, -1)):
                            v = t[:, :, :].rearrange("p t (i j) -> p t i j", j=4)
                            pool.affine_select(out=v, in_=v, compare_op=ALU.is_ge, fill=1.0, base=0,
                                               pattern=[[0, TILES], [-sign, 4], [sign, 4]],
                                               channel_multiplier=0).then_inc(made, 1)

                @block.tensor
                def _(pe):
                    pe.wait_ge(later_loaded(g), NLATER)
                    if layer:
                        pe.transpose(bank[0][:, 0:E], g["raw1_gate"][:, :], ident[0:E, 0:E]).then_inc(gate_transposed, 1)

                @block.scalar
                def _(act):
                    act.wait_ge(later_loaded(g), NLATER)
                    if layer:
                        act.wait_ge(gate_transposed, 1)
                        act.activation(gateT32[:, :], bank[0][:, 0:E], ACT.Copy).then_inc(gate_copied, 1)
                        act.wait_ge(gate_copied, 1)
                    split_weights(act, None, pairs, hi_done, lo_done)

                @block.vector
                def _(dve):
                    dve.wait_ge(later_loaded(g), NLATER)
                    dve.wait_ge(made, 3)
                    dve.tensor_copy(pick[:, :, :], pick32[:, :, :])
                    for t in range(TILES):
                        dve.tensor_copy(place[:, t, :], count[:, :])
                    split_weights(None, dve, pairs, hi_done, lo_done)

        nb = Norms(sb, sem, "n")
        yT = [[sb(f"yT_{k}{p}", [P, W], F32R) for k in ("hi", "lo")] for p in range(2)]
        silu = [sb(f"silu{p}", [P, W], F32) for p in range(2)]
        h = [sb(f"h{p}", [P, W], F32) for p in range(2)]
        h_w = [[sb(f"h_{k}{p}", [P, W], F32R) for k in ("hi", "lo")] for p in range(2)]
        outT = sb("outT", [P, W], F32)
        logitT = sb("logitT", [E, W], F32)
        gate = sb("gate", [P, TILES, E], F32)
        gT = [[sb(f"gT_{k}{p}", [E, W], F32R) for k in ("hi", "lo")] for p in range(2)]
        logit = sb("logit", [P, TILES, E], F32)
        probs = sb("probs", [P, TILES, E], F32)
        top = sb("top", [P, TILES, 8], F32)
        top_at = sb("top_at", [P, TILES, 8], U32)
        top_place = sb("top_place", [P, TILES, 2], F32)
        hit = [sb(f"hit{i}", [P, TILES, E], F32) for i in range(2)]
        one = [sb(f"one{i}", [P, TILES, 1], F32) for i in range(3)]
        quad = [sb(f"quad{i}", [P, TILES, 16], F32) for i in range(4)]
        four = [sb(f"four{i}", [P, TILES, 4], F32) for i in range(6)]
        a_bank, b_bank, gate_bank, o_bank, m_bank, r_bank = bank[0:2], bank[2:4], bank[4], bank[5], bank[6], bank[7]

        a_done, b_done, silu_done, prod_done = sem("a_done"), sem("b_done"), sem("silu_done"), sem("prod_done")
        map_done, h_done, h_hi_done, h_lo_done = sem("map_done"), sem("h_done"), sem("h_hi_done"), sem("h_lo_done")
        down_done, outT_done, back_done, delta_done = sem("down_done"), sem("outT_done"), sem("back_done"), sem("delta_done")
        lT_done, logitT_ready, logit_done = sem("lT_done"), sem("logitT_ready"), sem("logit_done")
        gate_ready, gT_done, gT_hi_ready, gT_lo_ready = sem("gate_ready"), sem("gT_done"), sem("gT_hi_ready"), sem("gT_lo_ready")
        diff_ready, exp_ready = sem("diff_ready"), sem("exp_ready")
        dve_step, passed = sem("dve_step"), sem("passed")
        S2, M2 = 2 * STEPS, 2 * MAPS
        T_ADD, T_ADD2, T_Y, T_YT, T_ROUTE, T_GATE, T_GT = (0, 1, 2, 3, 3, 4, 5) if layer else (1, 3, 5, 7, 8, 9, 12)

        block = ctx.enter_context(nc.Block())

        def gated(k):
            return k % STEPS >= SHARED

        def map_of(k):
            return k // STEPS * MAPS + (k % STEPS - SHARED) // HALVES

        @block.tensor
        def _(pe):
            def transpose_y(it, n):
                pe.wait_ge(nb.y_ready, at(it, 2, n + 1))
                if n:
                    pe.wait_ge(delta_done, at(it, 2, n))
                for t in range(TILES):
                    ins = pe.transpose(m_bank[:, t * P:(t + 1) * P], nb.y_tile(t), ident[:, :])
                ins.then_inc(nb.y_transposed, 1)

            def route(it, n):
                pe.wait_ge(nb.yT_hi_ready, at(it, 2, n + 1))
                pe.wait_ge(nb.yT_lo_ready, at(it, 2, n + 1))
                if n:
                    pe.wait_ge(gT_lo_ready, at(it, 2, n))
                product(pe, r_bank[0:E, :], [k[:, :] for k in router_w], [k[:, :] for k in yT[n % 2]])\
                    .then_inc(lT_done, 1)

            def route_back(it, n):
                wait_apart(pe, logitT_ready, at(it, 2, n + 1), passed)
                for t in range(TILES):
                    ins = pe.transpose(r_bank[:, t * E:(t + 1) * E], logitT[:, t * P:(t + 1) * P], ident[0:E, 0:E])
                ins.then_inc(logit_done, 1)

            def gates_across(it, n):
                pe.wait_ge(gate_ready, at(it, 2, n + 1))
                for t in range(TILES):
                    ins = pe.transpose(r_bank[0:E, t * P:(t + 1) * P], gate[:, t, :], ident[:, :])
                ins.then_inc(gT_done, 1)

            def up(it, k):
                s = k % STEPS
                if s == 0:
                    pe.wait_ge(nb.yT_hi_ready, at(it, 2, k // STEPS + 1))
                    pe.wait_ge(nb.yT_lo_ready, at(it, 2, k // STEPS + 1))
                y = [v[:, :] for v in yT[k // STEPS % 2]]
                if k >= 2:
                    pe.wait_ge(silu_done, at(it, S2, k - 1))
                product(pe, a_bank[k % 2][:, :], [v[:, s, :] for v in up_w[0]], y).then_inc(a_done, 1)
                if k >= 2:
                    pe.wait_ge(prod_done, at(it, S2, k - 1))
                product(pe, b_bank[k % 2][:, :], [v[:, s, :] for v in up_w[1]], y).then_inc(b_done, 1)

            def gate_map(it, k):
                if not gated(k) or (k % STEPS - SHARED) % HALVES:
                    return
                n = k // STEPS
                pe.wait_ge(gT_hi_ready, at(it, 2, n + 1))
                pe.wait_ge(gT_lo_ready, at(it, 2, n + 1))
                pe.wait_ge(h_done, at(it, S2, k))
                w = pick[:, (k % STEPS - SHARED) // HALVES, :]
                pe.matmul(gate_bank[:, :], w, gT[n % 2][0][:, :], start=True, stop=False)
                pe.matmul(gate_bank[:, :], w, gT[n % 2][1][:, :], start=False, stop=True).then_inc(map_done, 1)

            def down(it, k):
                s = k % STEPS
                pe.wait_ge(h_hi_done, at(it, S2, k + 1))
                pe.wait_ge(h_lo_done, at(it, S2, k + 1))
                if s == 0:
                    pe.wait_ge(outT_done, at(it, 2, k // STEPS + 1))
                product(pe, o_bank[:, :], [v[:, s, :] for v in down_w], [v[:, :] for v in h_w[k % 2]],
                        start=(s == 0), stop=(s == STEPS - 1)).then_inc(down_done, 1)
                if layer and s == 0:
                    product(pe, o_bank[:, :], [v[:, :] for v in be2_w], [v[:, :] for v in gT[k // STEPS % 2]],
                            start=False, stop=False)

            transpose_y(0, 0)
            route(0, 0)
            route_back(0, 0)
            up(0, 0)
            up(0, 1)
            gates_across(0, 0)
            pe.wait_ge(gT_hi_ready, 1)
            pe.wait_ge(gT_lo_ready, 1)
            with pe.Fori(0, ITS) as it:
                for p in range(2):
                    for s in range(STEPS):
                        k = STEPS * p + s
                        gate_map(it, k + 1)
                        if s == T_YT:
                            transpose_y(it, p + 1)
                        if s == T_ROUTE:
                            route(it, p + 1)
                        up(it, k + 2)
                        if s == T_GATE:
                            route_back(it, p + 1)
                        if s == T_GT:
                            gates_across(it, p + 1)
                        down(it, k)
                    pe.wait_ge(outT_done, at(it, 2, p + 2))
                    pe.wait_ge(nb.yT_lo_ready, at(it, 2, p + 2))
                    for t in range(TILES):
                        ins = pe.transpose(m_bank[:, t * P:(t + 1) * P], outT[:, t * P:(t + 1) * P], ident[:, :])
                    ins.then_inc(back_done, 1)

        @block.scalar
        def _(act):
            def yT_hi(it, n):
                act.wait_ge(nb.y_transposed, at(it, 2, n + 1))
                if n:
                    act.wait_ge(down_done, at(it, S2, STEPS * (n - 1) + 1))
                act.activation(yT[n % 2][0][:, :], m_bank[:, :], ACT.Copy).then_inc(nb.yT_hi_ready, 1)

            def logitT_out(it, n):
                act.wait_ge(lT_done, at(it, 2, n + 1))
                if n:
                    act.wait_ge(logit_done, at(it, 2, n))
                if layer:
                    ins = act.activation(logitT[:, :], r_bank[0:E, :], ACT.Copy)
                else:
                    ins = act.activation(logitT[:, :], r_bank[0:E, :], ACT.Identity, bias=rb[:, 0:1])
                ins.then_inc(logitT_ready, 1)

            def gT_hi(it, n):
                act.wait_ge(gT_done, at(it, 2, n + 1))
                if n:
                    act.wait_ge(down_done, at(it, S2, STEPS * (n - 1) + 1))
                act.activation(gT[n % 2][0][:, :], r_bank[0:E, :], ACT.Copy).then_inc(gT_hi_ready, 1)

            def silus(it, k):
                act.wait_ge(a_done, at(it, S2, k + 1))
                if k >= 2:
                    act.wait_ge(prod_done, at(it, S2, k - 1))
                kw = dict(bias=be1[:, k % STEPS:k % STEPS + 1]) if layer else {}
                act.activation(silu[k % 2][:, :], a_bank[k % 2][:, :], ACT.Silu, **kw).then_inc(silu_done, 1)

            def h_hi(it, k):
                act.wait_ge(h_done, at(it, S2, k + 1))
                act.wait_ge(down_done, at(it, S2, k))
                act.activation(h_w[k % 2][0][:, :], h[k % 2][:, :], ACT.Copy).then_inc(h_hi_done, 1)

            act.sem_inc(down_done, 1)
            act.sem_inc(outT_done, 1)
            yT_hi(0, 0)
            logitT_out(0, 0)
            silus(0, 0)
            silus(0, 1)
            act.wait_ge(h_done, 1)
            act.activation(h_w[0][0][:, :], h[0][:, :], ACT.Copy).then_inc(h_hi_done, 1)
            gT_hi(0, 0)
            with act.Fori(0, ITS) as it:
                for p in range(2):
                    for s in range(STEPS):
                        k = STEPS * p + s
                        h_hi(it, k + 1)
                        if s == T_YT:
                            yT_hi(it, p + 1)
                        if s == T_ROUTE:
                            logitT_out(it, p + 1)
                        silus(it, k + 2)
                        if s == T_GT:
                            gT_hi(it, p + 1)
                    act.wait_ge(down_done, at(it, S2, STEPS * (p + 1) + 1))
                    act.wait_ge(back_done, at(it, 2, p + 1))
                    if layer:
                        ins = act.activation(outT[:, :], o_bank[:, :], ACT.Identity, bias=bs2[:, 0:1])
                    else:
                        ins = act.activation(outT[:, :], o_bank[:, :], ACT.Copy)
                    ins.then_inc(outT_done, 1)

        @block.gpsimd
        def _(pool):
            def h_lo(it, k):
                pool.wait_ge(h_hi_done, at(it, S2, k + 1))
                pool.tensor_tensor(h_w[k % 2][1][:, :], h[k % 2][:, :], as32(h_w[k % 2][0][:, :]), ALU.subtract)\
                    .then_inc(h_lo_done, 1)

            def rstd(it, n, second):
                inverse_std(pool, nb.var_eps, minus_half, nb.rstd, nb.var_ready, at(it, 4, 2 * n + 1 + second),
                            nb.rstd_ready)

            def powers(it, n):
                pool.wait_ge(diff_ready, at(it, 2, n + 1))
                if layer:
                    ins = pool.tensor_tensor(probs[:, :, :], exp_base[:, :, :], logit[:, :, :], ALU.pow)
                else:
                    ins = pool.tensor_tensor(one[1][:, :, 0], exp_base[:, :, 0], one[0][:, :, 0], ALU.pow)
                ins.then_inc(exp_ready, 1)

            pool.sem_inc(back_done, 1)
            rstd(0, 0, 0)
            rstd(0, 0, 1)
            powers(0, 0)
            h_lo(0, 0)
            with pool.Fori(0, ITS) as it:
                for p in range(2):
                    for s in range(STEPS):
                        k = STEPS * p + s
                        h_lo(it, k + 1)
                        if s == T_ADD:
                            rstd(it, p + 1, 0)
                        if s == T_ADD2:
                            rstd(it, p + 1, 1)
                        if s == T_GATE:
                            powers(it, p + 1)

        @block.vector
        def _(dve):
            ch = Chain(dve, dve_step, passed, 98 if layer else 64)

            def blk(v, it, n):
                return v[:, it * 2 + n, :]

            def norm1(it, n):
                dve.wait_ge(later_loaded(g), NLATER)
                return add_branch(ch, nb, blk(x, it, n), blk(delta, it, n), it, n)

            def norm2(it, n):
                row_stats(ch, lambda t: x[:, it * 2 + n, t * P:(t + 1) * P], nb.stats, nb.mean_var, nb.var_eps,
                          nb.var_ready)

            def make_y(it, n):
                dve.wait_ge(nb.rstd_ready, at(it, 4, 2 * n + 2))
                if n:
                    dve.wait_ge(nb.y_transposed, at(it, 2, n))
                normalised(dve, nb.y_tile, lambda t: x[:, it * 2 + n, t * P:(t + 1) * P], nb.mean_var, nb.rstd)\
                    .then_inc(nb.y_ready, 1)

            def yT_lo(it, n):
                dve.wait_ge(nb.yT_hi_ready, at(it, 2, n + 1))
                dve.tensor_tensor(yT[n % 2][1][:, :], m_bank[:, :], as32(yT[n % 2][0][:, :]), ALU.subtract)\
                    .then_inc(nb.yT_lo_ready, 1)

            def gT_lo(it, n):
                dve.wait_ge(gT_hi_ready, at(it, 2, n + 1))
                dve.tensor_tensor(gT[n % 2][1][:, :], r_bank[0:E, :], as32(gT[n % 2][0][:, :]), ALU.subtract)\
                    .then_inc(gT_lo_ready, 1)

            def top_two(values):
                for t in range(TILES):
                    ch.link(dve.max(top[:, t, :], values[:, t, :]), apart=True)
                    ins = dve.max_index(top_at[:, t, :], top[:, t, :], values[:, t, :])
                ch.link(ins)
                ch.link(dve.tensor_copy(top_place[:, :, :], top_at[:, :, 0:2]))
                for i in range(2):
                    ch.link(dve.tensor_tensor(hit[i][:, :, :], place[:, :, :],
                                              top_place[:, :, i:i + 1].to_broadcast([P, TILES, E]), ALU.is_equal))

            def routing0(it, n):
                dve.wait_ge(logit_done, at(it, 2, n + 1))
                if n:
                    dve.wait_ge(gT_done, at(it, 2, n))
                ch.link(dve.tensor_copy(logit[:, :, :].rearrange("p t e -> p (t e)"), r_bank[:, 0:TILES * E]), apart=True)
                top_two(logit)
                dve.tensor_tensor(one[0][:, :, :], top[:, :, 1:2], top[:, :, 0:1], ALU.subtract)\
                    .then_inc(diff_ready, 1)
                dve.wait_ge(exp_ready, at(it, 2, n + 1))
                ch.link(dve.tensor_scalar(one[2][:, :, :], one[1][:, :, :], 1.0, None, ALU.add))
                ch.link(dve.reciprocal(one[2][:, :, :], one[2][:, :, :]))
                ch.link(dve.tensor_tensor(hit[1][:, :, :], hit[1][:, :, :],
                                          one[1][:, :, :].to_broadcast([P, TILES, E]), ALU.mult))
                ch.link(dve.tensor_tensor(hit[0][:, :, :], hit[0][:, :, :], hit[1][:, :, :], ALU.add))
                dve.tensor_tensor(gate[:, :, :], hit[0][:, :, :], one[2][:, :, :].to_broadcast([P, TILES, E]),
                                  ALU.mult).then_inc(gate_ready, 1)

            def routing1(it, n):
                dve.wait_ge(logit_done, at(it, 2, n + 1))
                if n:
                    dve.wait_ge(gT_done, at(it, 2, n))
                r = r_bank[:, 0:TILES * E].rearrange("p (t e) -> p t e", t=TILES)
                ch.link(dve.tensor_reduce(one[0][:, :, 0], r, AX, ALU.max))
                dve.tensor_tensor(logit[:, :, :], r, one[0][:, :, :].to_broadcast([P, TILES, E]), ALU.subtract)\
                    .then_inc(diff_ready, 1)
                dve.wait_ge(exp_ready, at(it, 2, n + 1))
                ch.link(dve.tensor_reduce(one[1][:, :, 0], probs[:, :, :], AX, ALU.add))
                ch.link(dve.reciprocal(one[2][:, :, :], one[1][:, :, :]))
                ch.link(dve.tensor_tensor(probs[:, :, :], probs[:, :, :], one[2][:, :, :].to_broadcast([P, TILES, E]),
                                          ALU.mult))
                ch.link(dve.tensor_tensor(logit[:, :, :], probs[:, :, :], gate_b[:, :, :], ALU.add))
                v = [logit[:, :, i::4] for i in range(4)]
                ch.link(dve.tensor_tensor(four[0][:, :, :], v[0], v[1], ALU.max))
                ch.link(dve.tensor_tensor(four[1][:, :, :], v[2], v[3], ALU.max))
                ch.link(dve.tensor_tensor(four[2][:, :, :], v[0], v[1], ALU.add))
                ch.link(dve.tensor_tensor(four[3][:, :, :], v[2], v[3], ALU.add))
                ch.link(dve.tensor_tensor(four[0][:, :, :], four[0][:, :, :], four[1][:, :, :], ALU.add))
                ch.link(dve.tensor_tensor(four[2][:, :, :], four[2][:, :, :], four[3][:, :, :], ALU.max))
                ch.link(dve.tensor_tensor(four[4][:, :, :], four[0][:, :, :], four[2][:, :, :], ALU.max))
                q = [v[:, :, :].rearrange("p t (i j) -> p t i j", j=4) for v in quad]
                own = four[4][:, :, :].rearrange("p t (i o) -> p t i o", o=1).to_broadcast([P, TILES, 4, 4])
                for i in range(4):
                    ins = dve.tensor_copy(quad[0][:, :, 4 * i:4 * i + 4], four[4][:, :, :])
                ch.link(ins)
                ch.link(dve.tensor_tensor(q[1], q[0], own, ALU.is_ge))
                ch.link(dve.tensor_tensor(q[2], q[0], own, ALU.is_gt))
                ch.link(dve.tensor_tensor(quad[1][:, :, :], quad[1][:, :, :], before[:, :, :], ALU.mult))
                ch.link(dve.tensor_tensor(quad[2][:, :, :], quad[2][:, :, :], after[:, :, :], ALU.mult))
                ch.link(dve.tensor_tensor(quad[3][:, :, :], quad[1][:, :, :], quad[2][:, :, :], ALU.add))
                ch.link(dve.tensor_reduce(four[5][:, :, :], q[3], AX, ALU.add))
                ch.link(dve.tensor_scalar(four[5][:, :, :], four[5][:, :, :], 1.5, -1e30, ALU.is_gt, ALU.mult))
                out4 = four[5][:, :, :].rearrange("p t (i o) -> p t i o", o=1).to_broadcast([P, TILES, 4, 4])
                l4 = logit[:, :, :].rearrange("p t (i j) -> p t i j", j=4)
                ch.link(dve.tensor_tensor(l4, l4, out4, ALU.add), apart=True)
                top_two(logit)
                ch.link(dve.tensor_tensor(hit[0][:, :, :], hit[0][:, :, :], hit[1][:, :, :], ALU.add))
                dve.tensor_tensor(gate[:, :, :], hit[0][:, :, :], probs[:, :, :], ALU.mult).then_inc(gate_ready, 1)

            routing = routing1 if layer else routing0

            def prod(it, k):
                dve.wait_ge(silu_done, at(it, S2, k + 1))
                dve.wait_ge(b_done, at(it, S2, k + 1))
                if k >= 2:
                    dve.wait_ge(h_lo_done, at(it, S2, k - 1))
                if layer:
                    ins = dve.scalar_tensor_tensor(out=h[k % 2][:, :], in0=b_bank[k % 2][:, :],
                                                   scalar=be3[:, k % STEPS:k % STEPS + 1], in1=silu[k % 2][:, :],
                                                   op0=ALU.add, op1=ALU.mult)
                else:
                    ins = dve.tensor_tensor(h[k % 2][:, :], b_bank[k % 2][:, :], silu[k % 2][:, :], ALU.mult)
                ins.then_inc(prod_done, 1)

            def weigh(it, k):
                dve.wait_ge(prod_done, at(it, S2, k + 1))
                if gated(k):
                    dve.wait_ge(map_done, at(it, M2, map_of(k) + 1))
                    dve.tensor_tensor(h[k % 2][:, :], gate_bank[:, :], h[k % 2][:, :], ALU.mult).then_inc(h_done, 1)
                else:
                    dve.sem_inc(h_done, 1)

            dve.sem_inc(delta_done, 1)
            norm1(0, 0)()
            norm2(0, 0)
            make_y(0, 0)
            yT_lo(0, 0)
            routing(0, 0)
            prod(0, 0)
            weigh(0, 0)
            prod(0, 1)
            gT_lo(0, 0)
            with dve.Fori(0, ITS) as it:
                ch.begin(it)
                for p in range(2):
                    for s in range(STEPS):
                        k = STEPS * p + s
                        weigh(it, k + 1)
                        if s == T_ADD:
                            rest = norm1(it, p + 1)
                        if s == T_ADD2:
                            rest()
                            norm2(it, p + 1)
                        if s == T_Y:
                            make_y(it, p + 1)
                        if s == T_YT:
                            yT_lo(it, p + 1)
                        prod(it, k + 2)
                        if s == T_GATE:
                            routing(it, p + 1)
                        if s == T_GT:
                            gT_lo(it, p + 1)
                    wait_apart(dve, back_done, at(it, 2, p + 2), passed)
                    ch.link(dve.tensor_copy(delta[:, it * 2 + p, :], m_bank[:, :]))
                    dve.sem_inc(delta_done, 1)
                ch.end()


def later_loaded(g):
    return g["later_w_loaded"]


def linear_attention(nc, a, g):
    x, delta, ident, bank, minus_half, raw = g["x"], g["delta"], g["ident"], g["bank"], g["minus_half"], g["raw_lin"]
    NBLK, ITS = g["NBLK"], g["ITS"]
    H, d = 16, 8
    KVN = H * d * d
    QKV = 3 * P
    PROJ = QKV + 2 * H
    NLATER = 16 * g["n_later"]
    ctx = ExitStack()
    with ctx:
        def sb(name, shape, dt):
            return ctx.enter_context(nc.sbuf_tensor(f"lin_{name}", shape, dt))

        def sem(name):
            return ctx.enter_context(nc.semaphore(f"lin_{name}"))

        proj32 = sb("proj32", [P, PROJ], F32)
        proj_w = [sb(f"proj_{k}", [P, PROJ], F32R) for k in ("hi", "lo")]
        woT = sb("woT", [P, P], F32)
        tri = sb("tri", [P, P], F32)
        ones = sb("ones", [P, P], F32)
        own = sb("own", [P, H], F32)
        sw_own = sb("sw_own", [P, H], F32)
        made, copied, folded, gated, hi_done, split = (sem(n) for n in
                                                       ("made", "copied", "folded", "gated", "hi_done", "split"))
        with nc.Block() as block:
            @block.gpsimd
            def _(pool):
                pool.memset(tri[:, :], 1.0).then_inc(made, 1)
                pool.memset(own[:, :], 1.0).then_inc(made, 1)
                pool.memset(ones[:, :], 1.0)
                pool.wait_ge(made, 2)
                pool.affine_select(out=tri[:, :], in_=tri[:, :], compare_op=ALU.is_ge, fill=0.0, base=0,
                                   pattern=[[1, P]], channel_multiplier=-1)
                pool.affine_select(out=own[:, :], in_=own[:, :], compare_op=ALU.is_ge, fill=0.0, base=0,
                                   pattern=[[-d, H]], channel_multiplier=1).then_inc(made, 1)
                pool.wait_ge(made, 3)
                pool.affine_select(out=own[:, :], in_=own[:, :], compare_op=ALU.is_ge, fill=0.0, base=d - 1,
                                   pattern=[[d, H]], channel_multiplier=-1).then_inc(made, 1)

            @block.tensor
            def _(pe):
                for i in range(4):
                    ins = pe.transpose(bank[0][:, i * P:(i + 1) * P], raw[:, i, :], ident[:, :])
                ins.then_inc(folded, 1)
                pe.wait_ge(gated, 2)
                pe.matmul(bank[1][:, 0:H], raw[:, 1, :], sw_own[:, :], start=True, stop=True).then_inc(folded, 1)

            @block.vector
            def _(dve):
                dve.wait_ge(made, 4)
                dve.tensor_scalar(sw_own[:, :], own[:, :], g["sw"][:, 0:1], None, ALU.mult).then_inc(gated, 1)
                dve.tensor_scalar(proj32[:, QKV + H:], own[:, :], g["gw"][:, 0:1], None, ALU.mult).then_inc(gated, 1)
                dve.wait_ge(hi_done, 1)
                dve.tensor_tensor(proj_w[1][:, :], proj32[:, :], as32(proj_w[0][:, :]), ALU.subtract)

            @block.scalar
            def _(act):
                act.wait_ge(folded, 1)
                act.activation(proj32[:, 0:QKV], bank[0][:, 0:QKV], ACT.Copy).then_inc(copied, 1)
                act.activation(woT[:, :], bank[0][:, QKV:], ACT.Copy)
                act.wait_ge(folded, 2)
                act.activation(proj32[:, QKV:QKV + H], bank[1][:, 0:H], ACT.Copy).then_inc(copied, 1)
                act.wait_ge(copied, 2)
                act.wait_ge(gated, 2)
                act.activation(proj_w[0][:, :], proj32[:, :], ACT.Copy).then_inc(hi_done, 1)

        nb = Norms(sb, sem, "n")
        yT = [sb(f"yT_{k}", [P, W], F32R) for k in ("hi", "lo")]
        qkvr = [sb(f"qkvr{p}", [P, TILES, QKV + H], F32) for p in range(2)]
        er = sb("er", [P, TILES, 2 * H], F32)
        g1 = sb("g1", [P, TILES, H], F32)
        lg = sb("lg", [P, TILES, H], F32)
        lc = sb("lc", [P, TILES, H], F32)
        gexp = sb("gexp", [P, TILES, H], F32)
        gc = [sb(f"gc{p}", [P, TILES, H], F32) for p in range(2)]
        den = sb("den", [P, TILES, H], F32)
        kw = [sb(f"kw{p}", [P, TILES, P], F32) for p in range(2)]
        qg = [sb(f"qg{p}", [P, TILES, P], F32) for p in range(2)]
        kv = sb("kv", [P, TILES, KVN], F32)
        qs = [sb(f"qs{p}", [P, KVN], F32) for p in range(2)]
        o = sb("o", [P, TILES, P], F32)
        oT = sb("oT", [P, W], F32)
        p_bank, s_bank, m_bank, oT_bank, sum_bank = bank[0], [bank[1:3], bank[3:5]], bank[5], bank[6], bank[7]

        proj_done, proj_read, g1_ready, ln_done = sem("proj_done"), sem("proj_read"), sem("g1_ready"), sem("ln_done")
        sum_done, lc_ready, gexp_done, gc_ready = sem("sum_done"), sem("lc_ready"), sem("gexp_done"), sem("gc_ready")
        kw_ready, qg_ready, kv_ready, s_done = sem("kw_ready"), sem("qg_ready"), sem("kv_ready"), sem("s_done")
        qs_done, o_ready, oT_done, oT_ready = sem("qs_done"), sem("o_ready"), sem("oT_done"), sem("oT_ready")
        out_done, delta_done, dve_step, passed = sem("out_done"), sem("delta_done"), sem("dve_step"), sem("passed")
        T2 = 2 * TILES

        def heads(v):
            return v.rearrange("p t (h k) -> p t h k", k=d)

        def over(v):
            return v[:, :, :].rearrange("p t (h o) -> p t h o", o=1).to_broadcast([P, TILES, H, d])

        block = ctx.enter_context(nc.Block())

        @block.tensor
        def _(pe):
            def transpose_y(it, n):
                pe.wait_ge(nb.y_ready, at(it, 2, n + 1))
                if n:
                    pe.wait_ge(nb.yT_lo_ready, at(it, 2, n))
                for t in range(TILES):
                    ins = pe.transpose(m_bank[:, t * P:(t + 1) * P], nb.y_tile(t), ident[:, :])
                ins.then_inc(nb.y_transposed, 1)

            def project(it, j):
                n, t = j // TILES, j % TILES
                if t == 0:
                    pe.wait_ge(nb.yT_hi_ready, at(it, 2, n + 1))
                    pe.wait_ge(nb.yT_lo_ready, at(it, 2, n + 1))
                    if n:
                        pe.wait_ge(delta_done, at(it, 2, n))
                if j:
                    pe.wait_ge(proj_read, at(it, T2, j))
                product(pe, p_bank[:, 0:PROJ], [v[:, t * P:(t + 1) * P] for v in yT], [v[:, :] for v in proj_w])\
                    .then_inc(proj_done, 1)

            def cumulate(it, n):
                pe.wait_ge(ln_done, at(it, 2, n + 1))
                if n:
                    pe.wait_ge(lc_ready, at(it, 2, n))
                v = lg[:, :, :].rearrange("p t h -> p (t h)")
                first = lg[:, :, :].rearrange("p (b j) h -> p b j h", j=2)[:, :, 0, :]
                second = sum_bank[:, 0:TILES * H].rearrange("p (b j h) -> p b j h", j=2, h=H)[:, :, 1, :]
                pe.matmul(sum_bank[:, 0:TILES * H], tri[:, :], v, start=True, stop=False)
                pe.matmul(second, ones[:, :], first, start=False, stop=True).then_inc(sum_done, 1)

            def states(it, j):
                t = j % TILES
                pe.wait_ge(kv_ready, at(it, T2, j + 1))
                pe.wait_ge(qs_done, at(it, T2, j + 1))
                for i in range(2):
                    s = slice(i * W, (i + 1) * W)
                    if t % 2:
                        pe.matmul(s_bank[j % 2][i][:, :], ones[:, :], kv[:, t - 1, s], start=True, stop=False)
                    ins = pe.matmul(s_bank[j % 2][i][:, :], tri[:, :], kv[:, t, s], start=(t % 2 == 0), stop=True)
                ins.then_inc(s_done, 1)

            def project_out(it, n):
                pe.wait_ge(o_ready, at(it, T2, TILES * n + TILES + 1))
                for t in range(TILES):
                    ins = pe.transpose(oT_bank[:, t * P:(t + 1) * P], o[:, t, :], ident[:, :])
                ins.then_inc(oT_done, 1)
                pe.wait_ge(oT_ready, at(it, 2, n + 1))
                pe.wait_ge(proj_read, at(it, T2, TILES * (n + 2)))
                for t in range(TILES):
                    ins = pe.matmul(p_bank[:, t * P:(t + 1) * P], oT[:, t * P:(t + 1) * P], woT[:, :],
                                    start=True, stop=True)
                ins.then_inc(out_done, 1)

            transpose_y(0, 0)
            for j in range(TILES):
                project(0, j)
            cumulate(0, 0)
            with pe.Fori(0, ITS) as it:
                for p in range(2):
                    for t in range(TILES):
                        states(it, TILES * p + t)
                        if t == 1:
                            transpose_y(it, p + 1)
                        if t == 2:
                            for j in range(TILES):
                                project(it, TILES * (p + 1) + j)
                    cumulate(it, p + 1)
                    project_out(it, p)

        @block.scalar
        def _(act):
            def yT_hi(it, n):
                act.wait_ge(nb.y_transposed, at(it, 2, n + 1))
                if n:
                    act.wait_ge(proj_done, at(it, T2, TILES * n))
                act.activation(yT[0][:, :], m_bank[:, :], ACT.Copy).then_inc(nb.yT_hi_ready, 1)

            def read_projection(it, j):
                n, t = j // TILES, j % TILES
                act.wait_ge(proj_done, at(it, T2, j + 1))
                if n:
                    act.wait_ge(o_ready, at(it, T2, TILES * (n - 1) + 1))
                    act.wait_ge(kw_ready, at(it, 2, n))
                act.activation(qkvr[n % 2][:, t, :], p_bank[:, 0:QKV + H], ACT.Copy)
                act.activation(er[:, t, :], p_bank[:, QKV:PROJ], ACT.Exp, scale=-1.0).then_inc(proj_read, 1)

            def log_gate(it, n):
                act.wait_ge(g1_ready, at(it, 2, n + 1))
                if n:
                    act.wait_ge(sum_done, at(it, 2, n))
                act.activation(lg[:, :, :], g1[:, :, :], ACT.Ln).then_inc(ln_done, 1)

            def exp_gate(it, n):
                act.wait_ge(lc_ready, at(it, 2, n + 1))
                act.activation(gexp[:, :, :], lc[:, :, :], ACT.Exp, scale=-1.0).then_inc(gexp_done, 1)

            act.preload_act_table_set("natural_log_exp_and_others")
            act.sem_inc(oT_done, 1)
            act.sem_inc(delta_done, 1)
            yT_hi(0, 0)
            for j in range(TILES):
                read_projection(0, j)
            log_gate(0, 0)
            exp_gate(0, 0)
            with act.Fori(0, ITS) as it:
                for p in range(2):
                    yT_hi(it, p + 1)
                    for j in range(TILES):
                        read_projection(it, TILES * (p + 1) + j)
                    log_gate(it, p + 1)
                    exp_gate(it, p + 1)
                    act.wait_ge(oT_done, at(it, 2, p + 2))
                    act.wait_ge(out_done, at(it, 2, p + 1))
                    act.activation(oT[:, :], oT_bank[:, :], ACT.Copy).then_inc(oT_ready, 1)
                    act.wait_ge(out_done, at(it, 2, p + 2))
                    act.activation(delta[:, it * 2 + p, :], p_bank[:, :], ACT.Copy).then_inc(delta_done, 1)

        @block.gpsimd
        def _(pool):
            def rstd(it, n, second):
                inverse_std(pool, nb.var_eps, minus_half, nb.rstd, nb.var_ready, at(it, 4, 2 * n + 1 + second),
                            nb.rstd_ready)

            def outer(it, j):
                n, t = j // TILES, j % TILES
                pool.wait_ge(kw_ready, at(it, 2, n + 1))
                pool.wait_ge(s_done, at(it, T2, j + (1 if t % 2 else 2)))
                out = kv[:, t, :].rearrange("p (h k e) -> p h k e", k=d, e=d)
                k = kw[n % 2][:, t, :].rearrange("p (h k o) -> p h k o", k=d, o=1).to_broadcast([P, H, d, d])
                v = qkvr[n % 2][:, t, 2 * P:QKV].rearrange("p (h o e) -> p h o e", e=d, o=1)\
                    .to_broadcast([P, H, d, d])
                pool.tensor_tensor(out, k, v, ALU.mult).then_inc(kv_ready, 1)

            def weigh_q(it, n):
                pool.wait_ge(gc_ready, at(it, 2, n + 1))
                pool.wait_ge(o_ready, at(it, T2, TILES * (n - 1) + 1)) if n else None
                pool.tensor_tensor(heads(qg[n % 2][:, :, :]), heads(qkvr[n % 2][:, :, 0:P]), over(gc[n % 2]),
                                   ALU.mult).then_inc(qg_ready, 1)

            pool.sem_inc(s_done, 4)
            pool.sem_inc(out_done, 1)
            rstd(0, 0, 0)
            rstd(0, 0, 1)
            weigh_q(0, 0)
            with pool.Fori(0, ITS) as it:
                for p in range(2):
                    outer(it, TILES * p)
                    rstd(it, p + 1, 0)
                    outer(it, TILES * p + 1)
                    rstd(it, p + 1, 1)
                    outer(it, TILES * p + 2)
                    outer(it, TILES * p + 3)
                    weigh_q(it, p + 1)

        @block.vector
        def _(dve):
            ch = Chain(dve, dve_step, passed, 2 * 21)

            def norm1(it, n):
                return add_branch(ch, nb, x[:, it * 2 + n, :], delta[:, it * 2 + n, :], it, n)

            def norm2(it, n):
                row_stats(ch, lambda t: x[:, it * 2 + n, t * P:(t + 1) * P], nb.stats, nb.mean_var, nb.var_eps,
                          nb.var_ready)

            def make_y(it, n):
                dve.wait_ge(nb.rstd_ready, at(it, 4, 2 * n + 2))
                if n:
                    dve.wait_ge(nb.y_transposed, at(it, 2, n))
                normalised(dve, nb.y_tile, lambda t: x[:, it * 2 + n, t * P:(t + 1) * P], nb.mean_var, nb.rstd)\
                    .then_inc(nb.y_ready, 1)

            def yT_lo(it, n):
                dve.wait_ge(nb.yT_hi_ready, at(it, 2, n + 1))
                dve.tensor_tensor(yT[1][:, :], m_bank[:, :], as32(yT[0][:, :]), ALU.subtract)\
                    .then_inc(nb.yT_lo_ready, 1)

            def gates(it, n):
                dve.wait_ge(proj_read, at(it, T2, TILES * (n + 1)))
                dve.tensor_scalar(g1[:, :, :], er[:, :, H:], 1.0, 1e6, ALU.add, ALU.min).then_inc(g1_ready, 1)
                dve.wait_ge(sum_done, at(it, 2, n + 1))
                dve.tensor_scalar(lc[:, :, :].rearrange("p t h -> p (t h)"), sum_bank[:, 0:TILES * H], 30.0, -30.0,
                                  ALU.min, ALU.max).then_inc(lc_ready, 1)
                dve.wait_ge(gexp_done, at(it, 2, n + 1))
                dve.tensor_scalar(gc[n % 2][:, :, :], gexp[:, :, :], 1e-6, None, ALU.add).then_inc(gc_ready, 1)
                dve.wait_ge(gc_ready, at(it, 2, n + 1))
                ch.link(dve.scalar_tensor_tensor(out=den[:, :, :], in0=er[:, :, 0:H], scalar=1.0,
                                                 in1=gc[n % 2][:, :, :], op0=ALU.add, op1=ALU.mult))
                ch.link(dve.reciprocal(den[:, :, :], den[:, :, :]))
                ch.link(dve.tensor_tensor(den[:, :, :], den[:, :, :], qkvr[n % 2][:, :, QKV:], ALU.mult))
                dve.tensor_tensor(heads(kw[n % 2][:, :, :]), heads(qkvr[n % 2][:, :, P:2 * P]), over(den),
                                  ALU.mult).then_inc(kw_ready, 1)

            def outputs(it, j):
                n, t = j // TILES, j % TILES
                dve.wait_ge(s_done, at(it, T2, j + 5))
                if t == 0:
                    dve.wait_ge(qg_ready, at(it, 2, n + 1))
                for i in range(2):
                    s = s_bank[j % 2][i][:, :].rearrange("p (h k e) -> p h e k", k=d, e=d)
                    q = qg[n % 2][:, t, i * P // 2:(i + 1) * P // 2].rearrange("p (h o k) -> p h o k", k=d, o=1)\
                        .to_broadcast([P, H // 2, d, d])
                    ins = dve.tensor_tensor(qs[j % 2][:, i * W:(i + 1) * W].rearrange("p (h e k) -> p h e k", k=d, e=d),
                                            s, q, ALU.mult)
                ins.then_inc(qs_done, 1)
                dve.wait_ge(qs_done, at(it, T2, j + 3))
                dve.wait_ge(oT_done, at(it, 2, n + 1))
                dve.tensor_reduce(o[:, t, :], qs[j % 2][:, :].rearrange("p (c k) -> p c k", k=d), AX, ALU.add)\
                    .then_inc(o_ready, 1)

            dve.sem_inc(qs_done, 2)
            dve.sem_inc(o_ready, 1)
            norm1(0, 0)()
            norm2(0, 0)
            make_y(0, 0)
            yT_lo(0, 0)
            gates(0, 0)
            with dve.Fori(0, ITS) as it:
                ch.begin(it)
                for p in range(2):
                    rest = norm1(it, p + 1)
                    outputs(it, TILES * p)
                    rest()
                    norm2(it, p + 1)
                    outputs(it, TILES * p + 1)
                    make_y(it, p + 1)
                    yT_lo(it, p + 1)
                    outputs(it, TILES * p + 2)
                    outputs(it, TILES * p + 3)
                    gates(it, p + 1)
                ch.end()


def finish(nc, g, out):
    x, delta, minus_half = g["x"], g["delta"], g["minus_half"]
    NBLK = g["NBLK"]
    with ExitStack() as ctx:
        def sb(name, shape, dt):
            return ctx.enter_context(nc.sbuf_tensor(f"fin_{name}", shape, dt))

        def sem(name):
            return ctx.enter_context(nc.semaphore(f"fin_{name}"))

        stats = sb("stats", [P, NBLK, TILES, 6], F32)
        mean_var = sb("mean_var", [P, NBLK, TILES, 2], F32)
        var_eps = sb("var_eps", [P, NBLK, TILES], F32)
        rstd = sb("rstd", [P, NBLK, TILES], F32)
        branch = [sb(f"branch{i}", [P, W], F32) for i in range(2)]
        var_ready, rstd_ready, x_ready = sem("var_ready"), sem("rstd_ready"), sem("x_ready")
        out_stored, dve_step, passed = sem("out_stored"), sem("dve_step"), sem("passed")
        o = out.rearrange("b n d -> (b n) d").rearrange("(m t p) d -> m p t d", p=P, t=TILES)
        with nc.Block() as block:
            @block.vector
            def _(dve):
                ch = Chain(dve, dve_step, passed, 0)
                for m in range(NBLK):
                    row_stats(ch, lambda t: delta[:, m, t * P:(t + 1) * P], stats[:, m], mean_var[:, m],
                              var_eps[:, m], var_ready)
                for m in range(NBLK):
                    dve.wait_ge(rstd_ready, m + 1)
                    ch.link(normalised(dve, lambda t: branch[m % 2][:, t * P:(t + 1) * P],
                                       lambda t: delta[:, m, t * P:(t + 1) * P], mean_var[:, m], rstd[:, m]))
                    dve.tensor_tensor(x[:, m, :], x[:, m, :], branch[m % 2][:, :], ALU.add).then_inc(x_ready, 1)

            @block.gpsimd
            def _(pool):
                for m in range(NBLK):
                    inverse_std(pool, var_eps[:, m], minus_half, rstd[:, m], var_ready, m + 1, rstd_ready)

            @block.sync
            def _(sp):
                for m in range(NBLK):
                    sp.wait_ge(x_ready, m + 1)
                    sp.dma_start(o[m], x[:, m, :].rearrange("p (t d) -> p t d", t=TILES)).then_inc(out_stored, 16)
                sp.wait_ge(out_stored, 16 * NBLK)


_INS = ["L0_attn_x", "L0_attn_w_qkv", "L0_attn_w_out", "L0_attn_b_out", "L0_ffn_sw1", "L0_ffn_sw2", "L0_ffn_sw3",
        "L0_ffn_ew1", "L0_ffn_ew2", "L0_ffn_ew3", "L0_ffn_rw", "L0_ffn_rb", "L1_attn_Wq", "L1_attn_Wk",
        "L1_attn_Wv", "L1_attn_Wo", "L1_attn_gw", "L1_attn_sw", "L1_ffn_gate_w", "L1_ffn_gate_b", "L1_ffn_We1",
        "L1_ffn_be1", "L1_ffn_We2", "L1_ffn_be2", "L1_ffn_We3", "L1_ffn_be3", "L1_ffn_ws1", "L1_ffn_bs1",
        "L1_ffn_ws2", "L1_ffn_bs2", "L1_ffn_ws3", "L1_ffn_bs3"]


def kernel(**inputs):
    import numpy as _np
    import concourse.bacc as _bacc
    from concourse import mybir as _mybir
    from concourse.bass_utils import run_bass_kernel_spmd as _run

    nc = _bacc.Bacc("TRN2", target_bir_lowering=False, num_devices=1)
    arrays, args = {}, {}
    for name in _INS:
        arr = _np.ascontiguousarray(inputs[name])
        arrays[f"in_{name}_dram"] = arr
        args[name] = nc.dram_tensor(f"in_{name}_dram", arr.shape, _mybir.dt.from_np(arr.dtype),
                                    kind="ExternalInput").ap()
    shape = inputs["L0_attn_x"].shape
    out = nc.dram_tensor("out_0_dram", shape, _mybir.dt.float32, kind="ExternalOutput").ap()
    build(nc, args, out)
    r = _run(nc, [arrays], core_ids=[0])
    return r.results[0]["out_0_dram"]
```

```python
import numpy as np
import concourse.bass as bass
from concourse import mybir
from contextlib import ExitStack

F32 = mybir.dt.float32
F32R = mybir.dt.float32r
I32 = mybir.dt.int32
U32 = mybir.dt.uint32
ALU = mybir.AluOpType
ACT = mybir.ActivationFunctionType
AX = mybir.AxisListType.X

P = 128
TILES = 4
W = TILES * P
EPS = 1e-5


def at(it, per, n):
    return it * per + n


def as32(ap):
    return ap.bitcast(F32)


def product(pe, out, w, x, start=True, stop=True):
    (wh, wl), (xh, xl) = w, x
    pe.matmul(out, wh, xh, start=start, stop=False)
    pe.matmul(out, wh, xl, start=False, stop=False)
    return pe.matmul(out, wl, xh, start=False, stop=stop)


def wait_apart(eng, sem, n, passed):
    eng.wait_ge(sem, n).then_inc(passed, 1)


class Chain:

    def __init__(self, eng, sem, passed, per):
        self.passed = passed
        self.eng, self.sem, self.per, self.it, self.n, self.base = eng, sem, per, 0, 0, 0

    def begin(self, it):
        self.base, self.it, self.n = self.n, it, 0

    def link(self, ins, apart=False):
        ins.then_inc(self.sem, 1)
        self.n += 1
        n = at(self.it, self.per, self.base + self.n)
        if apart:
            wait_apart(self.eng, self.sem, n, self.passed)
        else:
            self.eng.wait_ge(self.sem, n)

    def step(self, ins):
        ins.then_inc(self.sem, 1)
        self.n += 1

    def end(self):
        assert self.n == self.per, (self.n, self.per)


def row_stats(ch, tiles, stats, mean_var, var_eps, ready):
    dve = ch.eng
    for t in range(TILES):
        ins = dve.bn_stats(stats[:, t, :], tiles(t))
        if t < TILES - 1:
            ch.step(ins)
    ch.link(ins, apart=True)
    for t in range(TILES):
        ins = dve.bn_aggr(mean_var[:, t, :], stats[:, t, :])
        if t < TILES - 1:
            ch.step(ins)
    ch.link(ins)
    dve.tensor_scalar(var_eps[:, :], mean_var[:, :, 1], EPS, None, ALU.add).then_inc(ready, 1)


def inverse_std(pool, var_eps, minus_half, rstd, ready, n_ready, done):
    pool.wait_ge(ready, n_ready)
    pool.tensor_tensor(rstd[:, :], var_eps[:, :], minus_half[:, 0:TILES], ALU.pow).then_inc(done, 1)


def normalised(dve, tiles_out, tiles_in, mean_var, rstd):
    for t in range(TILES):
        ins = dve.tensor_scalar(tiles_out(t), tiles_in(t), mean_var[:, t, 0:1], rstd[:, t:t + 1],
                                ALU.subtract, ALU.mult)
    return ins


class Norms:

    def __init__(self, sb, sem, tag):
        self.stats = sb(f"{tag}_stats", [P, TILES, 6], F32)
        self.mean_var = sb(f"{tag}_mean_var", [P, TILES, 2], F32)
        self.var_eps = sb(f"{tag}_var_eps", [P, TILES], F32)
        self.rstd = sb(f"{tag}_rstd", [P, TILES], F32)
        self.branch = sb(f"{tag}_branch", [P, W], F32)
        self.y = sb(f"{tag}_y", [P, W], F32)
        self.var_ready = sem(f"{tag}_var_ready")
        self.rstd_ready = sem(f"{tag}_rstd_ready")
        self.y_ready = sem(f"{tag}_y_ready")
        self.y_transposed = sem(f"{tag}_y_transposed")
        self.yT_hi_ready = sem(f"{tag}_yT_hi_ready")
        self.yT_lo_ready = sem(f"{tag}_yT_lo_ready")

    def y_tile(self, t):
        return self.y[:, t * P:(t + 1) * P]


def add_branch(ch, nb, x_blk, delta_blk, it, n):
    dve = ch.eng
    row_stats(ch, lambda t: delta_blk[:, t * P:(t + 1) * P], nb.stats, nb.mean_var, nb.var_eps, nb.var_ready)

    def finish():
        dve.wait_ge(nb.rstd_ready, at(it, 4, 2 * n + 1))
        ch.link(normalised(dve, lambda t: nb.branch[:, t * P:(t + 1) * P],
                           lambda t: delta_blk[:, t * P:(t + 1) * P], nb.mean_var, nb.rstd))
        ch.link(dve.tensor_tensor(x_blk, x_blk, nb.branch[:, :], ALU.add), apart=True)
    return finish


def build(nc, a, out):
    x_in, w_qkv, w_out = a["L0_attn_x"], a["L0_attn_w_qkv"], a["L0_attn_w_out"]
    B, N, D = x_in.shape
    NT = B * N // P
    NBLK = NT // TILES
    INNER = w_out.shape[0]
    HEADS = 16
    DH = INNER // HEADS
    assert D == P and N == 2 * P and NBLK % 2 == 0
    E0, HID = a["L0_ffn_rw"].shape[1], a["L0_ffn_sw1"].shape[1]
    E1, INTER = a["L1_ffn_We1"].shape[0], a["L1_ffn_We1"].shape[2]
    ITS = NBLK // 2

    with ExitStack() as ctx:
        def sb(name, shape, dt):
            return ctx.enter_context(nc.sbuf_tensor(name, shape, dt))

        def sem(name):
            return ctx.enter_context(nc.semaphore(name))

        x = sb("x", [P, NBLK + 2, W], F32)
        delta = sb("delta", [P, NBLK + 3, W], F32)
        outT = sb("outT", [P, W], F32)
        ident = sb("ident", [P, P], F32)
        minus_half = sb("minus_half", [P, TILES], F32)
        bank = [ctx.enter_context(nc.psum_tensor(f"bank{i}", [P, W], F32)) for i in range(8)]
        b_out = sb("b_out", [P, 1], F32)
        raw0 = [sb(f"raw0_{i}", [P, (E0 + 1) * HID], F32) for i in range(2)]
        raw0_down = sb("raw0_down", [P, (E0 + 1) * HID], F32)
        raw0_router = sb("raw0_router", [P, E0], F32)
        rb = sb("rb", [P, TILES * E0], F32)
        raw1 = [sb(f"raw1_{i}", [P, (E1 + 2) * INTER], F32) for i in range(2)]
        raw1_down = sb("raw1_down", [P, (E1 + 2) * INTER], F32)
        raw1_gate = sb("raw1_gate", [E1, P], F32)
        be1 = sb("be1", [P, E1 // 2 + 1], F32)
        be3 = sb("be3", [P, E1 // 2 + 1], F32)
        be2 = sb("be2", [P, P], F32)
        bs2 = sb("bs2", [P, 1], F32)
        gate_b = sb("gate_b", [P, TILES, E1], F32)
        raw_lin = sb("raw_lin", [P, 4, P], F32)
        gw = sb("gw", [P, 1], F32)
        sw = sb("sw", [P, 1], F32)
        x_loaded = sem("x_loaded")
        attn_w_loaded = sem("attn_w_loaded")
        later_w_loaded = sem("later_w_loaded")
        lw = dict(locals())
        attention(nc, a, lw)
        experts(nc, a, lw, 0)
        linear_attention(nc, a, lw)
        experts(nc, a, lw, 1)
        finish(nc, lw, out)


def attention(nc, a, g):
    x, delta, ident, bank = g["x"], g["delta"], g["ident"], g["bank"]
    minus_half, b_out = g["minus_half"], g["b_out"]
    B, N, NBLK, INNER, HEADS, DH, ITS = (g[k] for k in ("B", "N", "NBLK", "INNER", "HEADS", "DH", "ITS"))
    x_loaded, attn_w_loaded, later_w_loaded = g["x_loaded"], g["attn_w_loaded"], g["later_w_loaded"]
    E0, HID, E1, INTER = g["E0"], g["HID"], g["E1"], g["INTER"]
    PAIRS = HEADS // 2
    SCALE = float(DH) ** -0.5
    ctx = ExitStack()
    with ctx:
        def sb(name, shape, dt):
            return ctx.enter_context(nc.sbuf_tensor(name, shape, dt))

        def sem(name):
            return ctx.enter_context(nc.semaphore(name))

        A_w = [sb(f"A_{k}", [P, HEADS, P], F32R) for k in ("hi", "lo")]
        U_w = [sb(f"U_{k}", [P, HEADS, P], F32R) for k in ("hi", "lo")]

        with ExitStack() as pctx:
            def psb(name, shape, dt):
                return pctx.enter_context(nc.sbuf_tensor(name, shape, dt))

            def psem(name):
                return pctx.enter_context(nc.semaphore(name))

            wqkv_sb = psb("wqkv_sb", [P, 3 * INNER], F32)
            wout_sb = psb("wout_sb", [P, PAIRS, P], F32)
            wT = psb("wT", [P, 3, PAIRS, P], F32)
            ident_ready = psem("ident_ready")
            w_transposed = psem("w_transposed")
            w_copied = psem("w_copied")
            folded = psem("folded")
            fold_hi = psem("fold_hi")
            fold_lo = psem("fold_lo")
            later = []

            def head_of(j):
                return j // 8 * 8 + j // 4 % 2 + j % 4 * 2

            def bank_of(j, k):
                h = head_of(4 * j % HEADS)
                return (A_w if j < HEADS // 4 else U_w)[k][:, h:h + 7:2, :]
            with nc.Block() as block:
                @block.sync
                def _(sp):
                    sp.dma_start(wqkv_sb[:, :], a["L0_attn_w_qkv"]).then_inc(attn_w_loaded, 16)
                    sp.dma_start(wout_sb[:, :, :],
                                 a["L0_attn_w_out"].rearrange("(c p) n -> p c n", p=P)).then_inc(attn_w_loaded, 16)
                    xr = a["L0_attn_x"].rearrange("b n d -> (b n) d").rearrange("(m t p) d -> m p t d", p=P, t=TILES)
                    with nc.allow_non_contiguous_dma(reason="a bias column"):
                        sp.dma_start(b_out[:, :], a["L0_attn_b_out"].rearrange("(p o) -> p o", o=1))\
                            .then_inc(attn_w_loaded, 16)
                    for m in range(NBLK):
                        sp.dma_start(x[:, m, :].rearrange("p (t d) -> p t d", t=TILES), xr[m]).then_inc(x_loaded, 16)

                    def column(v):
                        return v.rearrange("(p o) -> p o", o=1)

                    def load(dst, src):
                        later.append(1)
                        sp.dma_start(dst, src).then_inc(later_w_loaded, 16)
                    with nc.allow_non_contiguous_dma(reason="bias columns"):
                        load(g["bs2"][:, :], column(a["L1_ffn_bs2"]))
                        load(g["be1"][:, 0:1], column(a["L1_ffn_bs1"]))
                        load(g["be3"][:, 0:1], column(a["L1_ffn_bs3"]))
                        load(g["be1"][:, 1:], a["L1_ffn_be1"].rearrange("(s h) i -> (h i) s", h=2))
                        load(g["be3"][:, 1:], a["L1_ffn_be3"].rearrange("(s h) i -> (h i) s", h=2))
                        for h in range(16):
                            load(g["gw"][8 * h:8 * h + 8, :], a["L1_attn_gw"].rearrange("o d -> d o"))
                            load(g["sw"][8 * h:8 * h + 8, :], a["L1_attn_sw"].rearrange("o d -> d o"))
                    for i, n in enumerate(("1", "2")):
                        load(g["raw0"][i][:, 0:HID], a[f"L0_ffn_sw{n}"])
                        load(g["raw0"][i][:, HID:].rearrange("p (e h) -> p e h", e=E0),
                             a[f"L0_ffn_ew{n}"].rearrange("e d h -> d e h"))
                    load(g["raw0_down"][:, 0:HID].rearrange("p (j n) -> p j n", n=P),
                         a["L0_ffn_sw3"].rearrange("(j p) n -> p j n", p=P))
                    load(g["raw0_down"][:, HID:].rearrange("p (e n) -> p e n", n=P),
                         a["L0_ffn_ew3"].rearrange("e h n -> (e h) n").rearrange("(e p) n -> p e n", p=P))
                    load(g["raw0_router"][:, :], a["L0_ffn_rw"])
                    for i, n in enumerate(("1", "3")):
                        load(g["raw1"][i][:, 0:P], a[f"L1_ffn_ws{n}"])
                        load(g["raw1"][i][:, P:].rearrange("p (e h) -> p e h", e=E1),
                             a[f"L1_ffn_We{n}"].rearrange("e d h -> d e h"))
                    load(g["raw1_down"][:, 0:P], a["L1_ffn_ws2"])
                    load(g["raw1_down"][:, P:].rearrange("p (e n) -> p e n", n=P),
                         a["L1_ffn_We2"].rearrange("e h n -> (e h) n").rearrange("(e p) n -> p e n", p=P))
                    load(g["raw1_gate"][:, :], a["L1_ffn_gate_w"])
                    sp.wait_ge(ident_ready, 3)
                    for row in (0, 32):
                        load(g["be2"][row:row + E1, :], a["L1_ffn_be2"])
                    for t in range(TILES):
                        load(g["rb"][:, t * E0:(t + 1) * E0],
                             a["L0_ffn_rb"].rearrange("(o e) -> o e", o=1).to_broadcast([P, E0]))
                        load(g["gate_b"][:, t, :],
                             a["L1_ffn_gate_b"].rearrange("(o e) -> o e", o=1).to_broadcast([P, E1]))
                    for i, n in enumerate(("Wq", "Wk", "Wv", "Wo")):
                        load(g["raw_lin"][:, i, :], a[f"L1_attn_{n}"])

                @block.gpsimd
                def _(pool):
                    pool.memset(ident[:, :], 0.0).then_inc(ident_ready, 1)
                    pool.wait_ge(ident_ready, 1)
                    pool.affine_select(out=ident[:, :], in_=ident[:, :], compare_op=ALU.not_equal, fill=1.0,
                                       base=0, pattern=[[-1, P]], channel_multiplier=1).then_inc(ident_ready, 1)
                    pool.memset(g["be2"][:, :], 0.0).then_inc(ident_ready, 1)
                    pool.memset(minus_half[:, :], -0.5)
                    pool.memset(x[:, NBLK:, :], 0.0)
                    pool.memset(delta[:, NBLK + 1:, :], 0.0)
                    pool.memset(g["outT"][:, :], 0.0)

                @block.tensor
                def _(pe):
                    pe.wait_ge(ident_ready, 2)
                    pe.wait_ge(attn_w_loaded, 48)
                    for j in range(3 * PAIRS):
                        ins = pe.transpose(bank[j // 4][:, j % 4 * P:(j % 4 + 1) * P], wqkv_sb[:, j * P:(j + 1) * P],
                                           ident[:, :])
                        if j % 4 == 3:
                            ins.then_inc(w_transposed, 1)
                    pe.wait_ge(w_copied, 3 * PAIRS // 4)
                    for j in range(2 * HEADS):
                        h = head_of(j % HEADS)
                        r = slice(DH * (h % 2), DH * (h % 2) + DH)
                        lhs, rhs = (wT[r, 0, h // 2, :], wT[r, 1, h // 2, :]) if j < HEADS else \
                            (wT[r, 2, h // 2, :], wout_sb[r, h // 2, :])
                        ins = pe.matmul(bank[j // 4][:, j % 4 * P:(j % 4 + 1) * P], lhs, rhs, start=True, stop=True)
                        if j % 4 == 3:
                            ins.then_inc(folded, 1)

                @block.scalar
                def _(act):
                    for j in range(3 * PAIRS // 4):
                        act.wait_ge(w_transposed, j + 1)
                        act.activation(wT[:, :, :, :].rearrange("p a c d -> p (a c d)")[:, j * W:(j + 1) * W],
                                       bank[j][:, :], ACT.Copy).then_inc(w_copied, 1)
                    for j in range(HEADS // 2):
                        act.wait_ge(folded, j + 1)
                        act.activation(bank_of(j, 0), bank[j][:, :].rearrange("p (h d) -> p h d", d=P), ACT.Copy,
                                       scale=SCALE if j < HEADS // 4 else 1.0).then_inc(fold_hi, 1)

                @block.vector
                def _(dve):
                    for j in range(HEADS // 2):
                        dve.wait_ge(fold_hi, j + 1)
                        dve.scalar_tensor_tensor(out=bank_of(j, 1), in0=bank[j][:, :].rearrange("p (h d) -> p h d", d=P),
                                                 scalar=SCALE if j < HEADS // 4 else 1.0, in1=as32(bank_of(j, 0)), op0=ALU.mult, op1=ALU.subtract).then_inc(fold_lo, 1)
            g["n_later"] = len(later)

        nb = Norms(sb, sem, "l0a")
        y_tok = [[sb(f"y_tok_{k}{p}", [P, W], F32R) for k in ("hi", "lo")] for p in range(2)]
        yT = [[sb(f"yT_{k}{p}", [P, W], F32R) for k in ("hi", "lo")] for p in range(2)]
        z = [[sb(f"z_{k}{p}", [P, W], F32R) for k in ("hi", "lo")] for p in range(2)]
        probs = [sb(f"probs{p}", [P, W], F32) for p in range(2)]
        pT = [[sb(f"pT_{k}{p}", [P, W], F32R) for k in ("hi", "lo")] for p in range(2)]
        c = [[sb(f"c_{k}{p}", [P, W], F32R) for k in ("hi", "lo")] for p in range(2)]
        outT = g["outT"]
        neg_max = sb("neg_max", [P, 2, 2], F32)
        row_sum = sb("row_sum", [P, 2, 2], F32)
        inv_sum = sb("inv_sum", [P, 2, 2], F32)
        z_bank, s_bank, t_bank, c_bank, o_bank, m_bank = bank[0], bank[1:3], bank[3:5], bank[5], bank[6], bank[7]

        z_done, z_hi_done, z_lo_done = sem("z_done"), sem("z_hi_done"), sem("z_lo_done")
        s_done, max_done, exp_done = sem("s_done"), sem("max_done"), sem("exp_done")
        inv_done, probs_ready = sem("inv_done"), sem("probs_ready")
        t_done, t_hi_done, t_lo_done = sem("t_done"), sem("t_hi_done"), sem("t_lo_done")
        c_done, c_hi_done, c_lo_done = sem("c_done"), sem("c_hi_done"), sem("c_lo_done")
        o_done, outT_done, back_done, delta_done = sem("o_done"), sem("outT_done"), sem("back_done"), sem("delta_done")
        y_lo_done, y_hi_done = sem("y_lo_done"), sem("y_hi_done")
        dve_step, passed = sem("dve_step"), sem("passed")
        UN = 2 * HEADS
        U2, H2 = 2 * UN, 2 * HEADS
        LEAD = 3

        def xt(it, n):
            return lambda t: x[:, it * 2 + n, t * P:(t + 1) * P]

        block = ctx.enter_context(nc.Block())

        @block.tensor
        def _(pe):
            def transpose_y(it, n):
                pe.wait_ge(nb.y_ready, at(it, 2, n + 1))
                if n:
                    pe.wait_ge(delta_done, at(it, 2, n))
                for t in range(TILES):
                    ins = pe.transpose(m_bank[:, t * P:(t + 1) * P], nb.y_tile(t), ident[:, :])
                ins.then_inc(nb.y_transposed, 1)

            def project(it, h):
                if h % HEADS == 0:
                    pe.wait_ge(nb.yT_hi_ready, at(it, 2, h // HEADS + 1))
                    pe.wait_ge(nb.yT_lo_ready, at(it, 2, h // HEADS + 1))
                if h:
                    pe.wait_ge(z_hi_done, at(it, H2, h))
                    pe.wait_ge(z_lo_done, at(it, H2, h))
                y = [k[:, :] for k in yT[h // HEADS % 2]]
                product(pe, z_bank[:, :], [k[:, h % HEADS, :] for k in A_w], y).then_inc(z_done, 1)

            def scores(it, u):
                h, b = u // 2, u % 2
                if b == 0:
                    pe.wait_ge(z_hi_done, at(it, H2, h + 1))
                    pe.wait_ge(z_lo_done, at(it, H2, h + 1))
                if u >= 2:
                    pe.wait_ge(exp_done, at(it, U2, u - 1))
                keys = [k[:, b * N:(b + 1) * N] for k in yT[h // HEADS % 2]]
                for q in range(2):
                    ins = product(pe, s_bank[u % 2][:, q * N:(q + 1) * N],
                                  [k[:, b * N + q * P:b * N + (q + 1) * P] for k in z[h % 2]], keys)
                ins.then_inc(s_done, 1)

            def transpose_probs(it, u):
                pe.wait_ge(probs_ready, at(it, U2, u + 1))
                pe.wait_ge(t_hi_done, at(it, U2, u + 1))
                pe.wait_ge(t_lo_done, at(it, U2, u + 1))
                for q in range(2):
                    for k in range(2):
                        ins = pe.transpose(t_bank[u % 2][:, k * N + q * P:k * N + (q + 1) * P],
                                           probs[u % 2][:, q * N + k * P:q * N + (k + 1) * P], ident[:, :])
                ins.then_inc(t_done, 1)

            def mix(it, u):
                h, b = u // 2, u % 2
                pe.wait_ge(t_hi_done, at(it, U2, u + 3))
                pe.wait_ge(t_lo_done, at(it, U2, u + 3))
                if b == 0:
                    pe.wait_ge(c_hi_done, at(it, H2, h + 1))
                    pe.wait_ge(c_lo_done, at(it, H2, h + 1))
                for k in range(2):
                    s = slice((2 * b + k) * P, (2 * b + k + 1) * P)
                    ins = product(pe, c_bank[:, b * N:(b + 1) * N], [v[:, s] for v in y_tok[h // HEADS % 2]],
                                  [v[:, k * N:(k + 1) * N] for v in pT[u % 2]], start=(k == 0), stop=(k == 1))
                ins.then_inc(c_done, 1)

            def project_out(it, h):
                pe.wait_ge(c_hi_done, at(it, H2, h + 2))
                pe.wait_ge(c_lo_done, at(it, H2, h + 2))
                if h % HEADS == 0:
                    pe.wait_ge(outT_done, at(it, 2, h // HEADS + 1))
                product(pe, o_bank[:, :], [k[:, h % HEADS, :] for k in U_w], [k[:, :] for k in c[h % 2]],
                        start=(h % HEADS == 0), stop=(h % HEADS == HEADS - 1)).then_inc(o_done, 1)

            def slot(it, h):
                project(it, h + 3)
                if h >= -1:
                    mix(it, 2 * h + 2)
                if h >= 0:
                    project_out(it, h)
                if h >= -2:
                    transpose_probs(it, 2 * h + 4)
                scores(it, 2 * h + 6)
                if h >= -1:
                    mix(it, 2 * h + 3)
                scores(it, 2 * h + 7)
                if h >= -2:
                    transpose_probs(it, 2 * h + 5)

            def transpose_out(it, n):
                pe.wait_ge(outT_done, at(it, 2, n + 1))
                pe.wait_ge(nb.yT_lo_ready, at(it, 2, n + 1))
                for t in range(TILES):
                    ins = pe.transpose(m_bank[:, t * P:(t + 1) * P], outT[:, t * P:(t + 1) * P], ident[:, :])
                ins.then_inc(back_done, 1)

            transpose_y(0, 0)
            for h in range(-LEAD, 0):
                slot(0, h)
            with pe.Fori(0, ITS) as it:
                for p in range(2):
                    for j in range(HEADS):
                        slot(it, HEADS * p + j)
                        if j == 1:
                            transpose_out(it, p)
                        if j == 8:
                            transpose_y(it, p + 1)
            transpose_out(ITS, 0)

        @block.scalar
        def _(act):
            def yT_hi(it, n):
                act.wait_ge(nb.y_transposed, at(it, 2, n + 1))
                if n:
                    act.wait_ge(c_done, at(it, U2, UN * (n - 1) + 2))
                act.activation(yT[n % 2][0][:, :], m_bank[:, :], ACT.Copy).then_inc(nb.yT_hi_ready, 1)

            def z_hi(it, h):
                act.wait_ge(z_done, at(it, H2, h + 1))
                if h >= 2:
                    act.wait_ge(s_done, at(it, U2, 2 * h - 2))
                act.activation(z[h % 2][0][:, :], z_bank[:, :], ACT.Copy).then_inc(z_hi_done, 1)

            def exps(it, u):
                act.wait_ge(max_done, at(it, U2, u + 1))
                if u >= 2:
                    act.wait_ge(t_done, at(it, U2, u - 1))
                for q in range(2):
                    ins = act.activation(probs[u % 2][:, q * N:(q + 1) * N], s_bank[u % 2][:, q * N:(q + 1) * N],
                                         ACT.Exp, bias=neg_max[:, u % 2, q:q + 1],
                                         accum_out=row_sum[:, u % 2, q:q + 1])
                ins.then_inc(exp_done, 1)

            def pT_hi(it, u):
                act.wait_ge(t_done, at(it, U2, u + 1))
                act.wait_ge(c_done, at(it, U2, u + 1))
                act.activation(pT[u % 2][0][:, :], t_bank[u % 2][:, :], ACT.Copy).then_inc(t_hi_done, 1)

            def c_hi(it, h):
                act.wait_ge(c_done, at(it, U2, 2 * h + 4))
                act.wait_ge(o_done, at(it, H2, h + 1))
                act.activation(c[h % 2][0][:, :], c_bank[:, :], ACT.Copy).then_inc(c_hi_done, 1)

            act.sem_inc(t_hi_done, 2)
            act.sem_inc(c_hi_done, 1)
            act.sem_inc(outT_done, 1)
            def slot(it, h):
                z_hi(it, h + 3)
                if h >= -2:
                    exps(it, 2 * h + 5)
                    pT_hi(it, 2 * h + 4)
                if h >= -1:
                    c_hi(it, h + 1)
                exps(it, 2 * h + 6)
                if h >= -2:
                    pT_hi(it, 2 * h + 5)

            yT_hi(0, 0)
            for h in range(-LEAD, 0):
                slot(0, h)
            with act.Fori(0, ITS) as it:
                for p in range(2):
                    for j in range(HEADS):
                        slot(it, HEADS * p + j)
                        if j == 8:
                            yT_hi(it, p + 1)
                    act.wait_ge(o_done, at(it, H2, HEADS * (p + 1) + 2))
                    act.wait_ge(back_done, at(it, 2, p + 1))
                    act.activation(outT[:, :], o_bank[:, :], ACT.Identity, bias=b_out[:, 0:1]).then_inc(outT_done, 1)

        @block.gpsimd
        def _(pool):
            def norm_probs(it, u):
                wait_apart(pool, inv_done, at(it, U2, u + 1), passed)
                for q in range(2):
                    v = probs[u % 2][:, q * N:(q + 1) * N]
                    ins = pool.tensor_scalar(v, v, inv_sum[:, u % 2, q:q + 1], 1.0, ALU.mult, ALU.mult)
                ins.then_inc(probs_ready, 1)

            def y_lo(it, n):
                pool.wait_ge(y_hi_done, at(it, 2, n + 1))
                pool.tensor_tensor(y_tok[n % 2][1][:, :], nb.y[:, :], as32(y_tok[n % 2][0][:, :]), ALU.subtract)\
                    .then_inc(y_lo_done, 1)

            pool.sem_inc(c_done, 2)
            pool.sem_inc(o_done, 2)
            inverse_std(pool, nb.var_eps, minus_half, nb.rstd, nb.var_ready, 1, nb.rstd_ready)
            y_lo(0, 0)
            for u in range(2 * LEAD - 1):
                norm_probs(0, u)
            with pool.Fori(0, ITS) as it:
                for p in range(2):
                    for s in range(UN):
                        norm_probs(it, UN * p + s + 2 * LEAD - 1)
                        if s == 8:
                            inverse_std(pool, nb.var_eps, minus_half, nb.rstd, nb.var_ready, at(it, 2, p + 2),
                                        nb.rstd_ready)
                        if s == 13:
                            y_lo(it, p + 1)

        @block.vector
        def _(dve):
            ch = Chain(dve, dve_step, passed, 2 * 9)

            def stats_of(it, n):
                row_stats(ch, xt(it, n), nb.stats, nb.mean_var, nb.var_eps, nb.var_ready)

            def make_y(it, n):
                dve.wait_ge(nb.rstd_ready, at(it, 2, n + 1))
                if n:
                    dve.wait_ge(nb.y_transposed, at(it, 2, n))
                    dve.wait_ge(y_lo_done, at(it, 2, n))
                    dve.wait_ge(c_done, at(it, U2, UN * (n - 1) + 2))
                normalised(dve, nb.y_tile, xt(it, n), nb.mean_var, nb.rstd).then_inc(nb.y_ready, 1)
                dve.wait_ge(nb.y_ready, at(it, 2, n + 1))
                ch.link(dve.tensor_copy(y_tok[n % 2][0][:, :], nb.y[:, :]))
                dve.sem_inc(y_hi_done, 1)

            def yT_lo(it, n):
                dve.wait_ge(nb.yT_hi_ready, at(it, 2, n + 1))
                dve.tensor_tensor(yT[n % 2][1][:, :], m_bank[:, :], as32(yT[n % 2][0][:, :]), ALU.subtract)\
                    .then_inc(nb.yT_lo_ready, 1)

            def z_lo(it, h):
                dve.wait_ge(z_hi_done, at(it, H2, h + 1))
                dve.tensor_tensor(z[h % 2][1][:, :], z_bank[:, :], as32(z[h % 2][0][:, :]), ALU.subtract)\
                    .then_inc(z_lo_done, 1)

            def maxima(it, u):
                dve.wait_ge(s_done, at(it, U2, u + 1))
                dve.tensor_reduce(neg_max[:, u % 2, :], s_bank[u % 2][:, :].rearrange("p (q k) -> p q k", q=2),
                                  AX, ALU.max, negate=True).then_inc(max_done, 1)

            def inverse_sums(it, u):
                dve.wait_ge(exp_done, at(it, U2, u + 1))
                dve.reciprocal(inv_sum[:, u % 2, :], row_sum[:, u % 2, :]).then_inc(inv_done, 1)

            def pT_lo(it, u):
                dve.wait_ge(t_hi_done, at(it, U2, u + 3))
                dve.tensor_tensor(pT[u % 2][1][:, :], t_bank[u % 2][:, :], as32(pT[u % 2][0][:, :]), ALU.subtract)\
                    .then_inc(t_lo_done, 1)

            def c_lo(it, h):
                dve.wait_ge(c_hi_done, at(it, H2, h + 2))
                dve.tensor_tensor(c[h % 2][1][:, :], c_bank[:, :], as32(c[h % 2][0][:, :]), ALU.subtract)\
                    .then_inc(c_lo_done, 1)

            dve.sem_inc(t_lo_done, 2)
            dve.sem_inc(c_lo_done, 1)
            dve.wait_ge(x_loaded, 16 * NBLK)
            stats_of(0, 0)
            make_y(0, 0)
            yT_lo(0, 0)
            def slot(it, h):
                z_lo(it, h + 3)
                if h >= -1:
                    pT_lo(it, 2 * h + 3)
                if h >= -2:
                    inverse_sums(it, 2 * h + 5)
                maxima(it, 2 * h + 6)
                if h >= -2:
                    pT_lo(it, 2 * h + 4)
                if h >= -1:
                    c_lo(it, h + 1)
                inverse_sums(it, 2 * h + 6)
                maxima(it, 2 * h + 7)

            def store(it, n):
                wait_apart(dve, back_done, at(it, 2, n + 1), passed)
                dve.tensor_copy(delta[:, it * 2 + n, :], m_bank[:, :]).then_inc(delta_done, 1)

            for h in range(-LEAD, 0):
                slot(0, h)
            with dve.Fori(0, ITS) as it:
                ch.begin(it)
                for p in range(2):
                    for j in range(HEADS):
                        slot(it, HEADS * p + j)
                        if j == 1:
                            store(it, p)
                        if j == 3:
                            stats_of(it, p + 1)
                        if j == 6:
                            make_y(it, p + 1)
                        if j == 8:
                            yT_lo(it, p + 1)
                ch.end()
            store(ITS, 0)


def split_weights(act, dve, pairs, hi_done, staged):
    for n, (raw, hi, lo) in enumerate(pairs):
        if act is not None:
            act.activation(hi, raw, ACT.Copy).then_inc(hi_done, 1)
        else:
            dve.wait_ge(hi_done, n + 1)
            dve.tensor_tensor(lo, raw, as32(hi), ALU.subtract).then_inc(staged, 1)


def experts(nc, a, g, layer):
    x, delta, ident, bank, minus_half = g["x"], g["delta"], g["ident"], g["bank"], g["minus_half"]
    NBLK, ITS = g["NBLK"], g["ITS"]
    E = g["E1"] if layer else g["E0"]
    LO = 32
    HALVES = 1 if layer else g["HID"] // P
    STEPS = E // 2 + 1 if layer else (E + 1) * HALVES
    SHARED = HALVES
    MAPS = (STEPS - SHARED) // HALVES
    raw = g["raw1"] if layer else g["raw0"]
    raw_down = g["raw1_down"] if layer else g["raw0_down"]
    be1, be3, be2, bs2, rb, gate_b = (g[k] for k in ("be1", "be3", "be2", "bs2", "rb", "gate_b"))
    tag = f"l{layer}e"
    NLATER = 16 * g["n_later"]
    ctx = ExitStack()
    with ctx:
        def sb(name, shape, dt):
            return ctx.enter_context(nc.sbuf_tensor(f"{tag}_{name}", shape, dt))

        def sem(name):
            return ctx.enter_context(nc.semaphore(f"{tag}_{name}"))

        up_w = [[sb(f"up{i}_{k}", [P, STEPS, P], F32R) for k in ("hi", "lo")] for i in range(2)]
        down_w = [sb(f"down_{k}", [P, STEPS, P], F32R) for k in ("hi", "lo")]
        router_w = [sb(f"router_{k}", [P, E], F32R) for k in ("hi", "lo")]
        be2_w = [sb(f"be2_{k}", [P, P], F32R) for k in ("hi", "lo")]
        pick32 = sb("pick32", [P, MAPS, P], F32)
        pick = sb("pick", [P, MAPS, P], F32R)
        gate = sb("gate", [P, TILES, P], F32)
        count = sb("count", [P, E], I32)
        place = sb("place", [P, TILES, E], F32)
        exp_base = sb("exp_base", [P, TILES], F32)
        gateT32 = sb("gateT32", [P, E], F32)
        if layer:
            before = sb("before", [P, TILES, 16], F32)
            after = sb("after", [P, TILES, 16], F32)

        with ExitStack() as pctx:
            made = pctx.enter_context(nc.semaphore(f"{tag}_made"))
            hi_done = pctx.enter_context(nc.semaphore(f"{tag}_hi_done"))
            lo_done = pctx.enter_context(nc.semaphore(f"{tag}_split"))
            gate_transposed = pctx.enter_context(nc.semaphore(f"{tag}_gate_transposed"))
            gate_copied = pctx.enter_context(nc.semaphore(f"{tag}_gate_copied"))
            small = pctx.enter_context(nc.semaphore(f"{tag}_small"))
            pairs = []
            flat = [(raw[0], up_w[0]), (raw[1], up_w[1]), (raw_down, down_w)]
            for r, w in flat:
                for s0 in range(0, STEPS, 9):
                    pairs.append((r[:, s0 * P:(s0 + 9) * P],) +
                                 tuple(k[:, s0:s0 + 9, :].rearrange("p s n -> p (s n)") for k in w))
            pairs.append((gateT32[:, :] if layer else g["raw0_router"][:, :],) + tuple(k[:, :] for k in router_w))
            if layer:
                pairs.append((be2[:, :],) + tuple(k[:, :] for k in be2_w))
            with nc.Block() as block:
                @block.gpsimd
                def _(pool):
                    pool.memset(pick32[:, :, :], 0.0).then_inc(made, 1)
                    pool.iota(count[:, :], pattern=[[1, E]], base=0, channel_multiplier=0).then_inc(made, 1)
                    pool.memset(exp_base[:, :], float(np.e))
                    pool.memset(gate[:, :, :], 0.0)
                    if layer:
                        v = pick32[:, :, :].rearrange("e m (h i) -> e m h i", h=2)
                        pattern = [[2, MAPS], [1, 2], [0, P // 2]]
                    else:
                        v, pattern = pick32[:, :, :], [[1, MAPS], [0, P]]
                    for n, row in enumerate((0, LO)):
                        pool.wait_ge(made, 2 + n)
                        pool.affine_select(out=v, in_=v, compare_op=ALU.not_equal, fill=1.0, base=row,
                                           pattern=pattern, channel_multiplier=-1).then_inc(made, 1)
                    if layer:
                        pool.memset(before[:, :, :], 0.0).then_inc(made, 1)
                        pool.memset(after[:, :, :], 0.0).then_inc(made, 1)
                        pool.wait_ge(made, 6)
                        for t, sign in ((before, 1), (after, -1)):
                            v = t[:, :, :].rearrange("p t (i j) -> p t i j", j=4)
                            pool.affine_select(out=v, in_=v, compare_op=ALU.is_ge, fill=1.0, base=0,
                                               pattern=[[0, TILES], [-sign, 4], [sign, 4]],
                                               channel_multiplier=0).then_inc(made, 1)

                @block.tensor
                def _(pe):
                    pe.wait_ge(later_loaded(g), NLATER)
                    if layer:
                        pe.transpose(bank[0][:, 0:E], g["raw1_gate"][:, :], ident[0:E, 0:E]).then_inc(gate_transposed, 1)

                @block.scalar
                def _(act):
                    act.wait_ge(later_loaded(g), NLATER)
                    if layer:
                        act.wait_ge(gate_transposed, 1)
                        act.activation(gateT32[:, :], bank[0][:, 0:E], ACT.Copy).then_inc(gate_copied, 1)
                        act.wait_ge(gate_copied, 1)
                    split_weights(act, None, pairs, hi_done, lo_done)

                @block.vector
                def _(dve):
                    dve.wait_ge(later_loaded(g), NLATER)
                    dve.wait_ge(made, 4)
                    dve.tensor_copy(pick[:, :, :], pick32[:, :, :])
                    for t in range(TILES):
                        dve.tensor_copy(place[:, t, :], count[:, :])
                    split_weights(None, dve, pairs, hi_done, lo_done)

        nb = Norms(sb, sem, "n")
        yT = [[sb(f"yT_{k}{p}", [P, W], F32R) for k in ("hi", "lo")] for p in range(2)]
        silu = [sb(f"silu{p}", [P, W], F32) for p in range(2)]
        h = [sb(f"h{p}", [P, W], F32) for p in range(3)]
        h_w = [[sb(f"h_{k}{p}", [P, W], F32R) for k in ("hi", "lo")] for p in range(3)]
        outT = g["outT"]
        gT = [sb(f"gT{p}", [P, W], F32R) for p in range(2)]
        logit = sb("logit", [P, TILES, E], F32)
        probs = sb("probs", [P, TILES, E], F32)
        top = sb("top", [P, TILES, 8], F32)
        top_at = sb("top_at", [P, TILES, 8], U32)
        top_place = sb("top_place", [P, TILES, 2], F32)
        hit = [sb(f"hit{i}", [P, TILES, E], F32) for i in range(2)]
        one = [sb(f"one{i}", [P, TILES, 1], F32) for i in range(3)]
        quad = [sb(f"quad{i}", [P, TILES, 16], F32) for i in range(3)]
        eight = [sb(f"eight{i}", [P, TILES, 8], F32) for i in range(2)]
        four = [sb(f"four{i}", [P, TILES, 4], F32) for i in range(4)]
        a_bank, b_bank, gate_bank, o_bank, m_bank, r_bank = bank[0:2], bank[2:4], bank[4], bank[5], bank[6], bank[7]

        a_done, b_done, silu_done, prod_done = sem("a_done"), sem("b_done"), sem("silu_done"), sem("prod_done")
        map_done, h_done, h_hi_done, h_lo_done = sem("map_done"), sem("h_done"), sem("h_hi_done"), sem("h_lo_done")
        down_done, outT_done, back_done, delta_done = sem("down_done"), sem("outT_done"), sem("back_done"), sem("delta_done")
        logit_done = sem("logit_done")
        gate_ready, gT_done, gT_hi_ready, gT_lo_ready = sem("gate_ready"), sem("gT_done"), sem("gT_hi_ready"), sem("gT_lo_ready")
        branch_ready, x_added = sem("branch_ready"), sem("x_added")
        diff_ready, exp_ready = sem("diff_ready"), sem("exp_ready")
        dve_step, passed = sem("dve_step"), sem("passed")
        S2, M2 = 2 * STEPS, 2 * MAPS
        (T_STATS1, T_RSTD1, T_BRANCH, T_ADD, T_STATS2, T_RSTD2, T_Y, T_YT, T_ROUTE, T_GATE, T_EXP, T_GT, AHEAD) = \
            (1, 2, 3, 4, 6, 7, 8, 0, 1, 1, 2, 6, 2) if layer else (0, 1, 2, 3, 4, 5, 6, 7, 8, 9, 12, 14, 1)
        T_OUT = 2 if layer else 1
        PARTS = 5

        block = ctx.enter_context(nc.Block())

        def gated(k):
            return k % STEPS >= SHARED

        def map_of(k):
            return k // STEPS * MAPS + (k % STEPS - SHARED) // HALVES

        @block.tensor
        def _(pe):
            def transpose_y(it, n):
                pe.wait_ge(nb.y_ready, at(it, 2, n + 1))
                if n:
                    pe.wait_ge(delta_done, at(it, 2, n))
                for t in range(TILES):
                    ins = pe.transpose(m_bank[:, t * P:(t + 1) * P], nb.y_tile(t), ident[:, :])
                ins.then_inc(nb.y_transposed, 1)

            def route(it, n):
                pe.wait_ge(nb.yT_hi_ready, at(it, 2, n + 1))
                pe.wait_ge(nb.yT_lo_ready, at(it, 2, n + 1))
                if n:
                    pe.wait_ge(gT_lo_ready, at(it, 2, n))
                for t in range(TILES):
                    ins = product(pe, r_bank[:, t * E:(t + 1) * E], [k[:, t * P:(t + 1) * P] for k in yT[n % 2]],
                                  [k[:, :] for k in router_w])
                ins.then_inc(logit_done, 1)

            def gates_across(it, n):
                pe.wait_ge(gate_ready, at(it, 2, n + 1))
                for t in range(TILES):
                    ins = pe.transpose(r_bank[:, t * P:(t + 1) * P], gate[:, t, :], ident[:, :])
                ins.then_inc(gT_done, 1)

            def up(it, k):
                s = k % STEPS
                if s == 0:
                    pe.wait_ge(nb.yT_hi_ready, at(it, 2, k // STEPS + 1))
                    pe.wait_ge(nb.yT_lo_ready, at(it, 2, k // STEPS + 1))
                y = [v[:, :] for v in yT[k // STEPS % 2]]
                if k >= 2:
                    pe.wait_ge(silu_done, at(it, S2, k - 1))
                product(pe, a_bank[k % 2][:, :], [v[:, s, :] for v in up_w[0]], y).then_inc(a_done, 1)
                if k >= 2:
                    pe.wait_ge(prod_done, at(it, S2, k - 1))
                product(pe, b_bank[k % 2][:, :], [v[:, s, :] for v in up_w[1]], y).then_inc(b_done, 1)

            def gate_map(it, k):
                if not gated(k) or (k % STEPS - SHARED) % HALVES:
                    return
                n = k // STEPS
                pe.wait_ge(gT_hi_ready, at(it, 2, n + 1))
                pe.wait_ge(gT_lo_ready, at(it, 2, n + 1))
                pe.wait_ge(h_done, at(it, S2, k))
                w = pick[:, (k % STEPS - SHARED) // HALVES, :]
                pe.matmul(gate_bank[:, :], w, gT[n % 2][:, :], start=True, stop=True).then_inc(map_done, 1)

            def down(it, k):
                s = k % STEPS
                pe.wait_ge(h_hi_done, at(it, S2, k + 1))
                pe.wait_ge(h_lo_done, at(it, S2, k + 1))
                if s == 0:
                    pe.wait_ge(outT_done, at(it, 2, k // STEPS + 1))
                product(pe, o_bank[:, :], [v[:, s, :] for v in down_w], [v[:, :] for v in h_w[k % 3]],
                        start=(s == 0), stop=(s == STEPS - 1)).then_inc(down_done, 1)
                if layer and s == 0:
                    for v in be2_w:
                        pe.matmul(o_bank[:, :], v[:, :], gT[k // STEPS % 2][:, :], start=False, stop=False)

            def transpose_out(it, n, ys):
                pe.wait_ge(outT_done, at(it, 2, n + 1))
                pe.wait_ge(nb.yT_lo_ready, at(it, 2, ys))
                for t in range(TILES):
                    ins = pe.transpose(m_bank[:, t * P:(t + 1) * P], outT[:, t * P:(t + 1) * P], ident[:, :])
                ins.then_inc(back_done, 1)

            transpose_y(0, 0)
            route(0, 0)
            up(0, 0)
            up(0, 1)
            gates_across(0, 0)
            gate_map(0, 1)
            up(0, 2)
            with pe.Fori(0, ITS) as it:
                for p in range(2):
                    for s in range(STEPS):
                        k = STEPS * p + s
                        gate_map(it, k + 2)
                        if s == T_OUT:
                            transpose_out(it, p, p + 1 + (T_YT < T_OUT))
                        if s == T_YT:
                            transpose_y(it, p + 1)
                        if s == T_ROUTE:
                            route(it, p + 1)
                        up(it, k + 3)
                        if s == T_GT:
                            gates_across(it, p + 1)
                        down(it, k)
            transpose_out(ITS, 0, 1)

        @block.scalar
        def _(act):
            def yT_hi(it, n):
                act.wait_ge(nb.y_transposed, at(it, 2, n + 1))
                if n:
                    act.wait_ge(down_done, at(it, S2, STEPS * (n - 1) + 1))
                act.activation(yT[n % 2][0][:, :], m_bank[:, :], ACT.Copy).then_inc(nb.yT_hi_ready, 1)

            def gT_hi(it, n):
                act.wait_ge(gT_done, at(it, 2, n + 1))
                if n:
                    act.wait_ge(down_done, at(it, S2, STEPS * (n - 1) + 1))
                act.activation(gT[n % 2][:, :], r_bank[:, :], ACT.Copy).then_inc(gT_hi_ready, 1)

            def exps(it, n):
                act.wait_ge(diff_ready, at(it, 2, n + 1))
                act.activation(probs[:, :, :], logit[:, :, :], ACT.Exp).then_inc(exp_ready, 1)

            def silus(it, k):
                act.wait_ge(a_done, at(it, S2, k + 1))
                if k >= 2:
                    act.wait_ge(prod_done, at(it, S2, k - 1))
                kw = dict(bias=be1[:, k % STEPS:k % STEPS + 1]) if layer else {}
                act.activation(silu[k % 2][:, :], a_bank[k % 2][:, :], ACT.Silu, **kw).then_inc(silu_done, 1)

            def h_hi(it, k):
                act.wait_ge(h_done, at(it, S2, k + 1))
                if k >= 3:
                    act.wait_ge(down_done, at(it, S2, k - 1))
                act.activation(h_w[k % 3][0][:, :], h[k % 3][:, :], ACT.Copy).then_inc(h_hi_done, 1)

            def store(it, n):
                act.wait_ge(back_done, at(it, 2, n + 1))
                act.activation(delta[:, it * 2 + n, :], m_bank[:, :], ACT.Copy).then_inc(delta_done, 1)

            act.sem_inc(down_done, 1)
            if T_YT < T_OUT:
                act.sem_inc(delta_done, 1)
            act.sem_inc(outT_done, 1)
            yT_hi(0, 0)
            if layer:
                exps(0, 0)
            silus(0, 0)
            silus(0, 1)
            h_hi(0, 0)
            gT_hi(0, 0)
            h_hi(0, 1)
            silus(0, 2)
            with act.Fori(0, ITS) as it:
                for p in range(2):
                    for s in range(STEPS):
                        k = STEPS * p + s
                        if s == T_OUT:
                            store(it, p)
                        if s == T_YT:
                            yT_hi(it, p + 1)
                        silus(it, k + 3)
                        h_hi(it, k + 2)
                        if s == T_EXP and layer:
                            exps(it, p + 1)
                        if s == T_GT:
                            gT_hi(it, p + 1)
                    act.wait_ge(down_done, at(it, S2, STEPS * (p + 1) + 1))
                    act.wait_ge(back_done, at(it, 2, p + 1))
                    if layer:
                        ins = act.activation(outT[:, :], o_bank[:, :], ACT.Identity, bias=bs2[:, 0:1])
                    else:
                        ins = act.activation(outT[:, :], o_bank[:, :], ACT.Copy)
                    ins.then_inc(outT_done, 1)
            store(ITS, 0)

        @block.gpsimd
        def _(pool):
            def h_lo(it, k):
                pool.wait_ge(h_hi_done, at(it, S2, k + 1))
                pool.tensor_tensor(h_w[k % 3][1][:, :], h[k % 3][:, :], as32(h_w[k % 3][0][:, :]), ALU.subtract)\
                    .then_inc(h_lo_done, 1)

            def rstd(it, n, second):
                inverse_std(pool, nb.var_eps, minus_half, nb.rstd, nb.var_ready, at(it, 4, 2 * n + 1 + second),
                            nb.rstd_ready)

            def add(it, n):
                pool.wait_ge(branch_ready, at(it, 2, n + 1))
                pool.tensor_tensor(x[:, it * 2 + n, :], x[:, it * 2 + n, :], nb.branch[:, :], ALU.add)\
                    .then_inc(x_added, 1)

            def powers(it, n):
                pool.wait_ge(diff_ready, at(it, 2, n + 1))
                pool.tensor_tensor(one[1][:, :, 0], exp_base[:, :], one[0][:, :, 0], ALU.pow).then_inc(exp_ready, 1)

            for n in range(AHEAD):
                rstd(0, n, 0)
                add(0, n)
                rstd(0, n, 1)
            if not layer:
                powers(0, 0)
            h_lo(0, 0)
            h_lo(0, 1)
            with pool.Fori(0, ITS) as it:
                for p in range(2):
                    for s in range(STEPS):
                        k = STEPS * p + s
                        h_lo(it, k + 2)
                        if s == T_RSTD1:
                            rstd(it, p + AHEAD, 0)
                        if s == T_ADD:
                            add(it, p + AHEAD)
                        if s == T_RSTD2:
                            rstd(it, p + AHEAD, 1)
                        if s == T_EXP and not layer:
                            powers(it, p + 1)

        @block.vector
        def _(dve):
            ch = Chain(dve, dve_step, passed, 86 if layer else 58)

            def norm1(it, n):
                if n:
                    dve.wait_ge(nb.y_ready, at(it, 2, n))
                row_stats(ch, lambda t: delta[:, it * 2 + n + 1, t * P:(t + 1) * P], nb.stats, nb.mean_var,
                          nb.var_eps, nb.var_ready)

            def branch(it, n):
                dve.wait_ge(nb.rstd_ready, at(it, 4, 2 * n + 1))
                normalised(dve, lambda t: nb.branch[:, t * P:(t + 1) * P],
                           lambda t: delta[:, it * 2 + n + 1, t * P:(t + 1) * P], nb.mean_var, nb.rstd)\
                    .then_inc(branch_ready, 1)

            def make_y(it, n):
                dve.wait_ge(nb.rstd_ready, at(it, 4, 2 * n + 2))
                if n:
                    dve.wait_ge(nb.y_transposed, at(it, 2, n))
                normalised(dve, nb.y_tile, lambda t: x[:, it * 2 + n, t * P:(t + 1) * P], nb.mean_var, nb.rstd)\
                    .then_inc(nb.y_ready, 1)

            def norm2(it, n):
                wait_apart(dve, x_added, at(it, 2, n + 1), passed)
                row_stats(ch, lambda t: x[:, it * 2 + n, t * P:(t + 1) * P], nb.stats, nb.mean_var, nb.var_eps,
                          nb.var_ready)

            def yT_lo(it, n):
                dve.wait_ge(nb.yT_hi_ready, at(it, 2, n + 1))
                dve.tensor_tensor(yT[n % 2][1][:, :], m_bank[:, :], as32(yT[n % 2][0][:, :]), ALU.subtract)\
                    .then_inc(nb.yT_lo_ready, 1)

            def gT_lo(it, n):
                dve.wait_ge(gT_hi_ready, at(it, 2, n + 1))
                lo = gT[n % 2][LO:LO + E, :]
                dve.tensor_tensor(lo, r_bank[LO:LO + E, :], as32(lo), ALU.subtract)\
                    .then_inc(gT_lo_ready, 1)

            def top_two(values):
                for t in range(TILES - 1):
                    ch.step(dve.max(top[:, t, :], values[:, t, :]))
                ch.link(dve.max(top[:, TILES - 1, :], values[:, TILES - 1, :]), apart=True)
                for t in range(TILES):
                    ins = dve.max_index(top_at[:, t, :], top[:, t, :], values[:, t, :])
                ch.link(ins)
                ch.link(dve.tensor_copy(top_place[:, :, :], top_at[:, :, 0:2]))
                for i, count in enumerate((ch.step, ch.link)):
                    count(dve.tensor_tensor(hit[i][:, :, :], place[:, :, :],
                                            top_place[:, :, i:i + 1].to_broadcast([P, TILES, E]), ALU.is_equal))

            def routing0(it, n, part):
                if part == 0:
                    dve.wait_ge(logit_done, at(it, 2, n + 1))
                    if n:
                        dve.wait_ge(gT_done, at(it, 2, n))
                    ch.link(dve.tensor_tensor(logit[:, :, :], r_bank[:, 0:TILES * E].rearrange("p (t e) -> p t e", t=TILES),
                                              rb[:, :].rearrange("p (t e) -> p t e", t=TILES), ALU.add), apart=True)
                if part == 1:
                    top_two(logit)
                if part == 2:
                    dve.tensor_tensor(one[0][:, :, :], top[:, :, 1:2], top[:, :, 0:1], ALU.subtract)\
                        .then_inc(diff_ready, 1)
                if part == 4:
                    dve.wait_ge(exp_ready, at(it, 2, n + 1))
                    ch.link(dve.tensor_scalar(one[2][:, :, :], one[1][:, :, :], 1.0, None, ALU.add))
                    ch.link(dve.reciprocal(one[2][:, :, :], one[2][:, :, :]))
                    ch.link(dve.tensor_tensor(hit[1][:, :, :], hit[1][:, :, :],
                                              one[1][:, :, :].to_broadcast([P, TILES, E]), ALU.mult))
                    ch.link(dve.tensor_tensor(hit[0][:, :, :], hit[0][:, :, :], hit[1][:, :, :], ALU.add))
                    for row in (0, LO):
                        ins = dve.tensor_tensor(gate[:, :, row:row + E], hit[0][:, :, :],
                                                one[2][:, :, :].to_broadcast([P, TILES, E]), ALU.mult)
                    ins.then_inc(gate_ready, 1)

            def routing1(it, n, part):
                if part == 0:
                    dve.wait_ge(logit_done, at(it, 2, n + 1))
                    if n:
                        dve.wait_ge(gT_done, at(it, 2, n))
                    r = r_bank[:, 0:TILES * E].rearrange("p (t e) -> p t e", t=TILES)
                    ch.link(dve.tensor_reduce(one[0][:, :, 0], r, AX, ALU.max))
                    dve.tensor_tensor(logit[:, :, :], r, one[0][:, :, :].to_broadcast([P, TILES, E]), ALU.subtract)\
                        .then_inc(diff_ready, 1)
                if part == 1:
                    dve.wait_ge(exp_ready, at(it, 2, n + 1))
                    ch.link(dve.tensor_reduce(one[1][:, :, 0], probs[:, :, :], AX, ALU.add))
                    ch.link(dve.reciprocal(one[2][:, :, :], one[1][:, :, :]))
                    ch.link(dve.tensor_tensor(probs[:, :, :], probs[:, :, :], one[2][:, :, :].to_broadcast([P, TILES, E]),
                                              ALU.mult))
                    ch.link(dve.tensor_tensor(logit[:, :, :], probs[:, :, :], gate_b[:, :, :], ALU.add))
                    v = logit[:, :, :].rearrange("p t (g o) -> p t g o", o=2)
                    ch.step(dve.tensor_tensor(eight[0][:, :, :], v[:, :, :, 0], v[:, :, :, 1], ALU.max))
                    ch.link(dve.tensor_tensor(eight[1][:, :, :], v[:, :, :, 0], v[:, :, :, 1], ALU.add))
                    m, a = (v[:, :, :].rearrange("p t (g o) -> p t g o", o=2) for v in eight)
                    ch.step(dve.tensor_tensor(four[0][:, :, :], m[:, :, :, 0], m[:, :, :, 1], ALU.add))
                    ch.link(dve.tensor_tensor(four[1][:, :, :], a[:, :, :, 0], a[:, :, :, 1], ALU.max))
                    ch.link(dve.tensor_tensor(four[2][:, :, :], four[0][:, :, :], four[1][:, :, :], ALU.max))
                if part == 2:
                    q = [v[:, :, :].rearrange("p t (i j) -> p t i j", j=4) for v in quad]
                    own = four[2][:, :, :].rearrange("p t (i o) -> p t i o", o=1).to_broadcast([P, TILES, 4, 4])
                    other = four[2][:, :, :].rearrange("p t (o j) -> p t o j", o=1).to_broadcast([P, TILES, 4, 4])
                    ch.step(dve.tensor_tensor(q[1], other, own, ALU.is_ge))
                    ch.link(dve.tensor_tensor(q[2], other, own, ALU.is_gt))
                    ch.step(dve.tensor_tensor(quad[1][:, :, :], quad[1][:, :, :], before[:, :, :], ALU.mult))
                    ch.link(dve.tensor_tensor(quad[2][:, :, :], quad[2][:, :, :], after[:, :, :], ALU.mult))
                    ch.link(dve.tensor_tensor(quad[0][:, :, :], quad[1][:, :, :], quad[2][:, :, :], ALU.add))
                    ch.link(dve.tensor_reduce(four[3][:, :, :], q[0], AX, ALU.add))
                if part == 3:
                    ch.link(dve.tensor_scalar(four[3][:, :, :], four[3][:, :, :], 1.5, -1e30, ALU.is_gt, ALU.mult))
                    out4 = four[3][:, :, :].rearrange("p t (i o) -> p t i o", o=1).to_broadcast([P, TILES, 4, 4])
                    l4 = logit[:, :, :].rearrange("p t (i j) -> p t i j", j=4)
                    ch.link(dve.tensor_tensor(l4, l4, out4, ALU.add), apart=True)
                    top_two(logit)
                if part == 4:
                    ch.link(dve.tensor_tensor(hit[0][:, :, :], hit[0][:, :, :], hit[1][:, :, :], ALU.add))
                    for row in (0, LO):
                        ins = dve.tensor_tensor(gate[:, :, row:row + E], hit[0][:, :, :], probs[:, :, :], ALU.mult)
                    ins.then_inc(gate_ready, 1)

            routing = routing1 if layer else routing0

            def prod(it, k):
                dve.wait_ge(silu_done, at(it, S2, k + 1))
                dve.wait_ge(b_done, at(it, S2, k + 1))
                if k >= 3:
                    dve.wait_ge(h_lo_done, at(it, S2, k - 2))
                if layer:
                    ins = dve.scalar_tensor_tensor(out=h[k % 3][:, :], in0=b_bank[k % 2][:, :],
                                                   scalar=be3[:, k % STEPS:k % STEPS + 1], in1=silu[k % 2][:, :],
                                                   op0=ALU.add, op1=ALU.mult)
                else:
                    ins = dve.tensor_tensor(h[k % 3][:, :], b_bank[k % 2][:, :], silu[k % 2][:, :], ALU.mult)
                ins.then_inc(prod_done, 1)

            def weigh(it, k):
                dve.wait_ge(prod_done, at(it, S2, k + 1))
                if gated(k):
                    dve.wait_ge(map_done, at(it, M2, map_of(k) + 1))
                    dve.tensor_tensor(h[k % 3][:, :], gate_bank[:, :], h[k % 3][:, :], ALU.mult).then_inc(h_done, 1)
                else:
                    dve.sem_inc(h_done, 1)

            for n in range(AHEAD):
                norm1(0, n)
                branch(0, n)
                norm2(0, n)
                make_y(0, n)
                if n == 0:
                    yT_lo(0, 0)
            for part in range(PARTS):
                routing(0, 0, part)
            prod(0, 0)
            weigh(0, 0)
            prod(0, 1)
            gT_lo(0, 0)
            weigh(0, 1)
            prod(0, 2)
            with dve.Fori(0, ITS) as it:
                ch.begin(it)
                for p in range(2):
                    for s in range(STEPS):
                        k = STEPS * p + s
                        weigh(it, k + 2)
                        prod(it, k + 3)
                        if s == T_STATS1:
                            norm1(it, p + AHEAD)
                        if s == T_BRANCH:
                            branch(it, p + AHEAD)
                        if s == T_STATS2:
                            norm2(it, p + AHEAD)
                        if s == T_Y:
                            make_y(it, p + AHEAD)
                        if s == T_YT:
                            yT_lo(it, p + 1)
                        if T_GATE <= s < T_GATE + PARTS:
                            routing(it, p + 1, s - T_GATE)
                        if s == T_GT:
                            gT_lo(it, p + 1)
                ch.end()


def later_loaded(g):
    return g["later_w_loaded"]


def linear_attention(nc, a, g):
    x, delta, ident, bank, minus_half, raw = g["x"], g["delta"], g["ident"], g["bank"], g["minus_half"], g["raw_lin"]
    NBLK, ITS = g["NBLK"], g["ITS"]
    H, d = 16, 8
    KVN = H * d * d
    QKV = 3 * P
    PROJ = QKV + 2 * H
    NLATER = 16 * g["n_later"]
    ctx = ExitStack()
    with ctx:
        def sb(name, shape, dt):
            return ctx.enter_context(nc.sbuf_tensor(f"lin_{name}", shape, dt))

        def sem(name):
            return ctx.enter_context(nc.semaphore(f"lin_{name}"))

        proj32 = sb("proj32", [P, PROJ], F32)
        proj_w = [sb(f"proj_{k}", [P, PROJ], F32R) for k in ("hi", "lo")]
        woT = sb("woT", [P, P], F32)
        tri = sb("tri", [P, P], F32)
        ones = sb("ones", [P, P], F32)
        own = sb("own", [P, H], F32)
        sw_own = sb("sw_own", [P, H], F32)
        made, copied, folded, gated, hi_done, split = (sem(n) for n in
                                                       ("made", "copied", "folded", "gated", "hi_done", "split"))
        with nc.Block() as block:
            @block.gpsimd
            def _(pool):
                pool.memset(tri[:, :], 1.0).then_inc(made, 1)
                pool.memset(own[:, :], 1.0).then_inc(made, 1)
                pool.memset(ones[:, :], 1.0)
                pool.wait_ge(made, 2)
                pool.affine_select(out=tri[:, :], in_=tri[:, :], compare_op=ALU.is_ge, fill=0.0, base=0,
                                   pattern=[[1, P]], channel_multiplier=-1)
                pool.affine_select(out=own[:, :], in_=own[:, :], compare_op=ALU.is_ge, fill=0.0, base=0,
                                   pattern=[[-d, H]], channel_multiplier=1).then_inc(made, 1)
                pool.wait_ge(made, 3)
                pool.affine_select(out=own[:, :], in_=own[:, :], compare_op=ALU.is_ge, fill=0.0, base=d - 1,
                                   pattern=[[d, H]], channel_multiplier=-1).then_inc(made, 1)

            @block.tensor
            def _(pe):
                for i in range(4):
                    ins = pe.transpose(bank[0][:, i * P:(i + 1) * P], raw[:, i, :], ident[:, :])
                ins.then_inc(folded, 1)
                pe.wait_ge(gated, 2)
                pe.matmul(bank[1][:, 0:H], raw[:, 1, :], sw_own[:, :], start=True, stop=True).then_inc(folded, 1)

            @block.vector
            def _(dve):
                dve.wait_ge(made, 4)
                dve.tensor_scalar(sw_own[:, :], own[:, :], g["sw"][:, 0:1], None, ALU.mult).then_inc(gated, 1)
                dve.tensor_scalar(proj32[:, QKV + H:], own[:, :], g["gw"][:, 0:1], None, ALU.mult).then_inc(gated, 1)
                dve.wait_ge(hi_done, 1)
                dve.tensor_tensor(proj_w[1][:, :], proj32[:, :], as32(proj_w[0][:, :]), ALU.subtract)

            @block.scalar
            def _(act):
                act.wait_ge(folded, 1)
                act.activation(proj32[:, 0:QKV], bank[0][:, 0:QKV], ACT.Copy).then_inc(copied, 1)
                act.activation(woT[:, :], bank[0][:, QKV:], ACT.Copy)
                act.wait_ge(folded, 2)
                act.activation(proj32[:, QKV:QKV + H], bank[1][:, 0:H], ACT.Copy).then_inc(copied, 1)
                act.wait_ge(copied, 2)
                act.wait_ge(gated, 2)
                act.activation(proj_w[0][:, :], proj32[:, :], ACT.Copy).then_inc(hi_done, 1)

        nb = Norms(sb, sem, "n")
        yT = [sb(f"yT_{k}", [P, W], F32R) for k in ("hi", "lo")]
        qkvr = [sb(f"qkvr{p}", [P, TILES, QKV + H], F32) for p in range(2)]
        er = sb("er", [P, TILES, 2 * H], F32)
        g1 = sb("g1", [P, TILES, H], F32)
        lg = sb("lg", [P, TILES, H], F32)
        lc = sb("lc", [P, TILES, H], F32)
        gexp = sb("gexp", [P, TILES, H], F32)
        gc = [sb(f"gc{p}", [P, TILES, H], F32) for p in range(2)]
        den = sb("den", [P, TILES, H], F32)
        kw = [sb(f"kw{p}", [P, TILES, P], F32) for p in range(2)]
        qg = [sb(f"qg{p}", [P, TILES, P], F32) for p in range(2)]
        kv = sb("kv", [P, TILES, KVN], F32)
        qs = [sb(f"qs{p}", [P, KVN], F32) for p in range(2)]
        o = sb("o", [P, TILES, P], F32)
        oT = sb("oT", [P, W], F32)
        p_bank, s_bank, m_bank, oT_bank, sum_bank = bank[0], [bank[1:3], bank[3:5]], bank[5], bank[6], bank[7]

        proj_done, proj_read, g1_ready, ln_done = sem("proj_done"), sem("proj_read"), sem("g1_ready"), sem("ln_done")
        sum_done, lc_ready, gexp_done, gc_ready = sem("sum_done"), sem("lc_ready"), sem("gexp_done"), sem("gc_ready")
        kw_ready, qg_ready, kv_ready, s_done = sem("kw_ready"), sem("qg_ready"), sem("kv_ready"), sem("s_done")
        qs_done, o_ready, oT_done, oT_ready = sem("qs_done"), sem("o_ready"), sem("oT_done"), sem("oT_ready")
        out_done, delta_done, dve_step, passed = sem("out_done"), sem("delta_done"), sem("dve_step"), sem("passed")
        T2 = 2 * TILES

        def heads(v):
            return v.rearrange("p t (h k) -> p t h k", k=d)

        def over(v):
            return v[:, :, :].rearrange("p t (h o) -> p t h o", o=1).to_broadcast([P, TILES, H, d])

        block = ctx.enter_context(nc.Block())

        @block.tensor
        def _(pe):
            def transpose_y(it, n):
                pe.wait_ge(nb.y_ready, at(it, 2, n + 1))
                if n:
                    pe.wait_ge(nb.yT_lo_ready, at(it, 2, n))
                for t in range(TILES):
                    ins = pe.transpose(m_bank[:, t * P:(t + 1) * P], nb.y_tile(t), ident[:, :])
                ins.then_inc(nb.y_transposed, 1)

            def project(it, j):
                n, t = j // TILES, j % TILES
                if t == 0:
                    pe.wait_ge(nb.yT_hi_ready, at(it, 2, n + 1))
                    pe.wait_ge(nb.yT_lo_ready, at(it, 2, n + 1))
                    if n:
                        pe.wait_ge(delta_done, at(it, 2, n))
                if j:
                    pe.wait_ge(proj_read, at(it, T2, j))
                product(pe, p_bank[:, 0:PROJ], [v[:, t * P:(t + 1) * P] for v in yT], [v[:, :] for v in proj_w])\
                    .then_inc(proj_done, 1)

            def cumulate(it, n):
                pe.wait_ge(ln_done, at(it, 2, n + 1))
                if n:
                    pe.wait_ge(lc_ready, at(it, 2, n))
                v = lg[:, :, :].rearrange("p t h -> p (t h)")
                first = lg[:, :, :].rearrange("p (b j) h -> p b j h", j=2)[:, :, 0, :]
                second = sum_bank[:, 0:TILES * H].rearrange("p (b j h) -> p b j h", j=2, h=H)[:, :, 1, :]
                pe.matmul(sum_bank[:, 0:TILES * H], tri[:, :], v, start=True, stop=False)
                pe.matmul(second, ones[:, :], first, start=False, stop=True).then_inc(sum_done, 1)

            def states(it, j):
                t = j % TILES
                pe.wait_ge(kv_ready, at(it, T2, j + 1))
                pe.wait_ge(qs_done, at(it, T2, j + 1))
                for i in range(2):
                    s = slice(i * W, (i + 1) * W)
                    if t % 2:
                        pe.matmul(s_bank[j % 2][i][:, :], ones[:, :], kv[:, t - 1, s], start=True, stop=False)
                    ins = pe.matmul(s_bank[j % 2][i][:, :], tri[:, :], kv[:, t, s], start=(t % 2 == 0), stop=True)
                ins.then_inc(s_done, 1)

            def project_out(it, n):
                pe.wait_ge(o_ready, at(it, T2, TILES * n + TILES + 1))
                for t in range(TILES):
                    ins = pe.transpose(oT_bank[:, t * P:(t + 1) * P], o[:, t, :], ident[:, :])
                ins.then_inc(oT_done, 1)
                pe.wait_ge(oT_ready, at(it, 2, n + 1))
                pe.wait_ge(proj_read, at(it, T2, TILES * (n + 2)))
                for t in range(TILES):
                    ins = pe.matmul(p_bank[:, t * P:(t + 1) * P], oT[:, t * P:(t + 1) * P], woT[:, :],
                                    start=True, stop=True)
                ins.then_inc(out_done, 1)

            transpose_y(0, 0)
            for j in range(TILES):
                project(0, j)
            cumulate(0, 0)
            with pe.Fori(0, ITS) as it:
                for p in range(2):
                    for t in range(TILES):
                        states(it, TILES * p + t)
                        if t == 1:
                            transpose_y(it, p + 1)
                        if t == 2:
                            for j in range(TILES):
                                project(it, TILES * (p + 1) + j)
                    cumulate(it, p + 1)
                    project_out(it, p)

        @block.scalar
        def _(act):
            def yT_hi(it, n):
                act.wait_ge(nb.y_transposed, at(it, 2, n + 1))
                if n:
                    act.wait_ge(proj_done, at(it, T2, TILES * n))
                act.activation(yT[0][:, :], m_bank[:, :], ACT.Copy).then_inc(nb.yT_hi_ready, 1)

            def read_projection(it, j):
                n, t = j // TILES, j % TILES
                act.wait_ge(proj_done, at(it, T2, j + 1))
                if n:
                    act.wait_ge(o_ready, at(it, T2, TILES * (n - 1) + 1))
                    act.wait_ge(kw_ready, at(it, 2, n))
                act.activation(qkvr[n % 2][:, t, :], p_bank[:, 0:QKV + H], ACT.Copy)
                act.activation(er[:, t, :], p_bank[:, QKV:PROJ], ACT.Exp, scale=-1.0).then_inc(proj_read, 1)

            def log_gate(it, n):
                act.wait_ge(g1_ready, at(it, 2, n + 1))
                if n:
                    act.wait_ge(sum_done, at(it, 2, n))
                act.activation(lg[:, :, :], g1[:, :, :], ACT.Ln).then_inc(ln_done, 1)

            def exp_gate(it, n):
                act.wait_ge(lc_ready, at(it, 2, n + 1))
                act.activation(gexp[:, :, :], lc[:, :, :], ACT.Exp, scale=-1.0).then_inc(gexp_done, 1)

            act.preload_act_table_set("natural_log_exp_and_others")
            act.sem_inc(oT_done, 1)
            act.sem_inc(delta_done, 1)
            yT_hi(0, 0)
            for j in range(TILES):
                read_projection(0, j)
            log_gate(0, 0)
            exp_gate(0, 0)
            with act.Fori(0, ITS) as it:
                for p in range(2):
                    yT_hi(it, p + 1)
                    for j in range(TILES):
                        read_projection(it, TILES * (p + 1) + j)
                    log_gate(it, p + 1)
                    exp_gate(it, p + 1)
                    act.wait_ge(oT_done, at(it, 2, p + 2))
                    act.wait_ge(out_done, at(it, 2, p + 1))
                    act.activation(oT[:, :], oT_bank[:, :], ACT.Copy).then_inc(oT_ready, 1)
                    act.wait_ge(out_done, at(it, 2, p + 2))
                    act.activation(delta[:, it * 2 + p + 1, :], p_bank[:, :], ACT.Copy).then_inc(delta_done, 1)

        @block.gpsimd
        def _(pool):
            def rstd(it, n, second):
                inverse_std(pool, nb.var_eps, minus_half, nb.rstd, nb.var_ready, at(it, 4, 2 * n + 1 + second),
                            nb.rstd_ready)

            def outer(it, j):
                n, t = j // TILES, j % TILES
                pool.wait_ge(kw_ready, at(it, 2, n + 1))
                pool.wait_ge(s_done, at(it, T2, j + (1 if t % 2 else 2)))
                out = kv[:, t, :].rearrange("p (h k e) -> p h k e", k=d, e=d)
                k = kw[n % 2][:, t, :].rearrange("p (h k o) -> p h k o", k=d, o=1).to_broadcast([P, H, d, d])
                v = qkvr[n % 2][:, t, 2 * P:QKV].rearrange("p (h o e) -> p h o e", e=d, o=1)\
                    .to_broadcast([P, H, d, d])
                pool.tensor_tensor(out, k, v, ALU.mult).then_inc(kv_ready, 1)

            def weigh_q(it, n):
                pool.wait_ge(gc_ready, at(it, 2, n + 1))
                pool.wait_ge(o_ready, at(it, T2, TILES * (n - 1) + 1)) if n else None
                pool.tensor_tensor(heads(qg[n % 2][:, :, :]), heads(qkvr[n % 2][:, :, 0:P]), over(gc[n % 2]),
                                   ALU.mult).then_inc(qg_ready, 1)

            pool.sem_inc(s_done, 4)
            pool.sem_inc(out_done, 1)
            rstd(0, 0, 0)
            rstd(0, 0, 1)
            weigh_q(0, 0)
            with pool.Fori(0, ITS) as it:
                for p in range(2):
                    outer(it, TILES * p)
                    rstd(it, p + 1, 0)
                    outer(it, TILES * p + 1)
                    rstd(it, p + 1, 1)
                    outer(it, TILES * p + 2)
                    outer(it, TILES * p + 3)
                    weigh_q(it, p + 1)

        @block.vector
        def _(dve):
            ch = Chain(dve, dve_step, passed, 2 * 21)

            def norm1(it, n):
                return add_branch(ch, nb, x[:, it * 2 + n, :], delta[:, it * 2 + n + 1, :], it, n)

            def norm2(it, n):
                row_stats(ch, lambda t: x[:, it * 2 + n, t * P:(t + 1) * P], nb.stats, nb.mean_var, nb.var_eps,
                          nb.var_ready)

            def make_y(it, n):
                dve.wait_ge(nb.rstd_ready, at(it, 4, 2 * n + 2))
                if n:
                    dve.wait_ge(nb.y_transposed, at(it, 2, n))
                normalised(dve, nb.y_tile, lambda t: x[:, it * 2 + n, t * P:(t + 1) * P], nb.mean_var, nb.rstd)\
                    .then_inc(nb.y_ready, 1)

            def yT_lo(it, n):
                dve.wait_ge(nb.yT_hi_ready, at(it, 2, n + 1))
                dve.tensor_tensor(yT[1][:, :], m_bank[:, :], as32(yT[0][:, :]), ALU.subtract)\
                    .then_inc(nb.yT_lo_ready, 1)

            def gates(it, n):
                dve.wait_ge(proj_read, at(it, T2, TILES * (n + 1)))
                dve.tensor_scalar(g1[:, :, :], er[:, :, H:], 1.0, 1e6, ALU.add, ALU.min).then_inc(g1_ready, 1)
                dve.wait_ge(sum_done, at(it, 2, n + 1))
                dve.tensor_scalar(lc[:, :, :].rearrange("p t h -> p (t h)"), sum_bank[:, 0:TILES * H], 30.0, -30.0,
                                  ALU.min, ALU.max).then_inc(lc_ready, 1)
                dve.wait_ge(gexp_done, at(it, 2, n + 1))
                dve.tensor_scalar(gc[n % 2][:, :, :], gexp[:, :, :], 1e-6, None, ALU.add).then_inc(gc_ready, 1)
                dve.wait_ge(gc_ready, at(it, 2, n + 1))
                ch.link(dve.scalar_tensor_tensor(out=den[:, :, :], in0=er[:, :, 0:H], scalar=1.0,
                                                 in1=gc[n % 2][:, :, :], op0=ALU.add, op1=ALU.mult))
                ch.link(dve.reciprocal(den[:, :, :], den[:, :, :]))
                ch.link(dve.tensor_tensor(den[:, :, :], den[:, :, :], qkvr[n % 2][:, :, QKV:], ALU.mult))
                dve.tensor_tensor(heads(kw[n % 2][:, :, :]), heads(qkvr[n % 2][:, :, P:2 * P]), over(den),
                                  ALU.mult).then_inc(kw_ready, 1)

            def outputs(it, j):
                n, t = j // TILES, j % TILES
                dve.wait_ge(s_done, at(it, T2, j + 5))
                if t == 0:
                    dve.wait_ge(qg_ready, at(it, 2, n + 1))
                for i in range(2):
                    s = s_bank[j % 2][i][:, :].rearrange("p (h k e) -> p h e k", k=d, e=d)
                    q = qg[n % 2][:, t, i * P // 2:(i + 1) * P // 2].rearrange("p (h o k) -> p h o k", k=d, o=1)\
                        .to_broadcast([P, H // 2, d, d])
                    ins = dve.tensor_tensor(qs[j % 2][:, i * W:(i + 1) * W].rearrange("p (h e k) -> p h e k", k=d, e=d),
                                            s, q, ALU.mult)
                ins.then_inc(qs_done, 1)
                dve.wait_ge(qs_done, at(it, T2, j + 3))
                dve.wait_ge(oT_done, at(it, 2, n + 1))
                dve.tensor_reduce(o[:, t, :], qs[j % 2][:, :].rearrange("p (c k) -> p c k", k=d), AX, ALU.add)\
                    .then_inc(o_ready, 1)

            dve.sem_inc(qs_done, 2)
            dve.sem_inc(o_ready, 1)
            norm1(0, 0)()
            norm2(0, 0)
            make_y(0, 0)
            yT_lo(0, 0)
            gates(0, 0)
            with dve.Fori(0, ITS) as it:
                ch.begin(it)
                for p in range(2):
                    rest = norm1(it, p + 1)
                    outputs(it, TILES * p)
                    rest()
                    norm2(it, p + 1)
                    outputs(it, TILES * p + 1)
                    make_y(it, p + 1)
                    yT_lo(it, p + 1)
                    outputs(it, TILES * p + 2)
                    outputs(it, TILES * p + 3)
                    gates(it, p + 1)
                ch.end()


def finish(nc, g, out):
    x, delta, minus_half = g["x"], g["delta"], g["minus_half"]
    NBLK = g["NBLK"]
    with ExitStack() as ctx:
        def sb(name, shape, dt):
            return ctx.enter_context(nc.sbuf_tensor(f"fin_{name}", shape, dt))

        def sem(name):
            return ctx.enter_context(nc.semaphore(f"fin_{name}"))

        stats = sb("stats", [P, NBLK, TILES, 6], F32)
        mean_var = sb("mean_var", [P, NBLK, TILES, 2], F32)
        var_eps = sb("var_eps", [P, NBLK, TILES], F32)
        rstd = sb("rstd", [P, NBLK, TILES], F32)
        branch = [sb(f"branch{i}", [P, W], F32) for i in range(2)]
        var_ready, rstd_ready, x_ready = sem("var_ready"), sem("rstd_ready"), sem("x_ready")
        out_stored, dve_step, passed = sem("out_stored"), sem("dve_step"), sem("passed")
        o = out.rearrange("b n d -> (b n) d").rearrange("(m t p) d -> m p t d", p=P, t=TILES)
        with nc.Block() as block:
            @block.vector
            def _(dve):
                ch = Chain(dve, dve_step, passed, 0)
                for m in range(NBLK):
                    row_stats(ch, lambda t: delta[:, m + 1, t * P:(t + 1) * P], stats[:, m], mean_var[:, m],
                              var_eps[:, m], var_ready)
                for m in range(NBLK):
                    dve.wait_ge(rstd_ready, m + 1)
                    ch.link(normalised(dve, lambda t: branch[m % 2][:, t * P:(t + 1) * P],
                                       lambda t: delta[:, m + 1, t * P:(t + 1) * P], mean_var[:, m], rstd[:, m]))
                    dve.tensor_tensor(x[:, m, :], x[:, m, :], branch[m % 2][:, :], ALU.add).then_inc(x_ready, 1)

            @block.gpsimd
            def _(pool):
                for m in range(NBLK):
                    inverse_std(pool, var_eps[:, m], minus_half, rstd[:, m], var_ready, m + 1, rstd_ready)

            @block.sync
            def _(sp):
                for m in range(NBLK):
                    sp.wait_ge(x_ready, m + 1)
                    sp.dma_start(o[m], x[:, m, :].rearrange("p (t d) -> p t d", t=TILES)).then_inc(out_stored, 16)
                sp.wait_ge(out_stored, 16 * NBLK)


_INS = ["L0_attn_x", "L0_attn_w_qkv", "L0_attn_w_out", "L0_attn_b_out", "L0_ffn_sw1", "L0_ffn_sw2", "L0_ffn_sw3",
        "L0_ffn_ew1", "L0_ffn_ew2", "L0_ffn_ew3", "L0_ffn_rw", "L0_ffn_rb", "L1_attn_Wq", "L1_attn_Wk",
        "L1_attn_Wv", "L1_attn_Wo", "L1_attn_gw", "L1_attn_sw", "L1_ffn_gate_w", "L1_ffn_gate_b", "L1_ffn_We1",
        "L1_ffn_be1", "L1_ffn_We2", "L1_ffn_be2", "L1_ffn_We3", "L1_ffn_be3", "L1_ffn_ws1", "L1_ffn_bs1",
        "L1_ffn_ws2", "L1_ffn_bs2", "L1_ffn_ws3", "L1_ffn_bs3"]


def kernel(**inputs):
    import numpy as _np
    import concourse.bacc as _bacc
    from concourse import mybir as _mybir
    from concourse.bass_utils import run_bass_kernel_spmd as _run

    nc = _bacc.Bacc("TRN2", target_bir_lowering=False, num_devices=1)
    arrays, args = {}, {}
    for name in _INS:
        arr = _np.ascontiguousarray(inputs[name])
        arrays[f"in_{name}_dram"] = arr
        args[name] = nc.dram_tensor(f"in_{name}_dram", arr.shape, _mybir.dt.from_np(arr.dtype),
                                    kind="ExternalInput").ap()
    shape = inputs["L0_attn_x"].shape
    out = nc.dram_tensor("out_0_dram", shape, _mybir.dt.float32, kind="ExternalOutput").ap()
    build(nc, args, out)
    r = _run(nc, [arrays], core_ids=[0])
    return r.results[0]["out_0_dram"]
```

```python
import numpy as np
import concourse.bass as bass
from concourse import mybir
from contextlib import ExitStack

F32 = mybir.dt.float32
F32R = mybir.dt.float32r
I32 = mybir.dt.int32
U32 = mybir.dt.uint32
ALU = mybir.AluOpType
ACT = mybir.ActivationFunctionType
AX = mybir.AxisListType.X

P = 128
TILES = 4
W = TILES * P
EPS = 1e-5


def at(it, per, n):
    return it * per + n


def as32(ap):
    return ap.bitcast(F32)


def product(pe, out, w, x, start=True, stop=True):
    (wh, wl), (xh, xl) = w, x
    pe.matmul(out, wh, xh, start=start, stop=False)
    pe.matmul(out, wh, xl, start=False, stop=False)
    return pe.matmul(out, wl, xh, start=False, stop=stop)


def wait_apart(eng, sem, n, passed):
    eng.wait_ge(sem, n).then_inc(passed, 1)


class Chain:

    def __init__(self, eng, sem, passed, per):
        self.passed = passed
        self.eng, self.sem, self.per, self.it, self.n, self.base = eng, sem, per, 0, 0, 0

    def begin(self, it):
        self.base, self.it, self.n = self.n, it, 0

    def link(self, ins, apart=False):
        ins.then_inc(self.sem, 1)
        self.n += 1
        n = at(self.it, self.per, self.base + self.n)
        if apart:
            wait_apart(self.eng, self.sem, n, self.passed)
        else:
            self.eng.wait_ge(self.sem, n)

    def step(self, ins):
        ins.then_inc(self.sem, 1)
        self.n += 1

    def end(self):
        assert self.n == self.per, (self.n, self.per)


def row_stats(ch, tiles, nb, ready, negate=False):
    dve = ch.eng
    for t in range(TILES - 1):
        ch.step(dve.bn_stats(nb.stats[:, t, :], tiles(t)))
    ch.link(dve.bn_stats(nb.stats[:, TILES - 1, :], tiles(TILES - 1)), apart=True)
    for t in range(TILES - 1):
        ch.step(dve.bn_aggr(nb.mean_var[:, t, :], nb.stats[:, t, :]))
    ch.link(dve.bn_aggr(nb.mean_var[:, TILES - 1, :], nb.stats[:, TILES - 1, :]))
    if negate:
        dve.tensor_scalar(nb.neg_mean[:, :], nb.mean_var[:, :, 0], -1.0, None, ALU.mult)
    dve.tensor_scalar(nb.var_eps[:, :], nb.mean_var[:, :, 1], EPS, None, ALU.add).then_inc(ready, 1)


def inverse_std(pool, var_eps, minus_half, rstd, ready, n_ready, done):
    pool.wait_ge(ready, n_ready)
    pool.tensor_tensor(rstd[:, :], var_eps[:, :], minus_half[:, 0:TILES], ALU.pow).then_inc(done, 1)


def scale_and_shift(pool, nb, minus_half, n_ready):
    inverse_std(pool, nb.var_eps, minus_half, nb.rstd, nb.var_ready, n_ready, nb.pow_done)
    pool.wait_ge(nb.pow_done, n_ready)
    pool.tensor_tensor(nb.shift[:, :], nb.neg_mean[:, :], nb.rstd[:, :], ALU.mult).then_inc(nb.rstd_ready, 1)


def scaled(act, tiles_out, tiles_in, nb, tiles=range(TILES)):
    for t in tiles:
        ins = act.activation(tiles_out(t), tiles_in(t), ACT.Identity, bias=nb.shift[:, t:t + 1],
                             scale=nb.rstd[:, t:t + 1])
    return ins


def normalised(dve, tiles_out, tiles_in, mean_var, rstd, tiles=range(TILES)):
    for t in tiles:
        ins = dve.tensor_scalar(tiles_out(t), tiles_in(t), mean_var[:, t, 0:1], rstd[:, t:t + 1],
                                ALU.subtract, ALU.mult)
    return ins


class Norms:

    def __init__(self, sb, sem, tag):
        self.stats = sb(f"{tag}_stats", [P, TILES, 6], F32)
        self.mean_var = sb(f"{tag}_mean_var", [P, TILES, 2], F32)
        self.var_eps = sb(f"{tag}_var_eps", [P, TILES], F32)
        self.rstd = sb(f"{tag}_rstd", [P, TILES], F32)
        self.neg_mean = sb(f"{tag}_neg_mean", [P, TILES], F32)
        self.shift = sb(f"{tag}_shift", [P, TILES], F32)
        self.pow_done = sem(f"{tag}_pow_done")
        self.branch = sb(f"{tag}_branch", [P, W], F32)
        self.y = sb(f"{tag}_y", [P, W], F32)
        self.var_ready = sem(f"{tag}_var_ready")
        self.rstd_ready = sem(f"{tag}_rstd_ready")
        self.y_ready = sem(f"{tag}_y_ready")
        self.y_transposed = sem(f"{tag}_y_transposed")
        self.yT_hi_ready = sem(f"{tag}_yT_hi_ready")
        self.yT_lo_ready = sem(f"{tag}_yT_lo_ready")

    def y_tile(self, t):
        return self.y[:, t * P:(t + 1) * P]


def build(nc, a, out):
    x_in, w_qkv, w_out = a["L0_attn_x"], a["L0_attn_w_qkv"], a["L0_attn_w_out"]
    B, N, D = x_in.shape
    NT = B * N // P
    NBLK = NT // TILES
    INNER = w_out.shape[0]
    HEADS = 16
    DH = INNER // HEADS
    assert D == P and N == 2 * P and NBLK % 2 == 0
    E0, HID = a["L0_ffn_rw"].shape[1], a["L0_ffn_sw1"].shape[1]
    E1, INTER = a["L1_ffn_We1"].shape[0], a["L1_ffn_We1"].shape[2]
    ITS = NBLK // 2

    with ExitStack() as ctx:
        def sb(name, shape, dt):
            return ctx.enter_context(nc.sbuf_tensor(name, shape, dt))

        def sem(name):
            return ctx.enter_context(nc.semaphore(name))

        x = sb("x", [P, NBLK + 2, W], F32)
        delta = sb("delta", [P, NBLK + 3, W], F32)
        outT = sb("outT", [P, W], F32)
        ident = sb("ident", [P, P], F32)
        minus_half = sb("minus_half", [P, TILES], F32)
        bank = [ctx.enter_context(nc.psum_tensor(f"bank{i}", [P, W], F32)) for i in range(8)]
        b_out = sb("b_out", [P, 1], F32)
        raw0 = [sb(f"raw0_{i}", [P, (E0 + 1) * HID], F32) for i in range(2)]
        raw0_down = sb("raw0_down", [P, (E0 + 1) * HID], F32)
        raw0_router = sb("raw0_router", [P, E0], F32)
        rb = sb("rb", [P, TILES * E0], F32)
        raw1 = [sb(f"raw1_{i}", [P, (E1 + 2) * INTER], F32) for i in range(2)]
        raw1_down = sb("raw1_down", [P, (E1 + 2) * INTER], F32)
        raw1_gate = sb("raw1_gate", [E1, P], F32)
        be1 = sb("be1", [P, E1 // 2 + 1], F32)
        be3 = sb("be3", [P, E1 // 2 + 1], F32)
        be2 = sb("be2", [P, P], F32)
        bs2 = sb("bs2", [P, 1], F32)
        gate_b = sb("gate_b", [P, TILES, E1], F32)
        raw_lin = sb("raw_lin", [P, 4, P], F32)
        gw = sb("gw", [P, 1], F32)
        sw = sb("sw", [P, 1], F32)
        x_loaded = sem("x_loaded")
        attn_w_loaded = sem("attn_w_loaded")
        later_w_loaded = sem("later_w_loaded")
        lw = dict(locals())
        attention(nc, a, lw)
        experts(nc, a, lw, 0)
        linear_attention(nc, a, lw)
        experts(nc, a, lw, 1)
        finish(nc, lw, out)


def attention(nc, a, g):
    x, delta, ident, bank = g["x"], g["delta"], g["ident"], g["bank"]
    minus_half, b_out = g["minus_half"], g["b_out"]
    B, N, NBLK, INNER, HEADS, DH, ITS = (g[k] for k in ("B", "N", "NBLK", "INNER", "HEADS", "DH", "ITS"))
    x_loaded, attn_w_loaded, later_w_loaded = g["x_loaded"], g["attn_w_loaded"], g["later_w_loaded"]
    E0, HID, E1, INTER = g["E0"], g["HID"], g["E1"], g["INTER"]
    PAIRS = HEADS // 2
    SCALE = float(DH) ** -0.5
    ctx = ExitStack()
    with ctx:
        def sb(name, shape, dt):
            return ctx.enter_context(nc.sbuf_tensor(name, shape, dt))

        def sem(name):
            return ctx.enter_context(nc.semaphore(name))

        A_w = [sb(f"A_{k}", [P, HEADS, P], F32R) for k in ("hi", "lo")]
        U_w = [sb(f"U_{k}", [P, HEADS, P], F32R) for k in ("hi", "lo")]

        nb = Norms(sb, sem, "l0a")
        y_tok = [[sb(f"y_tok_{k}{p}", [P, W], F32R) for k in ("hi", "lo")] for p in range(2)]
        yT = [[sb(f"yT_{k}{p}", [P, W], F32R) for k in ("hi", "lo")] for p in range(2)]
        z = [[sb(f"z_{k}{p}", [P, W], F32R) for k in ("hi", "lo")] for p in range(2)]
        probs = [sb(f"probs{p}", [P, W], F32) for p in range(2)]
        pT = [[sb(f"pT_{k}{p}", [P, W], F32R) for k in ("hi", "lo")] for p in range(2)]
        c = [[sb(f"c_{k}{p}", [P, W], F32R) for k in ("hi", "lo")] for p in range(2)]
        outT = g["outT"]
        neg_max = sb("neg_max", [P, 2, 2], F32)
        row_sum = sb("row_sum", [P, 2, 2], F32)
        inv_sum = sb("inv_sum", [P, 2, 2], F32)
        z_bank, s_bank, t_bank, c_bank, o_bank, m_bank = bank[0], bank[1:3], bank[3:5], bank[5], bank[6], bank[7]

        z_done, z_hi_done, z_lo_done = sem("z_done"), sem("z_hi_done"), sem("z_lo_done")
        s_done, max_done, exp_done = sem("s_done"), sem("max_done"), sem("exp_done")
        inv_done, probs_ready = sem("inv_done"), sem("probs_ready")
        t_done, t_hi_done, t_lo_done = sem("t_done"), sem("t_hi_done"), sem("t_lo_done")
        c_done, c_hi_done, c_lo_done = sem("c_done"), sem("c_hi_done"), sem("c_lo_done")
        o_done, outT_done, back_done, delta_done = sem("o_done"), sem("outT_done"), sem("back_done"), sem("delta_done")
        half_y_ready, y_lo_done, y_hi_done = sem("half_y_ready"), sem("y_lo_done"), sem("y_hi_done")
        dve_step, passed = sem("dve_step"), sem("passed")
        UN = 2 * HEADS
        U2, H2 = 2 * UN, 2 * HEADS
        LEAD = 3

        def xt(it, n):
            return lambda t: x[:, it * 2 + n, t * P:(t + 1) * P]

        later = []
        xr = a["L0_attn_x"].rearrange("b n d -> (b n) d").rearrange("(m t p) d -> m p t d", p=P, t=TILES)
        dve_chain = Chain(nc.vector, dve_step, passed, 2 * 8)

        def norm(it, n, part):
            dve, tile = nc.vector, xt(it, n)
            if part == 0:
                for t in (0, 1):
                    dve_chain.step(dve.bn_stats(nb.stats[:, t, :], tile(t)))
            if part == 1:
                dve_chain.step(dve.bn_stats(nb.stats[:, 2, :], tile(2)))
                dve_chain.link(dve.bn_stats(nb.stats[:, 3, :], tile(3)), apart=True)
            if part == 2:
                for t in range(TILES):
                    (dve_chain.link if t == TILES - 1 else dve_chain.step)(
                        dve.bn_aggr(nb.mean_var[:, t, :], nb.stats[:, t, :]))
                dve.tensor_scalar(nb.var_eps[:, :], nb.mean_var[:, :, 1], EPS, None, ALU.add)\
                    .then_inc(nb.var_ready, 1)
            if part == 3:
                dve.wait_ge(nb.rstd_ready, at(it, 2, n + 1))
                if n:
                    dve.wait_ge(nb.y_transposed, at(it, 2, n))
                    dve.wait_ge(y_lo_done, at(it, 2, n))
                normalised(dve, nb.y_tile, tile, nb.mean_var, nb.rstd, (0, 1)).then_inc(half_y_ready, 1)
            if part == 4:
                normalised(dve, nb.y_tile, tile, nb.mean_var, nb.rstd, (2, 3)).then_inc(nb.y_ready, 1)
            if part == 5:
                if n:
                    dve.wait_ge(c_done, at(it, U2, UN * (n - 1) + 2))
                dve.wait_ge(half_y_ready, at(it, 2, n + 1))
                dve.wait_ge(nb.y_ready, at(it, 2, n + 1))
                dve.tensor_copy(y_tok[n % 2][0][:, :], nb.y[:, :]).then_inc(y_hi_done, 1)

        def y_lo(it, n):
            nc.gpsimd.wait_ge(y_hi_done, at(it, 2, n + 1))
            nc.gpsimd.tensor_tensor(y_tok[n % 2][1][:, :], nb.y[:, :], as32(y_tok[n % 2][0][:, :]), ALU.subtract)\
                .then_inc(y_lo_done, 1)

        with ExitStack() as pctx:
            def psb(name, shape, dt):
                return pctx.enter_context(nc.sbuf_tensor(name, shape, dt))

            def psem(name):
                return pctx.enter_context(nc.semaphore(name))

            wqkv_sb = psb("wqkv_sb", [P, 3 * INNER], F32)
            wout_sb = psb("wout_sb", [P, PAIRS, P], F32)
            wT = psb("wT", [P, 3, PAIRS, P], F32)
            ident_ready = psem("ident_ready")
            w_transposed = psem("w_transposed")
            w_copied = psem("w_copied")
            folded = psem("folded")
            fold_hi = psem("fold_hi")
            fold_lo = psem("fold_lo")

            def head_of(j):
                return j // 8 * 8 + j // 4 % 2 + j % 4 * 2

            def bank_of(j, k):
                h = head_of(4 * j % HEADS)
                return (A_w if j < HEADS // 4 else U_w)[k][:, h:h + 7:2, :]
            with nc.Block() as block:
                @block.sync
                def _(sp):
                    sp.dma_start(x[:, 0, :].rearrange("p (t d) -> p t d", t=TILES), xr[0]).then_inc(x_loaded, 16)
                    sp.dma_start(wqkv_sb[:, :], a["L0_attn_w_qkv"]).then_inc(attn_w_loaded, 16)
                    sp.dma_start(wout_sb[:, :, :],
                                 a["L0_attn_w_out"].rearrange("(c p) n -> p c n", p=P)).then_inc(attn_w_loaded, 16)
                    with nc.allow_non_contiguous_dma(reason="a bias column"):
                        sp.dma_start(b_out[:, :], a["L0_attn_b_out"].rearrange("(p o) -> p o", o=1))\
                            .then_inc(attn_w_loaded, 16)

                @block.gpsimd
                def _(pool):
                    pool.memset(ident[:, :], 0.0).then_inc(ident_ready, 1)
                    pool.wait_ge(ident_ready, 1)
                    pool.affine_select(out=ident[:, :], in_=ident[:, :], compare_op=ALU.not_equal, fill=1.0,
                                       base=0, pattern=[[-1, P]], channel_multiplier=1).then_inc(ident_ready, 1)
                    pool.memset(g["be2"][:, :], 0.0).then_inc(ident_ready, 1)
                    pool.memset(minus_half[:, :], -0.5).then_inc(ident_ready, 1)
                    pool.memset(x[:, NBLK:, :], 0.0)
                    pool.memset(delta[:, NBLK + 1:, :], 0.0)
                    pool.memset(g["outT"][:, :], 0.0)
                    pool.wait_ge(ident_ready, 4)
                    inverse_std(pool, nb.var_eps, minus_half, nb.rstd, nb.var_ready, 1, nb.rstd_ready)
                    y_lo(0, 0)

                @block.tensor
                def _(pe):
                    pe.wait_ge(ident_ready, 2)
                    pe.wait_ge(attn_w_loaded, 48)
                    for j in range(3 * PAIRS):
                        ins = pe.transpose(bank[j // 4][:, j % 4 * P:(j % 4 + 1) * P], wqkv_sb[:, j * P:(j + 1) * P],
                                           ident[:, :])
                        if j % 4 == 3:
                            ins.then_inc(w_transposed, 1)
                    pe.wait_ge(w_copied, 3 * PAIRS // 4)
                    for j in range(2 * HEADS):
                        h = head_of(j % HEADS)
                        r = slice(DH * (h % 2), DH * (h % 2) + DH)
                        lhs, rhs = (wT[r, 0, h // 2, :], wT[r, 1, h // 2, :]) if j < HEADS else \
                            (wT[r, 2, h // 2, :], wout_sb[r, h // 2, :])
                        ins = pe.matmul(bank[j // 4][:, j % 4 * P:(j % 4 + 1) * P], lhs, rhs, start=True, stop=True)
                        if j % 4 == 3:
                            ins.then_inc(folded, 1)

                @block.scalar
                def _(act):
                    for j in range(3 * PAIRS // 4):
                        act.wait_ge(w_transposed, j + 1)
                        act.activation(wT[:, :, :, :].rearrange("p a c d -> p (a c d)")[:, j * W:(j + 1) * W],
                                       bank[j][:, :], ACT.Copy).then_inc(w_copied, 1)
                    for j in range(HEADS // 2):
                        act.wait_ge(folded, j + 1)
                        act.activation(bank_of(j, 0), bank[j][:, :].rearrange("p (h d) -> p h d", d=P), ACT.Copy,
                                       scale=SCALE if j < HEADS // 4 else 1.0).then_inc(fold_hi, 1)

                @block.vector
                def _(dve):
                    dve.wait_ge(x_loaded, 16)
                    for part in range(6):
                        norm(0, 0, part)
                    for j in range(HEADS // 2):
                        dve.wait_ge(fold_hi, j + 1)
                        dve.scalar_tensor_tensor(out=bank_of(j, 1), in0=bank[j][:, :].rearrange("p (h d) -> p h d", d=P),
                                                 scalar=SCALE if j < HEADS // 4 else 1.0, in1=as32(bank_of(j, 0)), op0=ALU.mult, op1=ALU.subtract).then_inc(fold_lo, 1)
        block = ctx.enter_context(nc.Block())

        @block.sync
        def _(sp):
            for m in range(1, NBLK):
                sp.dma_start(x[:, m, :].rearrange("p (t d) -> p t d", t=TILES), xr[m]).then_inc(x_loaded, 16)

            def column(v):
                return v.rearrange("(p o) -> p o", o=1)

            def load(dst, src):
                later.append(1)
                sp.dma_start(dst, src).then_inc(later_w_loaded, 16)
            with nc.allow_non_contiguous_dma(reason="bias columns"):
                load(g["bs2"][:, :], column(a["L1_ffn_bs2"]))
                load(g["be1"][:, 0:1], column(a["L1_ffn_bs1"]))
                load(g["be3"][:, 0:1], column(a["L1_ffn_bs3"]))
                load(g["be1"][:, 1:], a["L1_ffn_be1"].rearrange("(s h) i -> (h i) s", h=2))
                load(g["be3"][:, 1:], a["L1_ffn_be3"].rearrange("(s h) i -> (h i) s", h=2))
                for h in range(16):
                    load(g["gw"][8 * h:8 * h + 8, :], a["L1_attn_gw"].rearrange("o d -> d o"))
                    load(g["sw"][8 * h:8 * h + 8, :], a["L1_attn_sw"].rearrange("o d -> d o"))
            for i, n in enumerate(("1", "2")):
                load(g["raw0"][i][:, 0:HID], a[f"L0_ffn_sw{n}"])
                load(g["raw0"][i][:, HID:].rearrange("p (e h) -> p e h", e=E0),
                     a[f"L0_ffn_ew{n}"].rearrange("e d h -> d e h"))
            load(g["raw0_down"][:, 0:HID].rearrange("p (j n) -> p j n", n=P),
                 a["L0_ffn_sw3"].rearrange("(j p) n -> p j n", p=P))
            load(g["raw0_down"][:, HID:].rearrange("p (e n) -> p e n", n=P),
                 a["L0_ffn_ew3"].rearrange("e h n -> (e h) n").rearrange("(e p) n -> p e n", p=P))
            load(g["raw0_router"][:, :], a["L0_ffn_rw"])
            for i, n in enumerate(("1", "3")):
                load(g["raw1"][i][:, 0:P], a[f"L1_ffn_ws{n}"])
                load(g["raw1"][i][:, P:].rearrange("p (e h) -> p e h", e=E1),
                     a[f"L1_ffn_We{n}"].rearrange("e d h -> d e h"))
            load(g["raw1_down"][:, 0:P], a["L1_ffn_ws2"])
            load(g["raw1_down"][:, P:].rearrange("p (e n) -> p e n", n=P),
                 a["L1_ffn_We2"].rearrange("e h n -> (e h) n").rearrange("(e p) n -> p e n", p=P))
            load(g["raw1_gate"][:, :], a["L1_ffn_gate_w"])
            for row in (0, 32):
                load(g["be2"][row:row + E1, :], a["L1_ffn_be2"])
            for t in range(TILES):
                load(g["rb"][:, t * E0:(t + 1) * E0],
                     a["L0_ffn_rb"].rearrange("(o e) -> o e", o=1).to_broadcast([P, E0]))
                load(g["gate_b"][:, t, :],
                     a["L1_ffn_gate_b"].rearrange("(o e) -> o e", o=1).to_broadcast([P, E1]))
            for i, n in enumerate(("Wq", "Wk", "Wv", "Wo")):
                load(g["raw_lin"][:, i, :], a[f"L1_attn_{n}"])
            g["n_later"] = len(later)

        @block.tensor
        def _(pe):
            def transpose_y(it, n):
                pe.wait_ge(nb.y_ready, at(it, 2, n + 1))
                if n:
                    pe.wait_ge(delta_done, at(it, 2, n))
                for t in range(TILES):
                    ins = pe.transpose(m_bank[:, t * P:(t + 1) * P], nb.y_tile(t), ident[:, :])
                ins.then_inc(nb.y_transposed, 1)

            def project(it, h):
                if h % HEADS == 0:
                    pe.wait_ge(nb.yT_hi_ready, at(it, 2, h // HEADS + 1))
                    pe.wait_ge(nb.yT_lo_ready, at(it, 2, h // HEADS + 1))
                if h:
                    pe.wait_ge(z_hi_done, at(it, H2, h))
                    pe.wait_ge(z_lo_done, at(it, H2, h))
                y = [k[:, :] for k in yT[h // HEADS % 2]]
                product(pe, z_bank[:, :], [k[:, h % HEADS, :] for k in A_w], y).then_inc(z_done, 1)

            def scores(it, u):
                h, b = u // 2, u % 2
                if b == 0:
                    pe.wait_ge(z_hi_done, at(it, H2, h + 1))
                    pe.wait_ge(z_lo_done, at(it, H2, h + 1))
                if u >= 2:
                    pe.wait_ge(exp_done, at(it, U2, u - 1))
                keys = [k[:, b * N:(b + 1) * N] for k in yT[h // HEADS % 2]]
                for q in range(2):
                    ins = product(pe, s_bank[u % 2][:, q * N:(q + 1) * N],
                                  [k[:, b * N + q * P:b * N + (q + 1) * P] for k in z[h % 2]], keys)
                ins.then_inc(s_done, 1)

            def transpose_probs(it, u):
                pe.wait_ge(probs_ready, at(it, U2, u + 1))
                pe.wait_ge(t_hi_done, at(it, U2, u + 1))
                pe.wait_ge(t_lo_done, at(it, U2, u + 1))
                for q in range(2):
                    for k in range(2):
                        ins = pe.transpose(t_bank[u % 2][:, k * N + q * P:k * N + (q + 1) * P],
                                           probs[u % 2][:, q * N + k * P:q * N + (k + 1) * P], ident[:, :])
                ins.then_inc(t_done, 1)

            def mix(it, u):
                h, b = u // 2, u % 2
                pe.wait_ge(t_hi_done, at(it, U2, u + 3))
                pe.wait_ge(t_lo_done, at(it, U2, u + 3))
                if b == 0:
                    pe.wait_ge(c_hi_done, at(it, H2, h + 1))
                    pe.wait_ge(c_lo_done, at(it, H2, h + 1))
                for k in range(2):
                    s = slice((2 * b + k) * P, (2 * b + k + 1) * P)
                    ins = product(pe, c_bank[:, b * N:(b + 1) * N], [v[:, s] for v in y_tok[h // HEADS % 2]],
                                  [v[:, k * N:(k + 1) * N] for v in pT[u % 2]], start=(k == 0), stop=(k == 1))
                ins.then_inc(c_done, 1)

            def project_out(it, h):
                pe.wait_ge(c_hi_done, at(it, H2, h + 2))
                pe.wait_ge(c_lo_done, at(it, H2, h + 2))
                if h % HEADS == 0:
                    pe.wait_ge(outT_done, at(it, 2, h // HEADS + 1))
                product(pe, o_bank[:, :], [k[:, h % HEADS, :] for k in U_w], [k[:, :] for k in c[h % 2]],
                        start=(h % HEADS == 0), stop=(h % HEADS == HEADS - 1)).then_inc(o_done, 1)

            def slot(it, h):
                project(it, h + 3)
                if h >= -1:
                    mix(it, 2 * h + 2)
                if h >= 0:
                    project_out(it, h)
                if h >= -2:
                    transpose_probs(it, 2 * h + 4)
                scores(it, 2 * h + 6)
                if h >= -1:
                    mix(it, 2 * h + 3)
                scores(it, 2 * h + 7)
                if h >= -2:
                    transpose_probs(it, 2 * h + 5)

            def transpose_out(it, n):
                pe.wait_ge(outT_done, at(it, 2, n + 1))
                pe.wait_ge(nb.yT_lo_ready, at(it, 2, n + 1))
                for t in range(TILES):
                    ins = pe.transpose(m_bank[:, t * P:(t + 1) * P], outT[:, t * P:(t + 1) * P], ident[:, :])
                ins.then_inc(back_done, 1)

            transpose_y(0, 0)
            for h in range(-LEAD, 0):
                slot(0, h)
            with pe.Fori(0, ITS) as it:
                for p in range(2):
                    for j in range(HEADS):
                        slot(it, HEADS * p + j)
                        if j == 1:
                            transpose_out(it, p)
                        if j == 8:
                            transpose_y(it, p + 1)
            transpose_out(ITS, 0)

        @block.scalar
        def _(act):
            def yT_hi(it, n):
                act.wait_ge(nb.y_transposed, at(it, 2, n + 1))
                if n:
                    act.wait_ge(c_done, at(it, U2, UN * (n - 1) + 2))
                act.activation(yT[n % 2][0][:, :], m_bank[:, :], ACT.Copy).then_inc(nb.yT_hi_ready, 1)

            def z_hi(it, h):
                act.wait_ge(z_done, at(it, H2, h + 1))
                if h >= 2:
                    act.wait_ge(s_done, at(it, U2, 2 * h - 2))
                act.activation(z[h % 2][0][:, :], z_bank[:, :], ACT.Copy).then_inc(z_hi_done, 1)

            def exps(it, u):
                act.wait_ge(max_done, at(it, U2, u + 1))
                if u >= 2:
                    act.wait_ge(t_done, at(it, U2, u - 1))
                for q in range(2):
                    ins = act.activation(probs[u % 2][:, q * N:(q + 1) * N], s_bank[u % 2][:, q * N:(q + 1) * N],
                                         ACT.Exp, bias=neg_max[:, u % 2, q:q + 1],
                                         accum_out=row_sum[:, u % 2, q:q + 1])
                ins.then_inc(exp_done, 1)

            def pT_hi(it, u):
                act.wait_ge(t_done, at(it, U2, u + 1))
                act.wait_ge(c_done, at(it, U2, u + 1))
                act.activation(pT[u % 2][0][:, :], t_bank[u % 2][:, :], ACT.Copy).then_inc(t_hi_done, 1)

            def c_hi(it, h):
                act.wait_ge(c_done, at(it, U2, 2 * h + 4))
                act.wait_ge(o_done, at(it, H2, h + 1))
                act.activation(c[h % 2][0][:, :], c_bank[:, :], ACT.Copy).then_inc(c_hi_done, 1)

            act.sem_inc(t_hi_done, 2)
            act.sem_inc(c_hi_done, 1)
            act.sem_inc(outT_done, 1)
            def slot(it, h):
                z_hi(it, h + 3)
                if h >= -2:
                    exps(it, 2 * h + 5)
                    pT_hi(it, 2 * h + 4)
                if h >= -1:
                    c_hi(it, h + 1)
                exps(it, 2 * h + 6)
                if h >= -2:
                    pT_hi(it, 2 * h + 5)

            yT_hi(0, 0)
            for h in range(-LEAD, 0):
                slot(0, h)
            with act.Fori(0, ITS) as it:
                for p in range(2):
                    for j in range(HEADS):
                        slot(it, HEADS * p + j)
                        if j == 8:
                            yT_hi(it, p + 1)
                    act.wait_ge(o_done, at(it, H2, HEADS * (p + 1) + 2))
                    act.wait_ge(back_done, at(it, 2, p + 1))
                    act.activation(outT[:, :], o_bank[:, :], ACT.Identity, bias=b_out[:, 0:1]).then_inc(outT_done, 1)

        @block.gpsimd
        def _(pool):
            def norm_probs(it, u):
                wait_apart(pool, inv_done, at(it, U2, u + 1), passed)
                for q in range(2):
                    v = probs[u % 2][:, q * N:(q + 1) * N]
                    ins = pool.tensor_scalar(v, v, inv_sum[:, u % 2, q:q + 1], 1.0, ALU.mult, ALU.mult)
                ins.then_inc(probs_ready, 1)

            pool.sem_inc(c_done, 2)
            pool.sem_inc(o_done, 2)
            for u in range(2 * LEAD - 1):
                norm_probs(0, u)
            with pool.Fori(0, ITS) as it:
                for p in range(2):
                    for s in range(UN):
                        norm_probs(it, UN * p + s + 2 * LEAD - 1)
                        if s == 10:
                            inverse_std(pool, nb.var_eps, minus_half, nb.rstd, nb.var_ready, at(it, 2, p + 2),
                                        nb.rstd_ready)
                        if s == 18:
                            y_lo(it, p + 1)

        @block.vector
        def _(dve):
            ch = dve_chain

            def yT_lo(it, n):
                dve.wait_ge(nb.yT_hi_ready, at(it, 2, n + 1))
                dve.tensor_tensor(yT[n % 2][1][:, :], m_bank[:, :], as32(yT[n % 2][0][:, :]), ALU.subtract)\
                    .then_inc(nb.yT_lo_ready, 1)

            def z_lo(it, h):
                dve.wait_ge(z_hi_done, at(it, H2, h + 1))
                dve.tensor_tensor(z[h % 2][1][:, :], z_bank[:, :], as32(z[h % 2][0][:, :]), ALU.subtract)\
                    .then_inc(z_lo_done, 1)

            def maxima(it, u):
                dve.wait_ge(s_done, at(it, U2, u + 1))
                dve.tensor_reduce(neg_max[:, u % 2, :], s_bank[u % 2][:, :].rearrange("p (q k) -> p q k", q=2),
                                  AX, ALU.max, negate=True).then_inc(max_done, 1)

            def inverse_sums(it, u):
                dve.wait_ge(exp_done, at(it, U2, u + 1))
                dve.reciprocal(inv_sum[:, u % 2, :], row_sum[:, u % 2, :]).then_inc(inv_done, 1)

            def pT_lo(it, u):
                dve.wait_ge(t_hi_done, at(it, U2, u + 3))
                dve.tensor_tensor(pT[u % 2][1][:, :], t_bank[u % 2][:, :], as32(pT[u % 2][0][:, :]), ALU.subtract)\
                    .then_inc(t_lo_done, 1)

            def c_lo(it, h):
                dve.wait_ge(c_hi_done, at(it, H2, h + 2))
                dve.tensor_tensor(c[h % 2][1][:, :], c_bank[:, :], as32(c[h % 2][0][:, :]), ALU.subtract)\
                    .then_inc(c_lo_done, 1)

            dve.sem_inc(t_lo_done, 2)
            dve.sem_inc(c_lo_done, 1)
            yT_lo(0, 0)
            def slot(it, h):
                z_lo(it, h + 3)
                if h >= -1:
                    pT_lo(it, 2 * h + 3)
                if h >= -2:
                    inverse_sums(it, 2 * h + 5)
                maxima(it, 2 * h + 6)
                if h >= -2:
                    pT_lo(it, 2 * h + 4)
                if h >= -1:
                    c_lo(it, h + 1)
                inverse_sums(it, 2 * h + 6)
                maxima(it, 2 * h + 7)

            def store(it, n):
                wait_apart(dve, back_done, at(it, 2, n + 1), passed)
                dve.tensor_copy(delta[:, it * 2 + n, :], m_bank[:, :]).then_inc(delta_done, 1)

            for h in range(-LEAD, 0):
                slot(0, h)
            with dve.Fori(0, ITS) as it:
                ch.begin(it)
                for p in range(2):
                    for j in range(HEADS):
                        slot(it, HEADS * p + j)
                        if j == 1:
                            store(it, p)
                        if j == 2:
                            dve.wait_ge(x_loaded, 16 * NBLK)
                        if 2 <= j < 8:
                            norm(it, p + 1, j - 2)
                        if j == 9:
                            yT_lo(it, p + 1)
                ch.end()
            store(ITS, 0)


def split_weights(act, dve, pairs, hi_done, staged, first=0):
    for n, (raw, hi, lo) in enumerate(pairs):
        if act is not None:
            act.activation(hi, raw, ACT.Copy).then_inc(hi_done, 1)
        else:
            dve.wait_ge(hi_done, first + n + 1)
            dve.tensor_tensor(lo, raw, as32(hi), ALU.subtract).then_inc(staged, 1)


def experts(nc, a, g, layer):
    x, delta, ident, bank, minus_half = g["x"], g["delta"], g["ident"], g["bank"], g["minus_half"]
    NBLK, ITS = g["NBLK"], g["ITS"]
    E = g["E1"] if layer else g["E0"]
    LO = 32
    HALVES = 1 if layer else g["HID"] // P
    STEPS = E // 2 + 1 if layer else (E + 1) * HALVES
    SHARED = HALVES
    MAPS = (STEPS - SHARED) // HALVES
    raw = g["raw1"] if layer else g["raw0"]
    raw_down = g["raw1_down"] if layer else g["raw0_down"]
    be1, be3, be2, bs2, rb, gate_b = (g[k] for k in ("be1", "be3", "be2", "bs2", "rb", "gate_b"))
    tag = f"l{layer}e"
    NLATER = 16 * g["n_later"]
    ctx = ExitStack()
    with ctx:
        def sb(name, shape, dt):
            return ctx.enter_context(nc.sbuf_tensor(f"{tag}_{name}", shape, dt))

        def sem(name):
            return ctx.enter_context(nc.semaphore(f"{tag}_{name}"))

        up_w = [[sb(f"up{i}_{k}", [P, STEPS, P], F32R) for k in ("hi", "lo")] for i in range(2)]
        down_w = [sb(f"down_{k}", [P, STEPS, P], F32R) for k in ("hi", "lo")]
        router_w = [sb(f"router_{k}", [P, E], F32R) for k in ("hi", "lo")]
        be2_w = [sb(f"be2_{k}", [P, P], F32R) for k in ("hi", "lo")]
        pick32 = sb("pick32", [P, MAPS, P], F32)
        pick = sb("pick", [P, MAPS, P], F32R)
        gate = sb("gate", [P, TILES, P], F32)
        count = sb("count", [P, E], I32)
        place = sb("place", [P, TILES, E], F32)
        exp_base = sb("exp_base", [P, TILES], F32)
        gateT32 = sb("gateT32", [P, E], F32)
        if layer:
            before = sb("before", [P, TILES, 16], F32)
            after = sb("after", [P, TILES, 16], F32)

        nb = Norms(sb, sem, "n")
        branch_ready, x_added = sem("branch_ready"), sem("x_added")
        dve_step, passed = sem("dve_step"), sem("passed")
        dve, pool = nc.vector, nc.gpsimd
        ch = Chain(dve, dve_step, passed, 86 if layer else 58)

        def norm1(it, n):
            if n:
                dve.wait_ge(nb.y_ready, at(it, 2, n))
            row_stats(ch, lambda t: delta[:, it * 2 + n + 1, t * P:(t + 1) * P], nb, nb.var_ready)

        def branch(it, n):
            dve.wait_ge(nb.rstd_ready, at(it, 4, 2 * n + 1))
            normalised(dve, lambda t: nb.branch[:, t * P:(t + 1) * P],
                       lambda t: delta[:, it * 2 + n + 1, t * P:(t + 1) * P], nb.mean_var, nb.rstd)\
                .then_inc(branch_ready, 1)

        def make_y(it, n):
            dve.wait_ge(nb.rstd_ready, at(it, 4, 2 * n + 2))
            if n:
                dve.wait_ge(nb.y_transposed, at(it, 2, n))
            normalised(dve, nb.y_tile, lambda t: x[:, it * 2 + n, t * P:(t + 1) * P], nb.mean_var, nb.rstd)\
                .then_inc(nb.y_ready, 1)

        def norm2(it, n):
            wait_apart(dve, x_added, at(it, 2, n + 1), passed)
            row_stats(ch, lambda t: x[:, it * 2 + n, t * P:(t + 1) * P], nb, nb.var_ready)

        def rstd(it, n, second):
            inverse_std(pool, nb.var_eps, minus_half, nb.rstd, nb.var_ready, at(it, 4, 2 * n + 1 + second),
                        nb.rstd_ready)

        def add(it, n):
            pool.wait_ge(branch_ready, at(it, 2, n + 1))
            pool.tensor_tensor(x[:, it * 2 + n, :], x[:, it * 2 + n, :], nb.branch[:, :], ALU.add)\
                .then_inc(x_added, 1)

        pairs = [(gateT32[:, :] if layer else g["raw0_router"][:, :],) + tuple(k[:, :] for k in router_w)]
        if layer:
            pairs.append((be2[:, :],) + tuple(k[:, :] for k in be2_w))
        small = len(pairs)
        for r, w in ((raw[0], up_w[0]), (raw[1], up_w[1]), (raw_down, down_w)):
            for s0 in range(0, STEPS, 9):
                pairs.append((r[:, s0 * P:(s0 + 9) * P],) +
                             tuple(k[:, s0:s0 + 9, :].rearrange("p s n -> p (s n)") for k in w))
        third = STEPS // 9
        hi_done, lo_done = sem("hi_done"), sem("lo_done")

        with ExitStack() as pctx:
            made = pctx.enter_context(nc.semaphore(f"{tag}_made"))
            gate_transposed = pctx.enter_context(nc.semaphore(f"{tag}_gate_transposed"))
            gate_copied = pctx.enter_context(nc.semaphore(f"{tag}_gate_copied"))
            with nc.Block() as block:
                @block.gpsimd
                def _(pool):
                    pool.memset(pick32[:, :, :], 0.0).then_inc(made, 1)
                    pool.iota(count[:, :], pattern=[[1, E]], base=0, channel_multiplier=0).then_inc(made, 1)
                    pool.memset(exp_base[:, :], float(np.e))
                    pool.memset(gate[:, :, :], 0.0)
                    if layer:
                        v = pick32[:, :, :].rearrange("e m (h i) -> e m h i", h=2)
                        pattern = [[2, MAPS], [1, 2], [0, P // 2]]
                    else:
                        v, pattern = pick32[:, :, :], [[1, MAPS], [0, P]]
                    for n, row in enumerate((0, LO)):
                        pool.wait_ge(made, 2 + n)
                        pool.affine_select(out=v, in_=v, compare_op=ALU.not_equal, fill=1.0, base=row,
                                           pattern=pattern, channel_multiplier=-1).then_inc(made, 1)
                    if layer:
                        pool.memset(before[:, :, :], 0.0).then_inc(made, 1)
                        pool.memset(after[:, :, :], 0.0).then_inc(made, 1)
                        pool.wait_ge(made, 6)
                        for t, sign in ((before, 1), (after, -1)):
                            v = t[:, :, :].rearrange("p t (i j) -> p t i j", j=4)
                            pool.affine_select(out=v, in_=v, compare_op=ALU.is_ge, fill=1.0, base=0,
                                               pattern=[[0, TILES], [-sign, 4], [sign, 4]],
                                               channel_multiplier=0).then_inc(made, 1)
                    rstd(0, 0, 0)
                    add(0, 0)
                    rstd(0, 0, 1)

                @block.tensor
                def _(pe):
                    pe.wait_ge(later_loaded(g), NLATER)
                    if layer:
                        pe.transpose(bank[0][:, 0:E], g["raw1_gate"][:, :], ident[0:E, 0:E]).then_inc(gate_transposed, 1)

                @block.scalar
                def _(act):
                    act.wait_ge(later_loaded(g), NLATER)
                    if layer:
                        act.wait_ge(gate_transposed, 1)
                        act.activation(gateT32[:, :], bank[0][:, 0:E], ACT.Copy).then_inc(gate_copied, 1)
                        act.wait_ge(gate_copied, 1)
                    split_weights(act, None, pairs, hi_done, lo_done)

                @block.vector
                def _(dve):
                    dve.wait_ge(later_loaded(g), NLATER)
                    norm1(0, 0)
                    split_weights(None, dve, pairs[:small + third], hi_done, lo_done)
                    branch(0, 0)
                    split_weights(None, dve, pairs[small + third:small + 2 * third], hi_done, lo_done, small + third)
                    norm2(0, 0)
                    dve.wait_ge(made, 4)
                    dve.tensor_copy(pick[:, :, :], pick32[:, :, :])
                    for t in range(TILES):
                        dve.tensor_copy(place[:, t, :], count[:, :])
                    make_y(0, 0)

        yT = [[sb(f"yT_{k}{p}", [P, W], F32R) for k in ("hi", "lo")] for p in range(2)]
        silu = [sb(f"silu{p}", [P, W], F32) for p in range(2)]
        h = [sb(f"h{p}", [P, W], F32) for p in range(3)]
        h_w = [[sb(f"h_{k}{p}", [P, W], F32R) for k in ("hi", "lo")] for p in range(3)]
        outT = g["outT"]
        gT = [sb(f"gT{p}", [P, W], F32R) for p in range(2)]
        logit = sb("logit", [P, TILES, E], F32)
        probs = sb("probs", [P, TILES, E], F32)
        top = sb("top", [P, TILES, 8], F32)
        top_at = sb("top_at", [P, TILES, 8], U32)
        top_place = sb("top_place", [P, TILES, 2], F32)
        hit = [sb(f"hit{i}", [P, TILES, E], F32) for i in range(2)]
        one = [sb(f"one{i}", [P, TILES, 1], F32) for i in range(3)]
        quad = [sb(f"quad{i}", [P, TILES, 16], F32) for i in range(3)]
        eight = [sb(f"eight{i}", [P, TILES, 8], F32) for i in range(2)]
        four = [sb(f"four{i}", [P, TILES, 4], F32) for i in range(4)]
        a_bank, b_bank, o_bank, m_bank = bank[0:2], bank[2:4], bank[5], bank[6]
        gate_bank = (bank[4], bank[7])

        a_done, b_done, silu_done, prod_done = sem("a_done"), sem("b_done"), sem("silu_done"), sem("prod_done")
        map_done, h_done, h_hi_done, h_lo_done = sem("map_done"), sem("h_done"), sem("h_hi_done"), sem("h_lo_done")
        down_done, outT_done, back_done, delta_done = sem("down_done"), sem("outT_done"), sem("back_done"), sem("delta_done")
        logit_done = sem("logit_done")
        gate_ready, gT_done, gT_hi_ready, gT_lo_ready = sem("gate_ready"), sem("gT_done"), sem("gT_hi_ready"), sem("gT_lo_ready")
        diff_ready, exp_ready = sem("diff_ready"), sem("exp_ready")
        S2, M2 = 2 * STEPS, 2 * MAPS
        (T_STATS1, T_RSTD1, T_BRANCH, T_ADD, T_STATS2, T_RSTD2, T_Y, T_YT, T_ROUTE, T_GATE, T_EXP, T_GT, AHEAD) = \
            (2, 2, 3, 4, 6, 7, 8, 0, 1, 1, 2, 6, 2) if layer else (0, 2, 3, 3, 5, 5, 6, 7, 8, 9, 12, 15, 1)
        T_OUT = 3 if layer else 2
        PARTS = 5

        block = ctx.enter_context(nc.Block())

        def gated(k):
            return k % STEPS >= SHARED

        def map_of(k):
            return k // STEPS * MAPS + (k % STEPS - SHARED) // HALVES

        def last_of(m):
            return m // MAPS * STEPS + SHARED + (m % MAPS + 1) * HALVES - 1

        logit_read = diff_ready

        @block.tensor
        def _(pe):
            def transpose_y(it, n):
                pe.wait_ge(nb.y_ready, at(it, 2, n + 1))
                if n and T_YT < T_OUT:
                    pe.wait_ge(gT_lo_ready, at(it, 2, n))
                elif n:
                    pe.wait_ge(delta_done, at(it, 2, n))
                for t in range(TILES):
                    ins = pe.transpose(m_bank[:, t * P:(t + 1) * P], nb.y_tile(t), ident[:, :])
                ins.then_inc(nb.y_transposed, 1)

            def route(it, n):
                pe.wait_ge(nb.yT_hi_ready, at(it, 2, n + 1))
                pe.wait_ge(nb.yT_lo_ready, at(it, 2, n + 1))
                for t in range(TILES):
                    ins = product(pe, m_bank[:, t * E:(t + 1) * E], [k[:, t * P:(t + 1) * P] for k in yT[n % 2]],
                                  [k[:, :] for k in router_w])
                ins.then_inc(logit_done, 1)

            def gates_across(it, n):
                pe.wait_ge(gate_ready, at(it, 2, n + 1))
                if T_YT < T_OUT and n:
                    pe.wait_ge(delta_done, at(it, 2, n))
                for t in range(TILES):
                    ins = pe.transpose(m_bank[:, t * P:(t + 1) * P], gate[:, t, :], ident[:, :])
                ins.then_inc(gT_done, 1)

            def up(it, k):
                s = k % STEPS
                if s == 0:
                    pe.wait_ge(nb.yT_hi_ready, at(it, 2, k // STEPS + 1))
                    pe.wait_ge(nb.yT_lo_ready, at(it, 2, k // STEPS + 1))
                y = [v[:, :] for v in yT[k // STEPS % 2]]
                if k >= 2:
                    pe.wait_ge(silu_done, at(it, S2, k - 1))
                product(pe, a_bank[k % 2][:, :], [v[:, s, :] for v in up_w[0]], y).then_inc(a_done, 1)
                if k >= 2:
                    pe.wait_ge(prod_done, at(it, S2, k - 1))
                product(pe, b_bank[k % 2][:, :], [v[:, s, :] for v in up_w[1]], y).then_inc(b_done, 1)

            def gate_map(it, k):
                if not gated(k) or (k % STEPS - SHARED) % HALVES:
                    return
                n = k // STEPS
                pe.wait_ge(gT_hi_ready, at(it, 2, n + 1))
                pe.wait_ge(gT_lo_ready, at(it, 2, n + 1))
                if map_of(k) >= 2:
                    pe.wait_ge(h_done, at(it, S2, last_of(map_of(k) - 2) + 1))
                w = pick[:, (k % STEPS - SHARED) // HALVES, :]
                pe.matmul(gate_bank[map_of(k) % 2][:, :], w, gT[n % 2][:, :], start=True, stop=True).then_inc(map_done, 1)

            def down(it, k):
                s = k % STEPS
                pe.wait_ge(h_hi_done, at(it, S2, k + 1))
                pe.wait_ge(h_lo_done, at(it, S2, k + 1))
                if s == 0:
                    pe.wait_ge(outT_done, at(it, 2, k // STEPS + 1))
                product(pe, o_bank[:, :], [v[:, s, :] for v in down_w], [v[:, :] for v in h_w[k % 3]],
                        start=(s == 0), stop=(s == STEPS - 1)).then_inc(down_done, 1)
                if layer and s == 0:
                    for v in be2_w:
                        pe.matmul(o_bank[:, :], v[:, :], gT[k // STEPS % 2][:, :], start=False, stop=False)

            def transpose_out(it, n):
                pe.wait_ge(outT_done, at(it, 2, n + 1))
                if T_YT < T_OUT and it is not ITS:
                    pe.wait_ge(logit_read, at(it, 2, n + 2))
                else:
                    pe.wait_ge(gT_lo_ready, at(it, 2, n + 1))
                for t in range(TILES):
                    ins = pe.transpose(m_bank[:, t * P:(t + 1) * P], outT[:, t * P:(t + 1) * P], ident[:, :])
                ins.then_inc(back_done, 1)

            transpose_y(0, 0)
            route(0, 0)
            up(0, 0)
            up(0, 1)
            gates_across(0, 0)
            gate_map(0, 1)
            up(0, 2)
            pe.wait_ge(lo_done, len(pairs))
            with pe.Fori(0, ITS) as it:
                for p in range(2):
                    for s in range(STEPS):
                        k = STEPS * p + s
                        gate_map(it, k + 2)
                        up(it, k + 3)
                        down(it, k)
                        if s == T_OUT:
                            transpose_out(it, p)
                        if s == T_YT:
                            transpose_y(it, p + 1)
                        if s == T_ROUTE:
                            route(it, p + 1)
                        if s == T_GT:
                            gates_across(it, p + 1)
            transpose_out(ITS, 0)

        @block.scalar
        def _(act):
            def yT_hi(it, n):
                act.wait_ge(nb.y_transposed, at(it, 2, n + 1))
                if n:
                    act.wait_ge(down_done, at(it, S2, STEPS * (n - 1) + 1))
                act.activation(yT[n % 2][0][:, :], m_bank[:, :], ACT.Copy).then_inc(nb.yT_hi_ready, 1)

            def gT_hi(it, n):
                act.wait_ge(gT_done, at(it, 2, n + 1))
                if n:
                    act.wait_ge(down_done, at(it, S2, STEPS * (n - 1) + 1))
                act.activation(gT[n % 2][:, :], m_bank[:, :], ACT.Copy).then_inc(gT_hi_ready, 1)

            def exps(it, n):
                act.wait_ge(diff_ready, at(it, 2, n + 1))
                act.activation(probs[:, :, :], logit[:, :, :], ACT.Exp).then_inc(exp_ready, 1)

            def silus(it, k):
                act.wait_ge(a_done, at(it, S2, k + 1))
                if k >= 2:
                    act.wait_ge(prod_done, at(it, S2, k - 1))
                kw = dict(bias=be1[:, k % STEPS:k % STEPS + 1]) if layer else {}
                act.activation(silu[k % 2][:, :], a_bank[k % 2][:, :], ACT.Silu, **kw).then_inc(silu_done, 1)

            def h_hi(it, k):
                act.wait_ge(h_done, at(it, S2, k + 1))
                if k >= 3:
                    act.wait_ge(down_done, at(it, S2, k - 1))
                act.activation(h_w[k % 3][0][:, :], h[k % 3][:, :], ACT.Copy).then_inc(h_hi_done, 1)

            def store(it, n):
                act.wait_ge(back_done, at(it, 2, n + 1))
                act.activation(delta[:, it * 2 + n, :], m_bank[:, :], ACT.Copy).then_inc(delta_done, 1)

            act.sem_inc(down_done, 1)
            act.sem_inc(outT_done, 1)
            yT_hi(0, 0)
            if layer:
                exps(0, 0)
            silus(0, 0)
            silus(0, 1)
            h_hi(0, 0)
            gT_hi(0, 0)
            h_hi(0, 1)
            silus(0, 2)
            with act.Fori(0, ITS) as it:
                for p in range(2):
                    for s in range(STEPS):
                        k = STEPS * p + s
                        silus(it, k + 3)
                        h_hi(it, k + 2)
                        if s == T_OUT:
                            store(it, p)
                        if s == T_YT:
                            yT_hi(it, p + 1)
                        if s == T_EXP and layer:
                            exps(it, p + 1)
                        if s == T_GT:
                            gT_hi(it, p + 1)
                    act.wait_ge(down_done, at(it, S2, STEPS * (p + 1) + 1))
                    act.wait_ge(back_done, at(it, 2, p + 1))
                    if layer:
                        ins = act.activation(outT[:, :], o_bank[:, :], ACT.Identity, bias=bs2[:, 0:1])
                    else:
                        ins = act.activation(outT[:, :], o_bank[:, :], ACT.Copy)
                    ins.then_inc(outT_done, 1)
            store(ITS, 0)

        @block.gpsimd
        def _(pool):
            def h_lo(it, k):
                pool.wait_ge(h_hi_done, at(it, S2, k + 1))
                pool.tensor_tensor(h_w[k % 3][1][:, :], h[k % 3][:, :], as32(h_w[k % 3][0][:, :]), ALU.subtract)\
                    .then_inc(h_lo_done, 1)

            def powers(it, n):
                pool.wait_ge(diff_ready, at(it, 2, n + 1))
                pool.tensor_tensor(one[1][:, :, 0], exp_base[:, :], one[0][:, :, 0], ALU.pow).then_inc(exp_ready, 1)

            for n in range(1, AHEAD):
                rstd(0, n, 0)
                add(0, n)
                rstd(0, n, 1)
            if not layer:
                powers(0, 0)
            h_lo(0, 0)
            h_lo(0, 1)
            with pool.Fori(0, ITS) as it:
                for p in range(2):
                    for s in range(STEPS):
                        k = STEPS * p + s
                        h_lo(it, k + 2)
                        if s == T_RSTD1:
                            rstd(it, p + AHEAD, 0)
                        if s == T_ADD:
                            add(it, p + AHEAD)
                        if s == T_RSTD2:
                            rstd(it, p + AHEAD, 1)
                        if s == T_EXP and not layer:
                            powers(it, p + 1)

        @block.vector
        def _(dve):
            def yT_lo(it, n):
                dve.wait_ge(nb.yT_hi_ready, at(it, 2, n + 1))
                dve.tensor_tensor(yT[n % 2][1][:, :], m_bank[:, :], as32(yT[n % 2][0][:, :]), ALU.subtract)\
                    .then_inc(nb.yT_lo_ready, 1)

            def gT_lo(it, n):
                dve.wait_ge(gT_hi_ready, at(it, 2, n + 1))
                lo = gT[n % 2][LO:LO + E, :]
                dve.tensor_tensor(lo, m_bank[LO:LO + E, :], as32(lo), ALU.subtract)\
                    .then_inc(gT_lo_ready, 1)

            def top_two(values):
                for t in range(TILES - 1):
                    ch.step(dve.max(top[:, t, :], values[:, t, :]))
                ch.link(dve.max(top[:, TILES - 1, :], values[:, TILES - 1, :]), apart=True)
                for t in range(TILES):
                    ins = dve.max_index(top_at[:, t, :], top[:, t, :], values[:, t, :])
                ch.link(ins)
                ch.link(dve.tensor_copy(top_place[:, :, :], top_at[:, :, 0:2]))
                for i, count in enumerate((ch.step, ch.link)):
                    count(dve.tensor_tensor(hit[i][:, :, :], place[:, :, :],
                                            top_place[:, :, i:i + 1].to_broadcast([P, TILES, E]), ALU.is_equal))

            def routing0(it, n, part):
                if part == 0:
                    dve.wait_ge(logit_done, at(it, 2, n + 1))
                    if n:
                        dve.wait_ge(gT_done, at(it, 2, n))
                    ch.link(dve.tensor_tensor(logit[:, :, :], m_bank[:, 0:TILES * E].rearrange("p (t e) -> p t e", t=TILES),
                                              rb[:, :].rearrange("p (t e) -> p t e", t=TILES), ALU.add), apart=True)
                if part == 1:
                    top_two(logit)
                if part == 2:
                    dve.tensor_tensor(one[0][:, :, :], top[:, :, 1:2], top[:, :, 0:1], ALU.subtract)\
                        .then_inc(diff_ready, 1)
                if part == 4:
                    dve.wait_ge(exp_ready, at(it, 2, n + 1))
                    ch.link(dve.tensor_scalar(one[2][:, :, :], one[1][:, :, :], 1.0, None, ALU.add))
                    ch.link(dve.reciprocal(one[2][:, :, :], one[2][:, :, :]))
                    ch.link(dve.tensor_tensor(hit[1][:, :, :], hit[1][:, :, :],
                                              one[1][:, :, :].to_broadcast([P, TILES, E]), ALU.mult))
                    ch.link(dve.tensor_tensor(hit[0][:, :, :], hit[0][:, :, :], hit[1][:, :, :], ALU.add))
                    for row in (0, LO):
                        ins = dve.tensor_tensor(gate[:, :, row:row + E], hit[0][:, :, :],
                                                one[2][:, :, :].to_broadcast([P, TILES, E]), ALU.mult)
                    ins.then_inc(gate_ready, 1)

            def routing1(it, n, part):
                if part == 0:
                    dve.wait_ge(logit_done, at(it, 2, n + 1))
                    if n:
                        dve.wait_ge(gT_done, at(it, 2, n))
                    r = m_bank[:, 0:TILES * E].rearrange("p (t e) -> p t e", t=TILES)
                    ch.link(dve.tensor_reduce(one[0][:, :, 0], r, AX, ALU.max))
                    dve.tensor_tensor(logit[:, :, :], r, one[0][:, :, :].to_broadcast([P, TILES, E]), ALU.subtract)\
                        .then_inc(diff_ready, 1)
                if part == 1:
                    dve.wait_ge(exp_ready, at(it, 2, n + 1))
                    ch.link(dve.tensor_reduce(one[1][:, :, 0], probs[:, :, :], AX, ALU.add))
                    ch.link(dve.reciprocal(one[2][:, :, :], one[1][:, :, :]))
                    ch.link(dve.tensor_tensor(probs[:, :, :], probs[:, :, :], one[2][:, :, :].to_broadcast([P, TILES, E]),
                                              ALU.mult))
                    ch.link(dve.tensor_tensor(logit[:, :, :], probs[:, :, :], gate_b[:, :, :], ALU.add))
                    v = logit[:, :, :].rearrange("p t (g o) -> p t g o", o=2)
                    ch.step(dve.tensor_tensor(eight[0][:, :, :], v[:, :, :, 0], v[:, :, :, 1], ALU.max))
                    ch.link(dve.tensor_tensor(eight[1][:, :, :], v[:, :, :, 0], v[:, :, :, 1], ALU.add))
                    m, a = (v[:, :, :].rearrange("p t (g o) -> p t g o", o=2) for v in eight)
                    ch.step(dve.tensor_tensor(four[0][:, :, :], m[:, :, :, 0], m[:, :, :, 1], ALU.add))
                    ch.link(dve.tensor_tensor(four[1][:, :, :], a[:, :, :, 0], a[:, :, :, 1], ALU.max))
                    ch.link(dve.tensor_tensor(four[2][:, :, :], four[0][:, :, :], four[1][:, :, :], ALU.max))
                if part == 2:
                    q = [v[:, :, :].rearrange("p t (i j) -> p t i j", j=4) for v in quad]
                    own = four[2][:, :, :].rearrange("p t (i o) -> p t i o", o=1).to_broadcast([P, TILES, 4, 4])
                    other = four[2][:, :, :].rearrange("p t (o j) -> p t o j", o=1).to_broadcast([P, TILES, 4, 4])
                    ch.step(dve.tensor_tensor(q[1], other, own, ALU.is_ge))
                    ch.link(dve.tensor_tensor(q[2], other, own, ALU.is_gt))
                    ch.step(dve.tensor_tensor(quad[1][:, :, :], quad[1][:, :, :], before[:, :, :], ALU.mult))
                    ch.link(dve.tensor_tensor(quad[2][:, :, :], quad[2][:, :, :], after[:, :, :], ALU.mult))
                    ch.link(dve.tensor_tensor(quad[0][:, :, :], quad[1][:, :, :], quad[2][:, :, :], ALU.add))
                    ch.link(dve.tensor_reduce(four[3][:, :, :], q[0], AX, ALU.add))
                if part == 3:
                    ch.link(dve.tensor_scalar(four[3][:, :, :], four[3][:, :, :], 1.5, -1e30, ALU.is_gt, ALU.mult))
                    out4 = four[3][:, :, :].rearrange("p t (i o) -> p t i o", o=1).to_broadcast([P, TILES, 4, 4])
                    l4 = logit[:, :, :].rearrange("p t (i j) -> p t i j", j=4)
                    ch.link(dve.tensor_tensor(l4, l4, out4, ALU.add), apart=True)
                    top_two(logit)
                if part == 4:
                    ch.link(dve.tensor_tensor(hit[0][:, :, :], hit[0][:, :, :], hit[1][:, :, :], ALU.add))
                    for row in (0, LO):
                        ins = dve.tensor_tensor(gate[:, :, row:row + E], hit[0][:, :, :], probs[:, :, :], ALU.mult)
                    ins.then_inc(gate_ready, 1)

            routing = routing1 if layer else routing0

            def prod(it, k):
                dve.wait_ge(silu_done, at(it, S2, k + 1))
                dve.wait_ge(b_done, at(it, S2, k + 1))
                if k >= 3:
                    dve.wait_ge(h_lo_done, at(it, S2, k - 2))
                if layer:
                    ins = dve.scalar_tensor_tensor(out=h[k % 3][:, :], in0=b_bank[k % 2][:, :],
                                                   scalar=be3[:, k % STEPS:k % STEPS + 1], in1=silu[k % 2][:, :],
                                                   op0=ALU.add, op1=ALU.mult)
                else:
                    ins = dve.tensor_tensor(h[k % 3][:, :], b_bank[k % 2][:, :], silu[k % 2][:, :], ALU.mult)
                ins.then_inc(prod_done, 1)

            def weigh(it, k):
                dve.wait_ge(prod_done, at(it, S2, k + 1))
                if gated(k):
                    dve.wait_ge(map_done, at(it, M2, map_of(k) + 1))
                    dve.tensor_tensor(h[k % 3][:, :], gate_bank[map_of(k) % 2][:, :], h[k % 3][:, :], ALU.mult).then_inc(h_done, 1)
                else:
                    dve.sem_inc(h_done, 1)

            yT_lo(0, 0)
            split_weights(None, dve, pairs[small + 2 * third:], hi_done, lo_done, small + 2 * third)
            for n in range(1, AHEAD):
                norm1(0, n)
                branch(0, n)
                norm2(0, n)
                make_y(0, n)
            for part in range(PARTS):
                routing(0, 0, part)
            prod(0, 0)
            weigh(0, 0)
            prod(0, 1)
            gT_lo(0, 0)
            weigh(0, 1)
            prod(0, 2)
            with dve.Fori(0, ITS) as it:
                ch.begin(it)
                for p in range(2):
                    for s in range(STEPS):
                        k = STEPS * p + s
                        weigh(it, k + 2)
                        prod(it, k + 3)
                        if s == T_STATS1:
                            norm1(it, p + AHEAD)
                        if s == T_BRANCH:
                            branch(it, p + AHEAD)
                        if s == T_STATS2:
                            norm2(it, p + AHEAD)
                        if s == T_Y:
                            make_y(it, p + AHEAD)
                        if s == T_YT:
                            yT_lo(it, p + 1)
                        if T_GATE <= s < T_GATE + PARTS:
                            routing(it, p + 1, s - T_GATE)
                        if s == T_GT:
                            gT_lo(it, p + 1)
                ch.end()


def later_loaded(g):
    return g["later_w_loaded"]


def linear_attention(nc, a, g):
    x, delta, ident, bank, minus_half, raw = g["x"], g["delta"], g["ident"], g["bank"], g["minus_half"], g["raw_lin"]
    NBLK, ITS = g["NBLK"], g["ITS"]
    H, d = 16, 8
    KVN = H * d * d
    QKV = 3 * P
    PROJ = QKV + 2 * H
    NLATER = 16 * g["n_later"]
    ctx = ExitStack()
    with ctx:
        def sb(name, shape, dt):
            return ctx.enter_context(nc.sbuf_tensor(f"lin_{name}", shape, dt))

        def sem(name):
            return ctx.enter_context(nc.semaphore(f"lin_{name}"))

        proj32 = sb("proj32", [P, PROJ], F32)
        proj_w = [sb(f"proj_{k}", [P, PROJ], F32R) for k in ("hi", "lo")]
        woT = sb("woT", [P, P], F32)
        tri = sb("tri", [P, P], F32)
        ones = sb("ones", [P, P], F32)
        own = sb("own", [P, H], F32)
        sw_own = sb("sw_own", [P, H], F32)
        o = [sb(f"o{p}", [P, TILES, P], F32) for p in range(2)]
        made, copied, folded, gated, hi_done = (sem(n) for n in
                                                       ("made", "copied", "folded", "gated", "hi_done"))
        dve_step, passed = sem("dve_step"), sem("passed")
        nb = Norms(sb, sem, "n")
        branch_ready = sem("branch_ready")
        dve, pool, act = nc.vector, nc.gpsimd, nc.scalar
        ch = Chain(dve, dve_step, passed, 2 * 20)

        def norm1(it, n):
            row_stats(ch, lambda t: delta[:, it * 2 + n + 1, t * P:(t + 1) * P], nb, nb.var_ready, negate=True)

        def branch(it, n):
            act.wait_ge(nb.rstd_ready, at(it, 4, 2 * n + 1))
            scaled(act, lambda t: nb.branch[:, t * P:(t + 1) * P],
                   lambda t: delta[:, it * 2 + n + 1, t * P:(t + 1) * P], nb).then_inc(branch_ready, 1)

        def add(it, n):
            dve.wait_ge(branch_ready, at(it, 2, n + 1))
            ch.link(dve.tensor_tensor(x[:, it * 2 + n, :], x[:, it * 2 + n, :], nb.branch[:, :], ALU.add), apart=True)

        def norm2(it, n):
            row_stats(ch, lambda t: x[:, it * 2 + n, t * P:(t + 1) * P], nb, nb.var_ready, negate=True)

        def make_y(it, n):
            act.wait_ge(nb.rstd_ready, at(it, 4, 2 * n + 2))
            if n:
                act.wait_ge(nb.y_transposed, at(it, 2, n))
            scaled(act, nb.y_tile, lambda t: x[:, it * 2 + n, t * P:(t + 1) * P], nb).then_inc(nb.y_ready, 1)

        def rstd(it, n, second):
            scale_and_shift(pool, nb, minus_half, at(it, 4, 2 * n + 1 + second))

        with nc.Block() as block:
            @block.gpsimd
            def _(pool):
                pool.memset(tri[:, :], 1.0).then_inc(made, 1)
                pool.memset(own[:, :], 1.0).then_inc(made, 1)
                pool.memset(ones[:, :], 1.0)
                pool.memset(o[1][:, :, :], 0.0)
                pool.wait_ge(made, 2)
                pool.affine_select(out=tri[:, :], in_=tri[:, :], compare_op=ALU.is_ge, fill=0.0, base=0,
                                   pattern=[[1, P]], channel_multiplier=-1)
                pool.affine_select(out=own[:, :], in_=own[:, :], compare_op=ALU.is_ge, fill=0.0, base=0,
                                   pattern=[[-d, H]], channel_multiplier=1).then_inc(made, 1)
                pool.wait_ge(made, 3)
                pool.affine_select(out=own[:, :], in_=own[:, :], compare_op=ALU.is_ge, fill=0.0, base=d - 1,
                                   pattern=[[d, H]], channel_multiplier=-1).then_inc(made, 1)
                rstd(0, 0, 0)
                rstd(0, 0, 1)

            @block.tensor
            def _(pe):
                for i in range(4):
                    ins = pe.transpose(bank[0][:, i * P:(i + 1) * P], raw[:, i, :], ident[:, :])
                ins.then_inc(folded, 1)
                pe.wait_ge(gated, 2)
                pe.matmul(bank[1][:, 0:H], raw[:, 1, :], sw_own[:, :], start=True, stop=True).then_inc(folded, 1)

            @block.vector
            def _(dve):
                dve.wait_ge(made, 4)
                dve.tensor_scalar(sw_own[:, :], own[:, :], g["sw"][:, 0:1], None, ALU.mult).then_inc(gated, 1)
                dve.tensor_scalar(proj32[:, QKV + H:], own[:, :], g["gw"][:, 0:1], None, ALU.mult).then_inc(gated, 1)
                norm1(0, 0)
                add(0, 0)
                norm2(0, 0)
                dve.wait_ge(hi_done, 1)
                dve.tensor_tensor(proj_w[1][:, :], proj32[:, :], as32(proj_w[0][:, :]), ALU.subtract)

            @block.scalar
            def _(act):
                act.wait_ge(folded, 1)
                act.activation(proj32[:, 0:QKV], bank[0][:, 0:QKV], ACT.Copy).then_inc(copied, 1)
                act.activation(woT[:, :], bank[0][:, QKV:], ACT.Copy)
                act.wait_ge(folded, 2)
                act.activation(proj32[:, QKV:QKV + H], bank[1][:, 0:H], ACT.Copy).then_inc(copied, 1)
                act.wait_ge(copied, 2)
                act.wait_ge(gated, 2)
                act.activation(proj_w[0][:, :], proj32[:, :], ACT.Copy).then_inc(hi_done, 1)
                branch(0, 0)
                make_y(0, 0)

        yT = [sb(f"yT_{k}", [P, W], F32R) for k in ("hi", "lo")]
        qkvr = [sb(f"qkvr{p}", [P, TILES, QKV + H], F32) for p in range(2)]
        er = sb("er", [P, TILES, 2 * H], F32)
        g1 = sb("g1", [P, TILES, H], F32)
        lg = sb("lg", [P, TILES, H], F32)
        lc = sb("lc", [P, TILES, H], F32)
        gexp = sb("gexp", [P, TILES, H], F32)
        gc = [sb(f"gc{p}", [P, TILES, H], F32) for p in range(2)]
        den = sb("den", [P, TILES, H], F32)
        kw = [sb(f"kw{p}", [P, TILES, P], F32) for p in range(2)]
        qg = [sb(f"qg{p}", [P, TILES, P], F32) for p in range(2)]
        kv = sb("kv", [P, TILES, KVN], F32)
        qs = [sb(f"qs{p}", [P, KVN], F32) for p in range(2)]
        oT = sb("oT", [P, W], F32)
        p_bank, s_bank, m_bank, oT_bank, sum_bank = bank[0], [bank[1:3], bank[3:5]], bank[5], bank[6], bank[7]

        proj_done, proj_read, g1_ready, ln_done = sem("proj_done"), sem("proj_read"), sem("g1_ready"), sem("ln_done")
        sum_done, lc_ready, gexp_done, gc_ready = sem("sum_done"), sem("lc_ready"), sem("gexp_done"), sem("gc_ready")
        kw_ready, qg_ready, kv_ready, s_done = sem("kw_ready"), sem("qg_ready"), sem("kv_ready"), sem("s_done")
        qs_done, o_ready, oT_done, oT_ready = sem("qs_done"), sem("o_ready"), sem("oT_done"), sem("oT_ready")
        out_done, delta_done = sem("out_done"), sem("delta_done")
        T2 = 2 * TILES

        def heads(v):
            return v.rearrange("p t (h k) -> p t h k", k=d)

        def over(v):
            return v[:, :, :].rearrange("p t (h o) -> p t h o", o=1).to_broadcast([P, TILES, H, d])

        block = ctx.enter_context(nc.Block())

        @block.tensor
        def _(pe):
            def transpose_y(it, n):
                pe.wait_ge(nb.y_ready, at(it, 2, n + 1))
                if n:
                    pe.wait_ge(proj_read, at(it, T2, TILES * n))
                for t in range(TILES):
                    ins = pe.transpose(m_bank[:, t * P:(t + 1) * P], nb.y_tile(t), ident[:, :])
                ins.then_inc(nb.y_transposed, 1)

            def project(it, j):
                n, t = j // TILES, j % TILES
                if t == 0:
                    pe.wait_ge(nb.yT_hi_ready, at(it, 2, n + 1))
                    pe.wait_ge(nb.yT_lo_ready, at(it, 2, n + 1))
                    if n:
                        pe.wait_ge(delta_done, at(it, 2, n))
                if t >= 2:
                    pe.wait_ge(proj_read, at(it, T2, j - 1))
                product(pe, (p_bank, m_bank)[t % 2][:, 0:PROJ], [v[:, t * P:(t + 1) * P] for v in yT], [v[:, :] for v in proj_w])\
                    .then_inc(proj_done, 1)

            def cumulate(it, n):
                pe.wait_ge(ln_done, at(it, 2, n + 1))
                if n:
                    pe.wait_ge(lc_ready, at(it, 2, n))
                v = lg[:, :, :].rearrange("p t h -> p (t h)")
                first = lg[:, :, :].rearrange("p (b j) h -> p b j h", j=2)[:, :, 0, :]
                second = sum_bank[:, 0:TILES * H].rearrange("p (b j h) -> p b j h", j=2, h=H)[:, :, 1, :]
                pe.matmul(sum_bank[:, 0:TILES * H], tri[:, :], v, start=True, stop=False)
                pe.matmul(second, ones[:, :], first, start=False, stop=True).then_inc(sum_done, 1)

            def states(it, j):
                t = j % TILES
                pe.wait_ge(kv_ready, at(it, T2, j + 2))
                if t % 2 == 0:
                    pe.wait_ge(qs_done, at(it, T2, j + 1))
                for i in range(2):
                    ins = pe.matmul(s_bank[j % 2][i][:, :], tri[:, :], kv[:, t, i * W:(i + 1) * W],
                                    start=(t % 2 == 0), stop=True)
                ins.then_inc(s_done, 1)

            def carry(it, j):
                pe.wait_ge(qs_done, at(it, T2, j + 2))
                for i in range(2):
                    pe.matmul(s_bank[(j + 1) % 2][i][:, :], ones[:, :], kv[:, j % TILES, i * W:(i + 1) * W],
                              start=True, stop=False)

            def transpose_o(it, n):
                pe.wait_ge(o_ready, at(it, T2, TILES * n + 1))
                for t in range(TILES):
                    ins = pe.transpose(oT_bank[:, t * P:(t + 1) * P], o[(n + 1) % 2][:, t, :], ident[:, :])
                ins.then_inc(oT_done, 1)

            def project_out(it, n, projected):
                pe.wait_ge(oT_ready, at(it, 2, n + 1))
                pe.wait_ge(proj_read, at(it, T2, projected))
                for t in range(TILES):
                    ins = pe.matmul(p_bank[:, t * P:(t + 1) * P], oT[:, t * P:(t + 1) * P], woT[:, :],
                                    start=True, stop=True)
                ins.then_inc(out_done, 1)

            transpose_y(0, 0)
            for j in range(TILES):
                project(0, j)
            cumulate(0, 0)
            with pe.Fori(0, ITS) as it:
                for p in range(2):
                    states(it, TILES * p)
                    transpose_y(it, p + 1)
                    carry(it, TILES * p)
                    project(it, TILES * (p + 1))
                    project(it, TILES * (p + 1) + 1)
                    project(it, TILES * (p + 1) + 2)
                    project(it, TILES * (p + 1) + 3)
                    states(it, TILES * p + 1)
                    states(it, TILES * p + 2)
                    cumulate(it, p + 1)
                    carry(it, TILES * p + 2)
                    transpose_o(it, p)
                    states(it, TILES * p + 3)
                    project_out(it, p, TILES * (p + 2))
            transpose_o(ITS, 0)
            project_out(ITS, 0, TILES)

        @block.scalar
        def _(act):
            def yT_hi(it, n):
                act.wait_ge(nb.y_transposed, at(it, 2, n + 1))
                if n:
                    act.wait_ge(proj_done, at(it, T2, TILES * n))
                act.activation(yT[0][:, :], m_bank[:, :], ACT.Copy).then_inc(nb.yT_hi_ready, 1)

            def read_projection(it, j):
                n, t = j // TILES, j % TILES
                act.wait_ge(proj_done, at(it, T2, j + 1))
                if n:
                    act.wait_ge(kv_ready, at(it, T2, TILES * (n - 1) + 1))
                    act.wait_ge(kw_ready, at(it, 2, n))
                bank = (p_bank, m_bank)[t % 2]
                act.activation(qkvr[n % 2][:, t, :], bank[:, 0:QKV + H], ACT.Copy)
                act.activation(er[:, t, :], bank[:, QKV:PROJ], ACT.Exp, scale=-1.0).then_inc(proj_read, 1)

            def log_gate(it, n):
                act.wait_ge(g1_ready, at(it, 2, n + 1))
                if n:
                    act.wait_ge(sum_done, at(it, 2, n))
                act.activation(lg[:, :, :], g1[:, :, :], ACT.Ln).then_inc(ln_done, 1)

            def exp_gate(it, n):
                act.wait_ge(lc_ready, at(it, 2, n + 1))
                act.activation(gexp[:, :, :], lc[:, :, :], ACT.Exp, scale=-1.0).then_inc(gexp_done, 1)

            def output(it, n):
                act.wait_ge(oT_done, at(it, 2, n + 2))
                act.wait_ge(out_done, at(it, 2, n + 1))
                act.activation(oT[:, :], oT_bank[:, :], ACT.Copy).then_inc(oT_ready, 1)
                act.wait_ge(out_done, at(it, 2, n + 2))
                act.activation(delta[:, it * 2 + n, :], p_bank[:, :], ACT.Copy).then_inc(delta_done, 1)

            act.preload_act_table_set("natural_log_exp_and_others")
            act.sem_inc(oT_done, 1)
            act.sem_inc(delta_done, 1)
            yT_hi(0, 0)
            for j in range(TILES):
                read_projection(0, j)
            log_gate(0, 0)
            exp_gate(0, 0)
            branch(0, 1)
            make_y(0, 1)
            with act.Fori(0, ITS) as it:
                for p in range(2):
                    yT_hi(it, p + 1)
                    for j in range(TILES):
                        read_projection(it, TILES * (p + 1) + j)
                    branch(it, p + 2)
                    log_gate(it, p + 1)
                    exp_gate(it, p + 1)
                    output(it, p)
                    make_y(it, p + 2)
            output(ITS, 0)

        @block.gpsimd
        def _(pool):
            def outer(it, j):
                n, t = j // TILES, j % TILES
                pool.wait_ge(kw_ready, at(it, 2, n + 1))
                pool.wait_ge(s_done, at(it, T2, j + (1 if t % 2 else 2)))
                out = kv[:, t, :].rearrange("p (h k e) -> p h k e", k=d, e=d)
                k = kw[n % 2][:, t, :].rearrange("p (h k o) -> p h k o", k=d, o=1).to_broadcast([P, H, d, d])
                v = qkvr[n % 2][:, t, 2 * P:QKV].rearrange("p (h o e) -> p h o e", e=d, o=1)\
                    .to_broadcast([P, H, d, d])
                pool.tensor_tensor(out, k, v, ALU.mult).then_inc(kv_ready, 1)

            def weigh_q(it, n):
                pool.wait_ge(gc_ready, at(it, 2, n + 1))
                pool.wait_ge(o_ready, at(it, T2, TILES * (n - 1) + 1)) if n else None
                pool.tensor_tensor(heads(qg[n % 2][:, :, :]), heads(qkvr[n % 2][:, :, 0:P]), over(gc[n % 2]),
                                   ALU.mult).then_inc(qg_ready, 1)

            pool.sem_inc(s_done, 4)
            pool.sem_inc(out_done, 1)
            pool.sem_inc(kv_ready, 1)
            weigh_q(0, 0)
            outer(0, 0)
            rstd(0, 1, 0)
            rstd(0, 1, 1)
            with pool.Fori(0, ITS) as it:
                for p in range(2):
                    outer(it, TILES * p + 1)
                    outer(it, TILES * p + 2)
                    rstd(it, p + 2, 0)
                    outer(it, TILES * p + 3)
                    rstd(it, p + 2, 1)
                    weigh_q(it, p + 1)
                    outer(it, TILES * (p + 1))

        @block.vector
        def _(dve):
            def yT_lo(it, n):
                dve.wait_ge(nb.yT_hi_ready, at(it, 2, n + 1))
                dve.tensor_tensor(yT[1][:, :], m_bank[:, :], as32(yT[0][:, :]), ALU.subtract)\
                    .then_inc(nb.yT_lo_ready, 1)

            def gate_cost(it, n):
                dve.wait_ge(proj_read, at(it, T2, TILES * (n + 1)))
                dve.tensor_scalar(g1[:, :, :], er[:, :, H:], 1.0, 1e6, ALU.add, ALU.min).then_inc(g1_ready, 1)

            def gate_sum(it, n):
                dve.wait_ge(sum_done, at(it, 2, n + 1))
                dve.tensor_scalar(lc[:, :, :].rearrange("p t h -> p (t h)"), sum_bank[:, 0:TILES * H], 30.0, -30.0,
                                  ALU.min, ALU.max).then_inc(lc_ready, 1)

            def weights(it, n):
                dve.wait_ge(gexp_done, at(it, 2, n + 1))
                dve.tensor_scalar(gc[n % 2][:, :, :], gexp[:, :, :], 1e-6, None, ALU.add).then_inc(gc_ready, 1)
                dve.wait_ge(gc_ready, at(it, 2, n + 1))
                ch.link(dve.scalar_tensor_tensor(out=den[:, :, :], in0=er[:, :, 0:H], scalar=1.0,
                                                 in1=gc[n % 2][:, :, :], op0=ALU.add, op1=ALU.mult))
                ch.link(dve.reciprocal(den[:, :, :], den[:, :, :]))
                ch.link(dve.tensor_tensor(den[:, :, :], den[:, :, :], qkvr[n % 2][:, :, QKV:], ALU.mult))
                dve.tensor_tensor(heads(kw[n % 2][:, :, :]), heads(qkvr[n % 2][:, :, P:2 * P]), over(den),
                                  ALU.mult).then_inc(kw_ready, 1)

            def multiply(it, j):
                n, t = j // TILES, j % TILES
                dve.wait_ge(s_done, at(it, T2, j + 5))
                if t == 0:
                    dve.wait_ge(qg_ready, at(it, 2, n + 1))
                for i in range(2):
                    s = s_bank[j % 2][i][:, :].rearrange("p (h k e) -> p h e k", k=d, e=d)
                    q = qg[n % 2][:, t, i * P // 2:(i + 1) * P // 2].rearrange("p (h o k) -> p h o k", k=d, o=1)\
                        .to_broadcast([P, H // 2, d, d])
                    ins = dve.tensor_tensor(qs[j % 2][:, i * W:(i + 1) * W].rearrange("p (h e k) -> p h e k", k=d, e=d),
                                            s, q, ALU.mult)
                ins.then_inc(qs_done, 1)

            def add_up(it, j):
                n, t = j // TILES, j % TILES
                dve.wait_ge(qs_done, at(it, T2, j + 3))
                dve.wait_ge(oT_done, at(it, 2, n + 1))
                dve.tensor_reduce(o[n % 2][:, t, :], qs[j % 2][:, :].rearrange("p (c k) -> p c k", k=d), AX, ALU.add)\
                    .then_inc(o_ready, 1)

            dve.sem_inc(qs_done, 2)
            dve.sem_inc(o_ready, 1)
            yT_lo(0, 0)
            gate_cost(0, 0)
            gate_sum(0, 0)
            weights(0, 0)
            norm1(0, 1)
            add(0, 1)
            norm2(0, 1)
            with dve.Fori(0, ITS) as it:
                ch.begin(it)
                for p in range(2):
                    multiply(it, TILES * p)
                    yT_lo(it, p + 1)
                    norm1(it, p + 2)
                    add_up(it, TILES * p)
                    multiply(it, TILES * p + 1)
                    gate_cost(it, p + 1)
                    add(it, p + 2)
                    add_up(it, TILES * p + 1)
                    multiply(it, TILES * p + 2)
                    gate_sum(it, p + 1)
                    norm2(it, p + 2)
                    weights(it, p + 1)
                    add_up(it, TILES * p + 2)
                    multiply(it, TILES * p + 3)
                    add_up(it, TILES * p + 3)
                ch.end()


class BlockNorm:

    def __init__(self, sb, m, var_ready, pow_done, rstd_ready):
        self.stats = sb(f"stats{m}", [P, TILES, 6], F32)
        self.mean_var = sb(f"mean_var{m}", [P, TILES, 2], F32)
        self.var_eps = sb(f"var_eps{m}", [P, TILES], F32)
        self.rstd = sb(f"rstd{m}", [P, TILES], F32)
        self.neg_mean = sb(f"neg_mean{m}", [P, TILES], F32)
        self.shift = sb(f"shift{m}", [P, TILES], F32)
        self.branch = sb(f"branch{m}", [P, W], F32)
        self.var_ready, self.pow_done, self.rstd_ready = var_ready, pow_done, rstd_ready


def finish(nc, g, out):
    x, delta, minus_half = g["x"], g["delta"], g["minus_half"]
    NBLK = g["NBLK"]
    with ExitStack() as ctx:
        def sb(name, shape, dt):
            return ctx.enter_context(nc.sbuf_tensor(f"fin_{name}", shape, dt))

        def sem(name):
            return ctx.enter_context(nc.semaphore(f"fin_{name}"))

        var_ready, pow_done, rstd_ready = sem("var_ready"), sem("pow_done"), sem("rstd_ready")
        branch_ready, odd_added, even_added = sem("branch_ready"), sem("odd_added"), sem("even_added")
        out_stored, dve_step, passed = sem("out_stored"), sem("dve_step"), sem("passed")
        norms = [BlockNorm(sb, m, var_ready, pow_done, rstd_ready) for m in range(NBLK)]
        LAG = 3
        o = out.rearrange("b n d -> (b n) d").rearrange("(m t p) d -> m p t d", p=P, t=TILES)

        def add(eng, m, added):
            eng.wait_ge(branch_ready, m + 1)
            eng.tensor_tensor(x[:, m, :], x[:, m, :], norms[m].branch[:, :], ALU.add).then_inc(added, 1)

        with nc.Block() as block:
            @block.vector
            def _(dve):
                ch = Chain(dve, dve_step, passed, 0)
                for m in range(NBLK + LAG):
                    if m < NBLK:
                        row_stats(ch, lambda t: delta[:, m + 1, t * P:(t + 1) * P], norms[m], var_ready, negate=True)
                    if m >= LAG and (m - LAG) % 2:
                        add(dve, m - LAG, odd_added)

            @block.gpsimd
            def _(pool):
                for m in range(NBLK + LAG):
                    if m < NBLK:
                        scale_and_shift(pool, norms[m], minus_half, m + 1)
                    if m >= LAG and (m - LAG) % 2 == 0:
                        add(pool, m - LAG, even_added)

            @block.scalar
            def _(act):
                for m in range(NBLK):
                    act.wait_ge(rstd_ready, m + 1)
                    scaled(act, lambda t: norms[m].branch[:, t * P:(t + 1) * P],
                           lambda t: delta[:, m + 1, t * P:(t + 1) * P], norms[m]).then_inc(branch_ready, 1)

            @block.sync
            def _(sp):
                for m in range(NBLK):
                    sp.wait_ge(odd_added if m % 2 else even_added, m // 2 + 1)
                    sp.dma_start(o[m], x[:, m, :].rearrange("p (t d) -> p t d", t=TILES)).then_inc(out_stored, 16)
                sp.wait_ge(out_stored, 16 * NBLK)


_INS = ["L0_attn_x", "L0_attn_w_qkv", "L0_attn_w_out", "L0_attn_b_out", "L0_ffn_sw1", "L0_ffn_sw2", "L0_ffn_sw3",
        "L0_ffn_ew1", "L0_ffn_ew2", "L0_ffn_ew3", "L0_ffn_rw", "L0_ffn_rb", "L1_attn_Wq", "L1_attn_Wk",
        "L1_attn_Wv", "L1_attn_Wo", "L1_attn_gw", "L1_attn_sw", "L1_ffn_gate_w", "L1_ffn_gate_b", "L1_ffn_We1",
        "L1_ffn_be1", "L1_ffn_We2", "L1_ffn_be2", "L1_ffn_We3", "L1_ffn_be3", "L1_ffn_ws1", "L1_ffn_bs1",
        "L1_ffn_ws2", "L1_ffn_bs2", "L1_ffn_ws3", "L1_ffn_bs3"]


def kernel(**inputs):
    import numpy as _np
    import concourse.bacc as _bacc
    from concourse import mybir as _mybir
    from concourse.bass_utils import run_bass_kernel_spmd as _run

    nc = _bacc.Bacc("TRN2", target_bir_lowering=False, num_devices=1)
    arrays, args = {}, {}
    for name in _INS:
        arr = _np.ascontiguousarray(inputs[name])
        arrays[f"in_{name}_dram"] = arr
        args[name] = nc.dram_tensor(f"in_{name}_dram", arr.shape, _mybir.dt.from_np(arr.dtype),
                                    kind="ExternalInput").ap()
    shape = inputs["L0_attn_x"].shape
    out = nc.dram_tensor("out_0_dram", shape, _mybir.dt.float32, kind="ExternalOutput").ap()
    build(nc, args, out)
    r = _run(nc, [arrays], core_ids=[0])
    return r.results[0]["out_0_dram"]
```
